# Optimizing a Trainium2 kernel written in Bass

```python
import numpy as np
import jax
import jax.numpy as jnp

def _softmax(x, axis=-1):
    return jax.nn.softmax(x, axis=axis)

def _gelu(x):
    return jax.nn.gelu(x, approximate=True)

def _silu(x):
    return jax.nn.silu(x)

def _sigmoid(x):
    return jax.nn.sigmoid(x)

def _layernorm(x, axis=-1, eps=1e-05):
    m = jnp.mean(x, axis=axis, keepdims=True)
    v = jnp.var(x, axis=axis, keepdims=True)
    return (x - m) / jnp.sqrt(v + eps)

def _scatter_add(tgt, idx, src, axis=0):
    return tgt.at[idx].add(src)

def _segment_sum(src, seg, n):
    return jax.ops.segment_sum(src, seg, n)
kernel_name = 'mk_gnn_resnorm_d4_gnn_r8_e02cb1'

def setup_inputs(seed: int=0):
    np.random.seed(seed)
    _w = jnp.asarray

    def _rec_inputs():
        import jax
        import jax.numpy as jnp
        _gk = jax.random.key(seed)
        x = -0.000202 + 1 * jax.random.normal(jax.random.fold_in(_gk, 1), (6250, 128), jnp.float32)
        _s = jax.random.randint(jax.random.fold_in(_gk, 2), (100000,), 0, 6250, jnp.int32)
        _d = jax.random.randint(jax.random.fold_in(_gk, 3), (100000,), 0, 6250, jnp.int32)
        _loop = jnp.arange(6250, dtype=jnp.int32)
        src = jnp.concatenate([_s, _d, _loop])
        dst = jnp.concatenate([_d, _s, _loop])
        _o = jnp.argsort(dst, stable=True)
        src = src[_o]
        dst = dst[_o]
        edge_attr_10 = jax.random.uniform(jax.random.fold_in(_gk, 12), (206250, 10), jnp.float32, 0.0, 1)
        edge_attr_32 = 0.000189758 + 1.00013 * jax.random.normal(jax.random.fold_in(_gk, 13), (206250, 32), jnp.float32)
        edge_attr_4 = 0.00121237 + 1.00026 * jax.random.normal(jax.random.fold_in(_gk, 14), (206250, 4), jnp.float32)
        edge_attr_64 = -8.16379e-05 + 0.999858 * jax.random.normal(jax.random.fold_in(_gk, 15), (206250, 64), jnp.float32)
        edge_weight = jax.random.uniform(jax.random.fold_in(_gk, 17), (206250,), jnp.float32, 0.0, 1)
        node_vec1 = jax.random.uniform(jax.random.fold_in(_gk, 18), (6250, 1), jnp.float32, 0.0, 1)
        return (x, src, dst, edge_attr_10, edge_attr_32, edge_attr_4, edge_attr_64, edge_weight, node_vec1)
    x, src, dst, edge_attr_10, edge_attr_32, edge_attr_4, edge_attr_64, edge_weight, node_vec1 = _rec_inputs()

    def _L0_gnn_setup():
        import jax, jax.numpy as jnp
        import numpy as np
        N = 6250
        E = 100000
        IN_F = 128
        OUT_F = 128
        NEG_SLOPE = 0.2
        EPS = 1e-10
        key = jax.random.key(seed)
        k1, k2, k3, k4 = jax.random.split(key, 4)
        h = jax.random.normal(k1, (N, IN_F), dtype=jnp.float32)
        edge_index = jax.random.randint(k2, (2, E), 0, N, dtype=jnp.int32)
        W = jax.random.normal(k3, (OUT_F, IN_F), dtype=jnp.float32) * (1.0 / np.sqrt(IN_F))
        lim = 1.414 * np.sqrt(6.0 / (2 * OUT_F + 1))
        a = jax.random.uniform(k4, (2 * OUT_F, 1), dtype=jnp.float32, minval=-lim, maxval=lim)
        return {'h': h, 'edge_index': edge_index, 'W': W, 'a': a}
    _L0_gnn_all = _L0_gnn_setup()
    _L0_gnn_in = {k: v for k, v in _L0_gnn_all.items() if k in ('W', 'a')}
    del _L0_gnn_all

    def _L1_gnn_setup():
        import jax, jax.numpy as jnp
        import numpy as np
        N_NODES = 6250
        N_EDGES = 100000
        D = 128
        LN_EPS = 1e-05
        key = jax.random.key(seed)
        ks = jax.random.split(key, 6)
        x = jax.random.normal(ks[0], (N_NODES, D), dtype=jnp.float32)
        edge_index = jax.random.randint(ks[1], (2, N_EDGES), 0, N_NODES, dtype=jnp.int32)
        agg_W = jax.random.normal(ks[2], (D, D), dtype=jnp.float32) / np.sqrt(D)
        agg_b = jnp.zeros((D,), dtype=jnp.float32)
        W = jax.random.normal(ks[3], (2 * D, D), dtype=jnp.float32) / np.sqrt(2 * D)
        b = jnp.zeros((D,), dtype=jnp.float32)
        gamma = jnp.ones((D,), dtype=jnp.float32)
        beta = jnp.zeros((D,), dtype=jnp.float32)
        return {'x': x, 'edge_index': edge_index, 'agg_W': agg_W, 'agg_b': agg_b, 'W': W, 'b': b, 'gamma': gamma, 'beta': beta}
    _L1_gnn_all = _L1_gnn_setup()
    _L1_gnn_in = {k: v for k, v in _L1_gnn_all.items() if k in ('agg_W', 'agg_b', 'W', 'b', 'gamma', 'beta')}
    del _L1_gnn_all

    def _L2_gnn_setup():
        import jax, jax.numpy as jnp
        import numpy as np
        N, E, MUL = (6250, 50000, 32)
        SQ3 = float(np.sqrt(3.0))
        key = jax.random.key(seed)
        ks = jax.random.split(key, 16)
        rn = lambda k, s: jax.random.normal(k, s, dtype=jnp.float32)
        return {'x': rn(ks[0], (N, 4 * MUL)), 'node_attr': jnp.ones((N, 1), jnp.float32), 'edge_src': jax.random.randint(ks[1], (E,), 0, N), 'edge_dst': jax.random.randint(ks[2], (E,), 0, N), 'edge_sh': rn(ks[3], (E, 4)), 'edge_scalars': jax.random.uniform(ks[4], (E, 10), dtype=jnp.float32), 'W_fc1': rn(ks[5], (10, 100)), 'W_fc2': rn(ks[6], (100, 4 * MUL)), 'W_sc0': rn(ks[7], (MUL, MUL)), 'W_sc1': rn(ks[8], (MUL, MUL)), 'W_l1_0': rn(ks[9], (MUL, MUL)), 'W_l1_1': rn(ks[10], (MUL, MUL)), 'W_l2_0': rn(ks[11], (2 * MUL, MUL)), 'W_l2_1': rn(ks[12], (2 * MUL, MUL)), 'W_alpha': rn(ks[13], (2 * MUL, 1))}
    _L2_gnn_all = _L2_gnn_setup()
    _L2_gnn_in = {k: v for k, v in _L2_gnn_all.items() if k in ('W_fc1', 'W_fc2', 'W_sc0', 'W_sc1', 'W_l1_0', 'W_l1_1', 'W_l2_0', 'W_l2_1', 'W_alpha')}
    del _L2_gnn_all

    def _L3_gnn_setup():
        import jax, jax.numpy as jnp
        import numpy as np
        N_NODES = 12500
        N_EDGES = 200000
        D = 128
        H = 8
        HD = D // H
        RAD_IN, SPH_IN, HID = (64, 32, 256)
        AVG_NUM_NEIGHBORS = 16.0

        def _mlp(x, w0, b0, w1, b1):
            return jax.nn.silu(x @ w0 + b0) @ w1 + b1
        key = jax.random.key(seed)
        ks = jax.random.split(key, 16)

        def glorot(k, shape):
            fan_in, fan_out = (shape[0], shape[1])
            s = jnp.sqrt(2.0 / (fan_in + fan_out))
            return jax.random.normal(k, shape, dtype=jnp.float32) * s
        return {'node_feats': jax.random.normal(ks[0], (N_NODES, D), dtype=jnp.float32), 'edge_feats': jax.random.normal(ks[1], (N_EDGES, RAD_IN), dtype=jnp.float32), 'chi_scalar': jax.random.normal(ks[2], (N_EDGES, SPH_IN), dtype=jnp.float32), 'cutoffs': jax.random.uniform(ks[3], (N_EDGES,), dtype=jnp.float32), 'senders': jax.random.randint(ks[4], (N_EDGES,), 0, N_NODES, dtype=jnp.int32), 'receivers': jax.random.randint(ks[5], (N_EDGES,), 0, N_NODES, dtype=jnp.int32), 'rad_w0': glorot(ks[6], (RAD_IN, HID)), 'rad_b0': jnp.zeros((HID,), jnp.float32), 'rad_w1': glorot(ks[7], (HID, D)), 'rad_b1': jnp.zeros((D,), jnp.float32), 'sph_w0': glorot(ks[8], (SPH_IN, HID)), 'sph_b0': jnp.zeros((HID,), jnp.float32), 'sph_w1': glorot(ks[9], (HID, D)), 'sph_b1': jnp.zeros((D,), jnp.float32), 'wq': glorot(ks[10], (D, D)), 'wk': glorot(ks[11], (D, D)), 'wv': glorot(ks[12], (D, D))}
    _L3_gnn_all = _L3_gnn_setup()
    _L3_gnn_in = {k: v for k, v in _L3_gnn_all.items() if k in ('rad_w0', 'rad_b0', 'rad_w1', 'rad_b1', 'sph_w0', 'sph_b0', 'sph_w1', 'sph_b1', 'wq', 'wk', 'wv')}
    del _L3_gnn_all
    return {'x': x, 'src': src, 'dst': dst, 'edge_attr_10': edge_attr_10, 'edge_attr_32': edge_attr_32, 'edge_attr_4': edge_attr_4, 'edge_attr_64': edge_attr_64, 'edge_weight': edge_weight, 'node_vec1': node_vec1, 'L0_gnn_W': _L0_gnn_in['W'], 'L0_gnn_a': _L0_gnn_in['a'], 'L1_gnn_agg_W': _L1_gnn_in['agg_W'], 'L1_gnn_agg_b': _L1_gnn_in['agg_b'], 'L1_gnn_W': _L1_gnn_in['W'], 'L1_gnn_b': _L1_gnn_in['b'], 'L1_gnn_gamma': _L1_gnn_in['gamma'], 'L1_gnn_beta': _L1_gnn_in['beta'], 'L2_gnn_W_fc1': _L2_gnn_in['W_fc1'], 'L2_gnn_W_fc2': _L2_gnn_in['W_fc2'], 'L2_gnn_W_sc0': _L2_gnn_in['W_sc0'], 'L2_gnn_W_sc1': _L2_gnn_in['W_sc1'], 'L2_gnn_W_l1_0': _L2_gnn_in['W_l1_0'], 'L2_gnn_W_l1_1': _L2_gnn_in['W_l1_1'], 'L2_gnn_W_l2_0': _L2_gnn_in['W_l2_0'], 'L2_gnn_W_l2_1': _L2_gnn_in['W_l2_1'], 'L2_gnn_W_alpha': _L2_gnn_in['W_alpha'], 'L3_gnn_rad_w0': _L3_gnn_in['rad_w0'], 'L3_gnn_rad_b0': _L3_gnn_in['rad_b0'], 'L3_gnn_rad_w1': _L3_gnn_in['rad_w1'], 'L3_gnn_rad_b1': _L3_gnn_in['rad_b1'], 'L3_gnn_sph_w0': _L3_gnn_in['sph_w0'], 'L3_gnn_sph_b0': _L3_gnn_in['sph_b0'], 'L3_gnn_sph_w1': _L3_gnn_in['sph_w1'], 'L3_gnn_sph_b1': _L3_gnn_in['sph_b1'], 'L3_gnn_wq': _L3_gnn_in['wq'], 'L3_gnn_wk': _L3_gnn_in['wk'], 'L3_gnn_wv': _L3_gnn_in['wv']}

def reference(x, src, dst, edge_attr_10, edge_attr_32, edge_attr_4, edge_attr_64, edge_weight, node_vec1, L0_gnn_W, L0_gnn_a, L1_gnn_agg_W, L1_gnn_agg_b, L1_gnn_W, L1_gnn_b, L1_gnn_gamma, L1_gnn_beta, L2_gnn_W_fc1, L2_gnn_W_fc2, L2_gnn_W_sc0, L2_gnn_W_sc1, L2_gnn_W_l1_0, L2_gnn_W_l1_1, L2_gnn_W_l2_0, L2_gnn_W_l2_1, L2_gnn_W_alpha, L3_gnn_rad_w0, L3_gnn_rad_b0, L3_gnn_rad_w1, L3_gnn_rad_b1, L3_gnn_sph_w0, L3_gnn_sph_b0, L3_gnn_sph_w1, L3_gnn_sph_b1, L3_gnn_wq, L3_gnn_wk, L3_gnn_wv):
    import jax
    import jax.numpy as jnp

    def _L0_gnn_ref(h, edge_index, W, a):
        import jax, jax.numpy as jnp
        import numpy as np
        N = 6250
        E = 100000
        IN_F = 128
        OUT_F = 128
        NEG_SLOPE = 0.2
        EPS = 1e-10
        Wh = h @ W.T
        rows = edge_index[0]
        cols = edge_index[1]
        a1 = a[:OUT_F, 0]
        a2 = a[OUT_F:, 0]
        s1 = Wh @ a1
        s2 = Wh @ a2
        e = jax.nn.leaky_relu(s1[rows] + s2[cols], negative_slope=NEG_SLOPE)
        e = e - jnp.max(e)
        exp_e = jnp.exp(e)
        sum_exp = jax.ops.segment_sum(exp_e, rows, num_segments=N)
        alpha = exp_e / (sum_exp[rows] + EPS)
        h_prime = jax.ops.segment_sum(alpha[:, None] * Wh[cols], rows, num_segments=N)
        return jax.nn.elu(h_prime)

    def _L1_gnn_ref(x, edge_index, agg_W, agg_b, W, b, gamma, beta):
        import jax, jax.numpy as jnp
        import numpy as np
        N_NODES = 6250
        N_EDGES = 100000
        D = 128
        LN_EPS = 1e-05
        row, col = (edge_index[0], edge_index[1])
        num_nodes = x.shape[0]
        nbr_sum = jax.ops.segment_sum(x[row], col, num_segments=num_nodes)
        deg = jax.ops.segment_sum(jnp.ones_like(col, dtype=x.dtype), col, num_segments=num_nodes)
        deg = jnp.clip(deg, 1.0)
        aggregated = nbr_sum / deg[:, None]
        agg_features = aggregated @ agg_W + agg_b
        combined = jnp.concatenate([x, agg_features], axis=-1)
        out = jax.nn.relu(combined @ W + b)
        mu = jnp.mean(out, axis=-1, keepdims=True)
        var = jnp.var(out, axis=-1, keepdims=True)
        out = (out - mu) * jax.lax.rsqrt(var + LN_EPS) * gamma + beta
        return out

    def _L2_gnn_ref(x, node_attr, edge_src, edge_dst, edge_sh, edge_scalars, W_fc1, W_fc2, W_sc0, W_sc1, W_l1_0, W_l1_1, W_l2_0, W_l2_1, W_alpha):
        import jax, jax.numpy as jnp
        import numpy as np
        N, E, MUL = (6250, 50000, 32)
        SQ3 = float(np.sqrt(3.0))
        n = x.shape[0]
        x0 = x[:, :MUL]
        x1 = x[:, MUL:].reshape(n, MUL, 3)
        a = node_attr
        inv = 1.0 / np.sqrt(MUL)
        inv2 = 1.0 / np.sqrt(2 * MUL)
        sc0 = x0 @ W_sc0 * inv * a
        sc1 = jnp.einsum('nuc,uv->nvc', x1, W_sc1) * inv * a[:, :, None]
        sc = jnp.concatenate([sc0, sc1.reshape(n, 3 * MUL)], axis=1)
        y0 = x0 @ W_l1_0 * inv * a
        y1 = jnp.einsum('nuc,uv->nvc', x1, W_l1_1) * inv * a[:, :, None]
        h = jax.nn.silu(edge_scalars @ W_fc1 / np.sqrt(10.0))
        w = h @ W_fc2 / np.sqrt(100.0)
        w00, w11 = (w[:, :MUL], w[:, MUL:2 * MUL])
        w01, w10 = (w[:, 2 * MUL:3 * MUL], w[:, 3 * MUL:])
        x0e = y0[edge_src]
        x1e = y1[edge_src]
        sh0 = edge_sh[:, :1]
        sh1 = edge_sh[:, 1:4]
        m00 = w00 * x0e * sh0
        m11 = w11 * jnp.einsum('euc,ec->eu', x1e, sh1) / SQ3
        m01 = w01[:, :, None] * x0e[:, :, None] * sh1[:, None, :]
        m10 = w10[:, :, None] * x1e * sh0[:, :, None]
        edge_feat = jnp.concatenate([m00, m11, m01.reshape(-1, 3 * MUL), m10.reshape(-1, 3 * MUL)], axis=1)
        sums = jax.ops.segment_sum(edge_feat, edge_dst, num_segments=n)
        cnt = jax.ops.segment_sum(jnp.ones((edge_feat.shape[0],), x.dtype), edge_dst, num_segments=n)
        mean = sums / jnp.maximum(cnt, 1.0)[:, None]
        mid0 = mean[:, :2 * MUL]
        mid1 = mean[:, 2 * MUL:].reshape(n, 2 * MUL, 3)
        alpha = mid0 @ W_alpha * inv2 * a
        c0 = mid0 @ W_l2_0 * inv2 * a
        c1 = jnp.einsum('nuc,uv->nvc', mid1, W_l2_1) * inv2 * a[:, :, None]
        conv = jnp.concatenate([c0, c1.reshape(n, 3 * MUL)], axis=1)
        return sc + alpha * conv

    def _L3_gnn_ref(node_feats, edge_feats, chi_scalar, cutoffs, senders, receivers, rad_w0, rad_b0, rad_w1, rad_b1, sph_w0, sph_b0, sph_w1, sph_b1, wq, wk, wv):
        import jax, jax.numpy as jnp
        import numpy as np
        N_NODES = 12500
        N_EDGES = 200000
        D = 128
        H = 8
        HD = D // H
        RAD_IN, SPH_IN, HID = (64, 32, 256)
        AVG_NUM_NEIGHBORS = 16.0

        def _mlp(x, w0, b0, w1, b1):
            return jax.nn.silu(x @ w0 + b0) @ w1 + b1
        n_nodes = node_feats.shape[0]
        w_ij = _mlp(edge_feats, rad_w0, rad_b0, rad_w1, rad_b1)
        w_ij = w_ij + _mlp(chi_scalar, sph_w0, sph_b0, sph_w1, sph_b1)
        w_ij = w_ij.reshape(-1, H, HD)
        q = (node_feats @ wq).reshape(-1, H, HD)[receivers]
        k = (node_feats @ wk).reshape(-1, H, HD)[senders]
        alpha = (q * w_ij * k).sum(axis=-1) / jnp.sqrt(jnp.float32(HD))
        alpha = alpha * cutoffs[:, None]
        v = (node_feats @ wv).reshape(-1, H, HD)[senders]
        out = jax.ops.segment_sum(alpha[..., None] * v, receivers, num_segments=n_nodes) / AVG_NUM_NEIGHBORS
        return out.reshape(n_nodes, D)
    edge_index = jnp.stack([src, dst])
    x = _layernorm(x + _L0_gnn_ref(x, edge_index, L0_gnn_W, L0_gnn_a), axis=-1)
    x = _layernorm(x + _L1_gnn_ref(x, edge_index, L1_gnn_agg_W, L1_gnn_agg_b, L1_gnn_W, L1_gnn_b, L1_gnn_gamma, L1_gnn_beta), axis=-1)
    x = _layernorm(x + _L2_gnn_ref(x, node_vec1, src, dst, edge_attr_4, edge_attr_10, L2_gnn_W_fc1, L2_gnn_W_fc2, L2_gnn_W_sc0, L2_gnn_W_sc1, L2_gnn_W_l1_0, L2_gnn_W_l1_1, L2_gnn_W_l2_0, L2_gnn_W_l2_1, L2_gnn_W_alpha), axis=-1)
    x = _layernorm(x + _L3_gnn_ref(x, edge_attr_64, edge_attr_32, edge_weight, src, dst, L3_gnn_rad_w0, L3_gnn_rad_b0, L3_gnn_rad_w1, L3_gnn_rad_b1, L3_gnn_sph_w0, L3_gnn_sph_b0, L3_gnn_sph_w1, L3_gnn_sph_b1, L3_gnn_wq, L3_gnn_wk, L3_gnn_wv), axis=-1)
    return x

_drawn_inputs = setup_inputs


def setup_inputs(seed=0):
    import zlib

    import numpy as np

    out = dict(_drawn_inputs(seed))
    spreads = {'L1_gnn_agg_b': (0.0, 0.1),
     'L1_gnn_b': (0.0, 0.1),
     'L1_gnn_gamma': (1.0, 0.2),
     'L1_gnn_beta': (0.0, 0.1),
     'L3_gnn_rad_b0': (0.0, 0.499),
     'L3_gnn_rad_b1': (0.0, 0.376),
     'L3_gnn_sph_b0': (0.0, 0.556),
     'L3_gnn_sph_b1': (0.0, 0.392)}
    factors = {'edge_attr_10': 8.0,
     'edge_attr_4': 8.0,
     'L2_gnn_W_fc1': 8.0,
     'L2_gnn_W_fc2': 8.0,
     'L2_gnn_W_l1_0': 8.0,
     'L2_gnn_W_l1_1': 8.0,
     'L2_gnn_W_l2_0': 8.0,
     'L2_gnn_W_l2_1': 8.0,
     'L2_gnn_W_alpha': 8.0}
    for name, (base, spread) in spreads.items():
        noise = np.random.default_rng([zlib.crc32(name.encode()), seed]).standard_normal(out[name].shape)
        drawn = base * np.exp(spread * noise) if base else spread * noise
        out[name] = jnp.asarray(drawn.astype(out[name].dtype))
    for name, factor in factors.items():
        out[name] = (out[name] * factor).astype(out[name].dtype)
    return out
```

```python
from contextlib import ExitStack

import concourse.bass as bass
import numpy as np
from concourse import mybir

f32 = mybir.dt.float32
bf16 = mybir.dt.bfloat16
i32 = mybir.dt.int32
i16 = mybir.dt.int16
ALU = mybir.AluOpType
ACT = mybir.ActivationFunctionType
AX = mybir.AxisListType

P = 128
N = 6250
E = 206250
D = 128
NW = -(-N // P)
NP = NW * P
PAD = NP - 1
T = 4
GE = T * P
S = 4
NI = -(-E // (S * GE))
NG = NI * S
NT = NG * T
EP = NT * P
EA = EP + GE
R = 7
NB = NW // R
MUL = 32
HEADS, HD = 8, 16
HID = 256
LN_EPS = 1e-5
SOFT_EPS = 1e-10


class Names:
    pass


class Steps:

    def __init__(self, eng, sem, base=0):
        self.eng, self.sem, self.base, self.n = eng, sem, base, 0

    def mark(self, ins):
        self.n += 1
        ins.then_inc(self.sem, 1)

    def wait(self):
        self.eng.wait_ge(self.sem, self.base + self.n)

    def do(self, ins):
        self.mark(ins)
        self.wait()


def over(ap, shape, axis):
    return ap.unsqueeze(axis).to_broadcast(shape)


def win(ap, w):
    return ap[:, bass.ds(w, 1), :].rearrange("p a f -> p (a f)")


def node_products(nc, c, name, ident, sources, weights, width, evacuate, bias=None):
    ns = len(sources)
    with ExitStack() as st:
        staged = st.enter_context(nc.sbuf_tensor(f"{name}_staged", [P, R, ns, P], f32))
        turned = st.enter_context(nc.sbuf_tensor(f"{name}_turned", [P, R, ns, P], f32))
        bank = st.enter_context(nc.psum_tensor(f"{name}_bank", [P, R, 4 * P], f32))
        stage_done, turn_done, copy_done, product_done, out_done = c.ring
        used = NW * c.ring_uses
        c.ring_uses += 1

        with nc.Block() as block:

            @block.vector
            def _(dve):
                with dve.Fori(0, NB) as i:
                    for j in range(R):
                        dve.wait_ge(turn_done, used + R * i + j + 1)
                        for n, source in enumerate(sources):
                            ins = nc.vector.tensor_copy(staged[:, j, n, :], source(R * i + j))
                        ins.then_inc(stage_done, 1)

            @block.tensor
            def _(pe):
                if used == 0:
                    pe.sem_inc(turn_done, R)
                if used == 0:
                    pe.sem_inc(product_done, R)
                with pe.Fori(0, NB) as i:
                    for j in range(R):
                        pe.wait_ge(stage_done, used + R * i + j + 1)
                        pe.wait_ge(out_done, used + R * i + j + 1)
                        for n in range(ns):
                            ins = nc.tensor.transpose(bank[:, j, n * P:(n + 1) * P], staged[:, j, n, :], ident)
                        ins.then_inc(turn_done, 1)
                    for j in range(R):
                        pe.wait_ge(copy_done, used + R + R * i + j + 1)
                        out = bank[:, j, 2 * P:2 * P + width]
                        for n in range(ns):
                            ins = nc.tensor.matmul(out, turned[:, j, n, :], weights[n], start=n == 0,
                                                   stop=bias is None and n == ns - 1)
                        if bias is not None:
                            ins = nc.tensor.matmul(out, bias[0], bias[1], start=False, stop=True)
                        ins.then_inc(product_done, 1)

            @block.scalar
            def _(act):
                if used == 0:
                    act.sem_inc(copy_done, R)
                if used == 0:
                    act.sem_inc(out_done, R)
                with act.Fori(0, NB) as i:
                    for j in range(R):
                        act.wait_ge(turn_done, used + R + R * i + j + 1)
                        act.wait_ge(product_done, used + R * i + j + 1)
                        nc.scalar.activation(turned[:, j].rearrange("p n f -> p (n f)"), bank[:, j, 0:ns * P], ACT.Copy).then_inc(copy_done, 1)
                    for j in range(R):
                        act.wait_ge(product_done, used + R + R * i + j + 1)
                        evacuate(nc, R * i + j, bank[:, j, 2 * P:2 * P + width]).then_inc(out_done, 1)


def layer_norm(nc, c, x, tmp, stat):
    shape = [P, NW, D]
    steps_done, var_ready, std_ready = c.norm
    used = c.norm_uses
    c.norm_uses += 1
    with nc.Block() as block:

        @block.vector
        def _(dve):
            own = Steps(dve, steps_done, 6 * used)
            own.do(nc.vector.tensor_reduce(stat[:, 0], x, AX.X, ALU.add))
            own.do(nc.vector.tensor_scalar(stat[:, 0], stat[:, 0], 1.0 / D, None, ALU.mult))
            own.do(nc.vector.tensor_tensor(x, x, over(stat[:, 0], shape, 2), ALU.subtract))
            own.do(nc.vector.tensor_tensor(tmp, x, x, ALU.mult))
            own.do(nc.vector.tensor_reduce(stat[:, 1], tmp, AX.X, ALU.add))
            nc.vector.tensor_scalar(stat[:, 1], stat[:, 1], 1.0 / D, LN_EPS, ALU.mult, ALU.add).then_inc(var_ready, 1)
            dve.wait_ge(std_ready, used + 1)
            own.do(nc.vector.reciprocal(stat[:, 1], stat[:, 0]))
            nc.vector.tensor_tensor(x, x, over(stat[:, 1], shape, 2), ALU.mult)

        @block.scalar
        def _(act):
            act.wait_ge(var_ready, used + 1)
            nc.scalar.activation(stat[:, 0], stat[:, 1], ACT.Sqrt).then_inc(std_ready, 1)


def store(nc, c, pairs):
    c.stores += len(pairs)
    with nc.Block() as block:

        @block.sync
        def _(sp):
            for dst, src in pairs:
                sp.dma_start(dst, src).then_inc(c.landed, 16)
            sp.wait_ge(c.landed, 16 * c.stores)


def load_span(eng, spans, g):
    v = eng.value_load(spans[0:1, bass.ds(g, 1)], min_val=0, max_val=2 ** 31 - 1)
    n = eng.snap(v & 63)
    first = eng.snap((v >> 6) & 63)
    before = eng.snap(v >> 12)
    return first, n, before


def window_of(nc, first, j):
    return nc.s_assert_within(first + j, 0, NW - 1, skip_runtime_bounds_check_because="spans hold windows of real nodes")


def vector_windows(nc, dve, c, g, acc, part_ps, weight=None):
    first, n, before = load_span(dve, c.spans, g)
    key = over(c.keys[:, bass.ds(g * T, T)], [P, T, P], 2)
    with dve.Fori(0, n) as j:
        w = window_of(nc, first, j)
        k = dve.snap(before + j)
        nodes = c.iota[:, bass.ds(w * P, P)].unsqueeze(1).to_broadcast([P, T, P])
        dve.wait_ge(c.sums_done, k)
        if weight is None:
            nc.vector.tensor_tensor(c.hot[:], nodes, key, ALU.is_equal).then_inc(c.hot_done, 1)
        else:
            nc.vector.tensor_tensor(c.hot[:], nodes, key, ALU.is_equal).then_inc(c.equal_done, 1)
            dve.wait_ge(c.equal_done, k + 1)
            wt = over(weight[:, bass.ds(g * T, T)], [P, T, P], 2)
            nc.vector.tensor_tensor(c.hot[:], c.hot[:], wt, ALU.mult).then_inc(c.hot_done, 1)
        dve.wait_ge(c.sums_done, k + 1)
        dve.wait_ge(c.added, k)
        nc.vector.tensor_tensor(win(acc, w), win(acc, w), part_ps, ALU.add).then_inc(c.added, 1)


def tensor_windows(nc, pe, c, g, part_ps, rows):
    first, n, before = load_span(pe, c.spans, g)
    with pe.Fori(0, n) as j:
        k = pe.snap(before + j)
        pe.wait_ge(c.hot_done, k + 1)
        pe.wait_ge(c.added, k)
        for t in range(T):
            ins = nc.tensor.matmul(part_ps, c.hot[:, t, :], rows[:, t, :], start=t == 0, stop=t == T - 1)
        ins.then_inc(c.sums_done, 1)


def span_semaphores(sem, c, name):
    c.hot_done = sem(f"{name}_hot_done")
    c.equal_done = sem(f"{name}_equal_done")
    c.sums_done = sem(f"{name}_sums_done")
    c.added = sem(f"{name}_added")


def sum_rows(nc, name, c, table, indices, acc, weight=None):
    with ExitStack() as st:
        def sb(n, shape, dt=f32):
            return st.enter_context(nc.sbuf_tensor(f"{name}_{n}", shape, dt))

        rows = sb("rows", [P, S, T, D + 1])
        stage = sb("stage", [P, S, T], i32)
        c.hot = sb("hot", [P, T, P])
        part_ps = st.enter_context(nc.psum_tensor(f"{name}_part", [P, 512], f32))
        part = part_ps[:, 0:D + 1]
        sem = nc.alloc_semaphore
        span_semaphores(sem, c, name)
        ones_set = sem(f"{name}_ones_set")
        staged = sem(f"{name}_staged")
        rows_used = sem(f"{name}_rows_used")
        turn = sem(f"{name}_turn")
        gathered = [nc.alloc_semaphore(f"{name}_gathered{s}") for s in range(S)]

        with nc.Block() as block:

            @block.scalar
            def _(act):
                with act.Fori(0, NI) as i:
                    for s in range(S):
                        act.wait_ge(gathered[s], 16 * T * i)
                        nc.scalar.activation(stage[:, s], indices(S * i + s), ACT.Copy).then_inc(staged, 1)

            @block.gpsimd
            def _(pool):
                with pool.Fori(0, NI) as i:
                    for s in range(S):
                        pool.wait_ge(staged, S * i + s + 1)
                        pool.wait_ge(rows_used, S * i + s + 1)
                        pool.sem_inc(turn, 1)
                        for t in range(T):
                            pool.indirect_dma_start(
                                rows[:, s, t, 0:D], None, table,
                                bass.IndirectOffsetOnAxis(ap=stage[:, s, t:t + 1], axis=0)).then_inc(gathered[s], 16)

            @block.vector
            def _(dve):
                nc.vector.memset(rows[:, :, :, D:D + 1], 1.0).then_inc(ones_set, 1)
                dve.sem_inc(rows_used, S)
                with dve.Fori(0, NI) as i:
                    for s in range(S):
                        vector_windows(nc, dve, c, S * i + s, acc, part, weight)
                        dve.sem_inc(rows_used, 1)

            @block.tensor
            def _(pe):
                pe.wait_ge(ones_set, 1)
                with pe.Fori(0, NI) as i:
                    for s in range(S):
                        pe.wait_ge(gathered[s], 16 * T * (i + 1))
                        tensor_windows(nc, pe, c, S * i + s, part, rows[:, s])


def gnn_kernel(nc, a, out):
    top = ExitStack()

    def dram(name, shape, dt=f32):
        return nc.dram_tensor(name, shape, dt).ap()

    def sb(st, name, shape, dt=f32):
        return st.enter_context(nc.sbuf_tensor(name, shape, dt))

    sem = nc.alloc_semaphore
    shared = Names()
    shared.ring = [sem(n) for n in ("stage_done", "turn_done", "copy_done", "product_done", "out_done")]
    shared.norm = [sem(n) for n in ("norm_steps_done", "var_ready", "std_ready")]
    shared.landed = sem("landed")
    shared.ring_uses = shared.norm_uses = shared.stores = 0
    lo_dram = dram("lo_dram", [2, EP], bf16)
    sorted_dram = dram("sorted_dram", [EP, 4], i32)
    wh_dram = dram("wh_dram", [NP, D])
    x_dram = dram("x_dram", [NP, D])
    y_dram = dram("y_dram", [NP, D])
    q_dram = dram("q_dram", [NP, D])
    kv_dram = dram("kv_dram", [NP, 2 * D])

    with top:
        iota = sb(top, "iota", [P, NP])
        own_lane = sb(top, "own_lane", [P, 1])
        ident = sb(top, "ident", [P, P])
        x = sb(top, "x", [P, NW, D])
        src = sb(top, "src", [P, NT], i32)
        dst = sb(top, "dst", [P, NT], i32)
        spans = sb(top, "spans", [1, 2, NG], i32)
        stat = sb(top, "stat", [P, 2, NW])
        degree = sb(top, "degree", [P, NW])
        keys = sb(top, "keys", [P, NT])
        L0 = ExitStack()
        before = sb(L0, "before", [P, P])
        ones = sb(L0, "ones", [P, P])
        s_nodes = sb(L0, "s_nodes", [P, NW, 2])
        w_ext = sb(L0, "w_ext", [P, D + 2])
        w0 = sb(L0, "w0", [P, D])
        a0 = sb(L0, "a0", [P, 2])
        wh = sb(L0, "wh", [P, NW, D])
        xt = sb(L0, "xt", [P, R, P])

        loaded = sem("loaded")
        pool_steps = sem("pool_steps")
        const_done = sem("const_done")
        with nc.Block() as block:

            @block.sync
            def _(sp):
                loads = [(x[:], a["x"]), (src[:], a["src_tiles"]),
                         (dst[:], a["dst_tiles"]), (w0[:], a["L0_W"]), (a0[:], a["L0_a"]),
                         (w_ext[:, 0:D], a["L0_WT"])]
                for to, of in loads:
                    sp.dma_start(to, of).then_inc(loaded, 16)
                sp.wait_ge(loaded, 16 * len(loads))

            @block.gpsimd
            def _(pool):
                nc.gpsimd.iota(iota[:], pattern=[[1, NP]], base=0, channel_multiplier=0,
                               allow_small_or_imprecise_dtypes=True).then_inc(pool_steps, 1)
                nc.gpsimd.iota(own_lane[:], pattern=[[0, 1]], base=0, channel_multiplier=1,
                               allow_small_or_imprecise_dtypes=True).then_inc(pool_steps, 1)

            @block.vector
            def _(dve):
                dve.wait_ge(pool_steps, 2)
                nc.vector.tensor_scalar(ident[:], iota[:, 0:P], own_lane[:], None, ALU.is_equal)
                nc.vector.tensor_scalar(before[:], iota[:, 0:P], own_lane[:], None, ALU.is_gt)
                nc.vector.memset(ones[:], 1.0)

        with ExitStack() as st:
            ps = st.enter_context(nc.psum_tensor("wh_ps", [P, R + 1, 4 * P], f32))
            xt_loaded = [sem(f"xt_loaded{j}") for j in range(R)]
            ext_ready = sem("ext_ready")
            ext_done = sem("ext_done")
            wh_product = sem("wh_product")
            wh_taken = sem("wh_taken")
            with nc.Block() as block:

                @block.sync
                def _(sp):
                    with sp.Fori(0, NB) as i:
                        for j in range(R):
                            sp.wait_ge(wh_product, R * i + j + 1)
                            sp.dma_start(xt[:, j, :], a["xT"][:, bass.ds((R * i + j) * P, P)]).then_inc(xt_loaded[j], 16)

                @block.tensor
                def _(pe):
                    nc.tensor.matmul(ps[:, R, 0:2], w0[:], a0[:], start=True, stop=True).then_inc(ext_ready, 1)
                    pe.sem_inc(wh_product, R)
                    pe.wait_ge(ext_done, 1)
                    with pe.Fori(0, NB) as i:
                        for j in range(R):
                            pe.wait_ge(xt_loaded[j], 16 * (i + 1))
                            pe.wait_ge(wh_taken, R * i + j + 1)
                            nc.tensor.matmul(ps[:, j, 0:D + 2], xt[:, j, :], w_ext[:], start=True, stop=True).then_inc(wh_product, 1)

                @block.scalar
                def _(act):
                    act.sem_inc(wh_taken, R)
                    with act.Fori(0, NB) as i:
                        for j in range(R):
                            act.wait_ge(wh_product, R + R * i + j + 1)
                            nc.scalar.activation(win(s_nodes, R * i + j), ps[:, j, D:D + 2], ACT.Copy)
                            nc.scalar.activation(win(wh, R * i + j), ps[:, j, 0:D], ACT.Copy).then_inc(wh_taken, 1)

                @block.vector
                def _(dve):
                    dve.wait_ge(ext_ready, 1)
                    nc.vector.tensor_copy(w_ext[:, D:D + 2], ps[:, R, 0:2]).then_inc(ext_done, 1)

        rec = sb(L0, "rec", [P, NT, 3], i32)
        hi = sb(L0, "hi", [P, 2, NT])
        with ExitStack() as st:
            flat = sb(st, "flat", [P, 2, NT], i32)
            flat_lo = sb(st, "flat_lo", [P, 2, NT], bf16)
            mask = sb(st, "mask", [P, NT], i16)
            ones_row = sb(st, "ones_row", [P, NT], bf16)
            running = sb(st, "running", [P, NT])
            place = sb(st, "place", [P, NT])
            count = sb(st, "count", [P, NW])
            offset = sb(st, "offset", [P, NW])
            upto = sb(st, "upto", [P, NW])
            count_ps = st.enter_context(nc.psum_tensor("count_ps", [P, 2, 512], f32))
            flat_loaded = sem("flat_loaded")
            lo_ready = sem("lo_ready")
            lo_stored = sem("lo_stored")
            own_done = sem("rank_own_done")
            counted = sem("counted")
            totals_done = sem("totals_done")
            first_done = sem("first_done")
            second_done = sem("second_done")
            rank_turn = sem("rank_turn")
            flat_src = a["edges"].rearrange("k (p c) -> p k c", p=P)
            with nc.Block() as block:

                @block.sync
                def _(sp):
                    sp.dma_start(flat[:], flat_src).then_inc(flat_loaded, 16)
                    sp.dma_start(wh_dram.rearrange("(w p) f -> p w f", p=P), wh[:]).then_inc(flat_loaded, 16)
                    sp.wait_ge(lo_ready, 1)
                    sp.dma_start(lo_dram.rearrange("k (p c) -> p k c", p=P), flat_lo[:]).then_inc(lo_stored, 16)
                    sp.wait_ge(flat_loaded, 32)
                    sp.wait_ge(lo_stored, 16)

                @block.gpsimd
                def _(pool):
                    last = s_nodes[:, NW - 1, 1:2]
                    nc.gpsimd.affine_select(out=last, in_=last, compare_op=ALU.is_gt, fill=-1e30,
                                            base=N - (NW - 1) * P, pattern=[[0, 1]], channel_multiplier=-1)

                @block.tensor
                def _(pe):
                    pe.wait_ge(counted, 1)
                    nc.tensor.matmul(count_ps[:, 0, 0:NW], before[:], count[:], start=True, stop=True)
                    nc.tensor.matmul(count_ps[:, 1, 0:NW], ones[:], count[:], start=True, stop=True).then_inc(totals_done, 1)

                @block.vector
                def _(dve):
                    own = Steps(dve, own_done)
                    own.mark(nc.vector.memset(ones_row[:], 1.0))
                    for n, nodes in enumerate((src, dst)):
                        own.do(nc.vector.tensor_scalar(rec[:, :, 2], nodes[:], 7, None, ALU.logical_shift_right))
                        own.do(nc.vector.tensor_copy(hi[:, n, :], rec[:, :, 2]))
                        own.mark(nc.vector.tensor_copy(rec[:, :, n], nodes[:]))
                    dve.wait_ge(flat_loaded, 32)
                    own.do(nc.vector.tensor_scalar(flat[:], flat[:], P - 1, None, ALU.bitwise_and))
                    nc.vector.tensor_copy(flat_lo[:], flat[:]).then_inc(lo_ready, 1)
                    with dve.Fori(0, NW) as w:
                        dve.wait_ge(first_done, 2 * w)
                        nc.vector.tensor_scalar(mask[:], hi[:, 0, :], iota[:, bass.ds(w, 1)], None, ALU.is_equal).then_inc(first_done, 1)
                        dve.wait_ge(first_done, 2 * w + 1)
                        nc.vector.tensor_reduce(count[:, bass.ds(w, 1)], mask[:], AX.X, ALU.add).then_inc(first_done, 1)
                    dve.wait_ge(first_done, 2 * NW)
                    dve.sem_inc(counted, 1)
                    dve.wait_ge(totals_done, 1)
                    own.do(nc.vector.tensor_copy(offset[:], count_ps[:, 1, 0:NW]))
                    own.do(nc.vector.tensor_tensor_scan(upto[:], ones_row[:, 0:NW], offset[:], 0.0, ALU.mult, ALU.add))
                    own.do(nc.vector.tensor_tensor(upto[:], upto[:], offset[:], ALU.subtract))
                    own.do(nc.vector.tensor_tensor(upto[:], upto[:], count_ps[:, 0, 0:NW], ALU.add))
                    own.do(nc.vector.tensor_scalar(offset[:], upto[:], -1.0, None, ALU.add))
                    own.do(nc.vector.memset(place[:], 0.0))
                    with dve.Fori(0, NW) as w:
                        dve.wait_ge(second_done, 3 * w)
                        nc.vector.tensor_scalar(mask[:], hi[:, 0, :], iota[:, bass.ds(w, 1)], None, ALU.is_equal).then_inc(second_done, 1)
                        dve.wait_ge(second_done, 3 * w + 1)
                        nc.vector.tensor_tensor_scan(running[:], ones_row[:], mask[:], offset[:, bass.ds(w, 1)], ALU.mult, ALU.add).then_inc(second_done, 1)
                        dve.wait_ge(second_done, 3 * w + 2)
                        dve.sem_inc(rank_turn, 1)
                        nc.vector.copy_predicated(place[:], mask[:], running[:]).then_inc(second_done, 1)
                    dve.wait_ge(second_done, 3 * NW)
                    group4, tile = flat[:, 0, :], flat[:, 1, :]
                    spot = rec[:, :, 2]
                    own.do(nc.vector.tensor_copy(spot, place[:]))
                    own.mark(nc.vector.tensor_scalar(group4, spot, 9, 2, ALU.logical_shift_right, ALU.logical_shift_left))
                    own.do(nc.vector.tensor_scalar(tile, spot, T - 1, None, ALU.bitwise_and))
                    own.mark(nc.vector.tensor_tensor(group4, group4, tile, ALU.bitwise_or))
                    own.do(nc.vector.tensor_scalar(spot, spot, 2, P - 1, ALU.logical_shift_right, ALU.bitwise_and))
                    own.do(nc.vector.tensor_scalar(place[:], spot, float(NT), None, ALU.mult))
                    nc.vector.tensor_tensor(spot, place[:], group4, ALU.add)

        with ExitStack() as st:
            lanes = sb(st, "lanes", [P, S, 2, GE], bf16)
            hot_t = sb(st, "hot_t", [P, S, 2, GE])
            pick = sb(st, "pick", [P, 2, T, 2, NW])
            pick_prod = sb(st, "pick_prod", [P, T, 2, NW])
            stage = sb(st, "rec_stage", [P, S, T, 4], i32)
            score_ps = st.enter_context(nc.psum_tensor("score_ps", [P, S, 512], f32))
            lanes_in = [sem(f"lanes_in{s}") for s in range(S)]
            hot_ready = sem("hot_ready")
            picked_from = sem("picked_from")
            tables_done = sem("tables_done")
            scored = sem("scored")
            rec_staged = sem("rec_staged")
            pick_own = sem("pick_own")
            turn = sem("scatter_turn")
            sent = [sem(f"sent{s}") for s in range(S)]
            with nc.Block() as block:

                @block.sync
                def _(sp):
                    with sp.Fori(0, NI) as i:
                        for s in range(S):
                            sp.wait_ge(hot_ready, S * i + s + 1)
                            rows = lo_dram[:, bass.ds((S * i + s) * GE, GE)].partition_broadcast(P)
                            sp.dma_start(lanes[:, s], rows).then_inc(lanes_in[s], 16)

                @block.tensor
                def _(pe):
                    pe.sem_inc(tables_done, S)
                    with pe.Fori(0, NI) as i:
                        for s in range(S):
                            pe.wait_ge(hot_ready, S + S * i + s + 1)
                            pe.wait_ge(scored, S * i + s + 1)
                            table = score_ps[:, s, 0:T * 2 * NW].rearrange("p (t k w) -> p t k w", t=T, k=2)
                            for t in range(T):
                                for n in range(2):
                                    ins = nc.tensor.matmul(table[:, t, n, :], hot_t[:, s, n, t * P:(t + 1) * P],
                                                           s_nodes[:, :, n], start=True, stop=True)
                            ins.then_inc(tables_done, 1)

                @block.vector
                def _(dve):
                    dve.sem_inc(hot_ready, S)
                    dve.sem_inc(scored, S)
                    with dve.Fori(0, NI) as i:
                        for s in range(S):
                            dve.wait_ge(lanes_in[s], 16 * (i + 1))
                            dve.wait_ge(tables_done, S * i + s + 1)
                            nc.vector.tensor_scalar(hot_t[:, s], lanes[:, s], own_lane[:], None, ALU.is_equal).then_inc(hot_ready, 1)
                        own = Steps(dve, pick_own, i * (2 * S))
                        for s in range(S):
                            g = S * i + s
                            windows = hi[:, :, bass.ds(g * T, T)].rearrange("p k t -> p t k").unsqueeze(3).to_broadcast([P, T, 2, NW])
                            cols = iota[:, 0:NW].unsqueeze(1).unsqueeze(1).to_broadcast([P, T, 2, NW])
                            own.do(nc.vector.tensor_tensor(pick[:, 0], cols, windows, ALU.is_equal))
                            dve.wait_ge(tables_done, S + g + 1)
                            table = score_ps[:, s, 0:T * 2 * NW].rearrange("p (t k w) -> p t k w", t=T, k=2)
                            own.do(nc.vector.tensor_tensor(pick_prod[:], pick[:, 0], table, ALU.mult))
                            dve.wait_ge(sent[s], 16 * T * i)
                            score = stage[:, s, :, 3].bitcast(f32)
                            nc.vector.tensor_reduce(score, pick_prod[:], AX.XY, ALU.add).then_inc(scored, 1)

                @block.scalar
                def _(act):
                    with act.Fori(0, NI) as i:
                        for s in range(S):
                            act.wait_ge(sent[s], 16 * T * i)
                            nc.scalar.activation(stage[:, s, :, 0:3], rec[:, bass.ds((S * i + s) * T, T), :], ACT.Copy).then_inc(rec_staged, 1)

                @block.gpsimd
                def _(pool):
                    with pool.Fori(0, NI) as i:
                        for s in range(S):
                            pool.wait_ge(rec_staged, S * i + s + 1)
                            pool.wait_ge(scored, S + S * i + s + 1)
                            pool.sem_inc(turn, 1)
                            for t in range(T):
                                pool.indirect_dma_start(
                                    sorted_dram, bass.IndirectOffsetOnAxis(ap=stage[:, s, t, 2:3], axis=0),
                                    stage[:, s, t, :], None).then_inc(sent[s], 16)
                    for s in range(S):
                        pool.wait_ge(sent[s], 16 * T * NI)
                    pool.sem_inc(turn, 1)
        L0.close()

        L0 = ExitStack()
        srec = sb(L0, "srec", [P, NG, T, 4], i32)
        weight = sb(L0, "weight", [P, NT])
        with ExitStack() as st:
            wide = sb(st, "wide", [P, 2, NT])
            wide_i = sb(st, "wide_i", [P, NT], i32)
            ends = sb(st, "ends", [P, 2, 2, NG])
            ends_all = sb(st, "ends_all", [P, 2, 2, NG])
            row = sb(st, "row", [1, 2, 3, NG])
            row_i = sb(st, "row_i", [1, 2, 3, NG], i32)
            one_row = sb(st, "one_row", [1, NG])
            top_score = sb(st, "top_score", [P, 3])
            recs_in = sem("recs_in")
            own_done = sem("span_own_done")
            ends_ready = sem("ends_ready")
            ends_reduced = sem("ends_reduced")
            weights_in = sem("weights_in")
            with nc.Block() as block:

                @block.sync
                def _(sp):
                    sp.dma_start(srec[:].rearrange("p g t c -> p (g t c)"),
                                 sorted_dram.rearrange("(p e) c -> p (e c)", p=P)).then_inc(recs_in, 16)

                @block.vector
                def _(dve):
                    own = Steps(dve, own_done)
                    own.mark(nc.vector.memset(one_row[:], 1.0))
                    dve.wait_ge(recs_in, 16)
                    flat_rec = srec[:].rearrange("p g t c -> p (g t) c")
                    own.do(nc.vector.tensor_copy(keys[:], flat_rec[:, :, 0]))
                    for n, nodes in enumerate((flat_rec[:, :, 0], dst[:])):
                        own.do(nc.vector.tensor_scalar(wide_i[:], nodes, 7, None, ALU.logical_shift_right))
                        own.do(nc.vector.tensor_copy(wide[:, n], wide_i[:]))
                        by_group = wide[:, n].rearrange("p (g t) -> p g t", t=T)
                        own.mark(nc.vector.tensor_reduce(ends[:, n, 1], by_group, AX.X, ALU.max))
                        own.do(nc.vector.tensor_reduce(ends[:, n, 0], by_group, AX.X, ALU.min, negate=True))
                    score = flat_rec[:, :, 3].bitcast(f32)
                    own.do(nc.vector.tensor_reduce(top_score[:, 0:1], score, AX.X, ALU.max))
                    dve.sem_inc(ends_ready, 1)
                    own.do(nc.vector.tensor_scalar(weight[:], score, 0.2, None, ALU.mult))
                    own.do(nc.vector.tensor_tensor(weight[:], weight[:], score, ALU.max))
                    dve.wait_ge(ends_reduced, 2)
                    own.do(nc.vector.tensor_scalar(top_score[:, 2:3], top_score[:, 1:2], 0.2, None, ALU.mult))
                    own.do(nc.vector.tensor_tensor(top_score[:, 2:3], top_score[:, 2:3], top_score[:, 1:2], ALU.max))
                    nc.vector.tensor_scalar(weight[:], weight[:], top_score[:, 2:3], None, ALU.subtract).then_inc(weights_in, 1)
                    for n in range(2):
                        lows, highs = ends_all[0:1, n, 0], ends_all[0:1, n, 1]
                        own.mark(nc.vector.tensor_scalar(row[:, n, 0], lows, -1.0, None, ALU.mult))
                        own.do(nc.vector.tensor_tensor(row[:, n, 1], highs, lows, ALU.add))
                        own.do(nc.vector.tensor_scalar(row[:, n, 1], row[:, n, 1], 1.0, None, ALU.add))
                        own.do(nc.vector.tensor_tensor_scan(row[:, n, 2], one_row[:], row[:, n, 1], 0.0, ALU.mult, ALU.add))
                        own.do(nc.vector.tensor_tensor(row[:, n, 2], row[:, n, 2], row[:, n, 1], ALU.subtract))
                        own.do(nc.vector.tensor_copy(row_i[:, n], row[:, n]))
                        own.mark(nc.vector.tensor_scalar(row_i[:, n, 0], row_i[:, n, 0], 6, None, ALU.logical_shift_left))
                        own.do(nc.vector.tensor_scalar(row_i[:, n, 2], row_i[:, n, 2], 12, None, ALU.logical_shift_left))
                        own.do(nc.vector.tensor_tensor(row_i[:, n, 0], row_i[:, n, 0], row_i[:, n, 1], ALU.bitwise_or))
                        own.do(nc.vector.tensor_tensor(spans[:, n], row_i[:, n, 0], row_i[:, n, 2], ALU.bitwise_or))

                @block.gpsimd
                def _(pool):
                    pool.wait_ge(ends_ready, 1)
                    from_all = bass.bass_isa.ReduceOp.max
                    nc.gpsimd.partition_all_reduce(top_score[:, 1:2], top_score[:, 0:1], P, from_all).then_inc(ends_reduced, 1)
                    nc.gpsimd.partition_all_reduce(ends_all[:].rearrange("p a b g -> p (a b g)"),
                                                   ends[:].rearrange("p a b g -> p (a b g)"), P, from_all).then_inc(ends_reduced, 1)

                @block.scalar
                def _(act):
                    act.wait_ge(weights_in, 1)
                    nc.scalar.activation(weight[:], weight[:], ACT.Exp)

        c = Names()
        c.iota, c.keys, c.spans = iota, keys, spans[:, 0]
        acc_scope = ExitStack()
        acc = sb(acc_scope, "acc0", [P, NW, D + 1])
        tmp = sb(acc_scope, "tmp0", [P, NW, D])
        with nc.Block() as block:

            @block.vector
            def _(dve):
                nc.vector.memset(acc[:], 0.0)

        flat_rec = srec[:].rearrange("p g t c -> p (g t) c")
        sum_rows(nc, "soft", c, wh_dram, lambda g: flat_rec[:, bass.ds(g * T, T), 1], acc, weight)

        def soft_end():
            own_done = sem("elu_own_done")
            low_ready = sem("low_ready")
            exp_done = sem("exp_done")
            shape = [P, NW, D]
            with nc.Block() as block:

                @block.vector
                def _(dve):
                    own = Steps(dve, own_done)
                    h = acc[:, :, 0:D]
                    own.do(nc.vector.tensor_scalar(stat[:, 0], acc[:, :, D], SOFT_EPS, None, ALU.add))
                    own.do(nc.vector.reciprocal(stat[:, 1], stat[:, 0]))
                    own.do(nc.vector.tensor_tensor(h, h, over(stat[:, 1], shape, 2), ALU.mult))
                    nc.vector.tensor_scalar(tmp[:], h, 0.0, None, ALU.min).then_inc(low_ready, 1)
                    own.do(nc.vector.tensor_scalar(h, h, 0.0, None, ALU.max))
                    own.do(nc.vector.tensor_tensor(x[:], x[:], h, ALU.add))
                    dve.wait_ge(exp_done, 1)
                    own.do(nc.vector.tensor_scalar(tmp[:], tmp[:], -1.0, None, ALU.add))
                    own.do(nc.vector.tensor_tensor(x[:], x[:], tmp[:], ALU.add))
                    nc.vector.tensor_copy(keys[:], dst[:])
                    nc.vector.memset(acc[:], 0.0)

                @block.scalar
                def _(act):
                    act.wait_ge(low_ready, 1)
                    nc.scalar.activation(tmp[:], tmp[:], ACT.Exp).then_inc(exp_done, 1)

        soft_end()
        layer_norm(nc, shared, x[:], tmp[:], stat)
        store(nc, shared, [(x_dram.rearrange("(w p) f -> p w f", p=P), x[:])])

        c = Names()
        c.iota, c.keys, c.spans = iota, keys, spans[:, 1]
        sum_rows(nc, "mean", c, x_dram, lambda g: src[:, bass.ds(g * T, T)], acc)
        with ExitStack() as st:
            w_top = sb(st, "w_top", [P, D])
            w_bot = sb(st, "w_bot", [P, D])
            w_agg = sb(st, "w_agg", [P, D])
            w_both = sb(st, "w_both", [P, D])
            b_agg = sb(st, "b_agg", [P, 1])
            b_row = sb(st, "b_row", [1, D])
            one_row = sb(st, "one_lane", [1, P])
            gamma = sb(st, "gamma", [P, 2, D])
            loaded1 = sem("loaded1")
            both_done = sem("both_done")
            own_done = sem("mean_own_done")
            with nc.psum_tensor("w_ps", [P, 2, 512], f32) as w_ps, nc.Block() as block:

                @block.sync
                def _(sp):
                    loads = [(w_top[:], a["L1_W"][0:D, :]), (w_bot[:], a["L1_W"][D:2 * D, :]), (w_agg[:], a["L1_aggWT"]),
                             (b_agg[:], a["L1_agg_b"]), (b_row[:], a["L1_b"]),
                             (gamma[:, 0, :], a["L1_gamma"].partition_broadcast(P)), (gamma[:, 1, :], a["L1_beta"].partition_broadcast(P))]
                    for to, of in loads:
                        sp.dma_start(to, of).then_inc(loaded1, 16)
                    sp.wait_ge(loaded1, 16 * 7)

                @block.tensor
                def _(pe):
                    pe.wait_ge(loaded1, 16 * 7)
                    nc.tensor.matmul(w_ps[:, 0, 0:D], w_agg[:], w_bot[:], start=True, stop=True)
                    nc.tensor.matmul(w_ps[0:1, 1, 0:D], b_agg[:], w_bot[:], start=True, stop=True).then_inc(both_done, 1)

                @block.vector
                def _(dve):
                    own = Steps(dve, own_done)
                    own.mark(nc.vector.memset(one_row[:], 1.0))
                    own.do(nc.vector.tensor_scalar(stat[:, 0], acc[:, :, D], 1.0, None, ALU.max))
                    own.do(nc.vector.reciprocal(degree[:], stat[:, 0]))
                    own.do(nc.vector.tensor_tensor(acc[:, :, 0:D], acc[:, :, 0:D], over(degree[:], [P, NW, D], 2), ALU.mult))
                    dve.wait_ge(both_done, 1)
                    nc.vector.tensor_copy(w_both[:], w_ps[:, 0, 0:D])
                    nc.vector.tensor_tensor(b_row[:], b_row[:], w_ps[0:1, 1, 0:D], ALU.add)

            node_products(nc, shared, "agg", ident[:], [lambda w: win(x, w), lambda w: acc[:, bass.ds(w, 1), 0:D].rearrange("p a f -> p (a f)")],
                          [w_top[:], w_both[:]], D,
                          lambda nc, w, ps: nc.scalar.activation(win(tmp, w), ps, ACT.Relu), bias=(one_row[:], b_row[:]))
            layer_norm(nc, shared, tmp[:], acc[:, :, 0:D], stat)
            own_done = sem("mean_end_own")
            with nc.Block() as block:

                @block.vector
                def _(dve):
                    own = Steps(dve, own_done)
                    shape = [P, NW, D]
                    own.do(nc.vector.tensor_tensor(tmp[:], tmp[:], gamma[:, 0, :].unsqueeze(1).to_broadcast(shape), ALU.mult))
                    own.do(nc.vector.tensor_tensor(tmp[:], tmp[:], gamma[:, 1, :].unsqueeze(1).to_broadcast(shape), ALU.add))
                    nc.vector.tensor_tensor(x[:], x[:], tmp[:], ALU.add)
            layer_norm(nc, shared, x[:], tmp[:], stat)
        acc_scope.close()
        L0.close()

        acc_scope = ExitStack()
        acc = sb(acc_scope, "acc2", [P, NW, 2 * D])
        direct = sb(acc_scope, "direct", [P, NW, D])
        node_scale = sb(acc_scope, "node_scale", [P, 2, NW])
        with ExitStack() as st:
            w_y = sb(st, "w_y", [P, 2 * D])
            y = sb(st, "y", [P, NW, D])
            loaded2 = sem("loaded2")
            with nc.Block() as block:

                @block.sync
                def _(sp):
                    sp.dma_start(w_y[:], a["L2_in"]).then_inc(loaded2, 16)
                    sp.dma_start(node_scale[:, 0], a["node_vec"]).then_inc(loaded2, 16)
                    sp.wait_ge(loaded2, 32)

                @block.vector
                def _(dve):
                    own = Steps(dve, sem("scale_own"))
                    dve.wait_ge(loaded2, 32)
                    own.do(nc.vector.tensor_scalar(node_scale[:, 1], node_scale[:, 0], (2 * MUL) ** -0.5, None, ALU.mult))
                    nc.vector.tensor_scalar(node_scale[:, 0], node_scale[:, 0], MUL ** -0.5, None, ALU.mult)
                    nc.vector.memset(acc[:], 0.0)

            def taken(to):
                return lambda nc, w, ps: nc.scalar.activation(win(to, w), ps, ACT.Copy, scale=node_scale[:, 0, bass.ds(w, 1)])

            node_products(nc, shared, "y", ident[:], [lambda w: win(x, w)], [w_y[:, 0:D]], D, taken(y))
            node_products(nc, shared, "direct", ident[:], [lambda w: win(x, w)], [w_y[:, D:2 * D]], D, taken(direct))
            store(nc, shared, [(y_dram.rearrange("(w p) f -> p w f", p=P), y[:])])
        conv_edges(nc, a, iota, spans, keys, src, y_dram, acc)
        with ExitStack() as st:
            w_z = sb(st, "w_z", [P, 2, D + 1])
            conv = sb(st, "conv", [P, NW, D + 1])
            loaded3 = sem("loaded3")
            with nc.Block() as block:

                @block.sync
                def _(sp):
                    sp.dma_start(w_z[:], a["L2_out"].rearrange("(k p) f -> p k f", p=P)).then_inc(loaded3, 16)
                    sp.wait_ge(loaded3, 16)

                @block.vector
                def _(dve):
                    nc.vector.tensor_tensor(acc[:], acc[:], over(degree[:], [P, NW, 2 * D], 2), ALU.mult)

            def half(n):
                return lambda w: acc[:, bass.ds(w, 1), n * D:(n + 1) * D].rearrange("p a f -> p (a f)")

            node_products(nc, shared, "conv", ident[:], [half(0), half(1)], [w_z[:, 0, :], w_z[:, 1, :]], D + 1,
                          lambda nc, w, ps: nc.scalar.activation(win(conv, w), ps, ACT.Copy, scale=node_scale[:, 1, bass.ds(w, 1)]))
            own_done = sem("conv_end_own")
            with nc.Block() as block:

                @block.vector
                def _(dve):
                    own = Steps(dve, own_done)
                    shape = [P, NW, D]
                    own.do(nc.vector.tensor_tensor(x[:], x[:], direct[:], ALU.add))
                    own.do(nc.vector.tensor_tensor(direct[:], conv[:, :, 0:D], conv[:, :, D:D + 1].to_broadcast(shape), ALU.mult))
                    nc.vector.tensor_tensor(x[:], x[:], direct[:], ALU.add)
            layer_norm(nc, shared, x[:], direct[:], stat)
        acc_scope.close()

        acc_scope = ExitStack()
        acc = sb(acc_scope, "acc3", [P, NW, D])
        with ExitStack() as st:
            w_qkv = sb(st, "w_qkv", [P, 3 * D])
            qkv = sb(st, "qkv", [P, NW, 2 * D])
            q = sb(st, "q", [P, NW, D])
            loaded4 = sem("loaded4")
            with nc.Block() as block:

                @block.sync
                def _(sp):
                    sp.dma_start(w_qkv[:], a["L3_wqkv"]).then_inc(loaded4, 16)
                    sp.wait_ge(loaded4, 16)

                @block.vector
                def _(dve):
                    nc.vector.memset(acc[:], 0.0)

            node_products(nc, shared, "q", ident[:], [lambda w: win(x, w)], [w_qkv[:, 0:D]], D,
                          lambda nc, w, ps: nc.scalar.activation(win(q, w), ps, ACT.Copy))
            node_products(nc, shared, "kv", ident[:], [lambda w: win(x, w)], [w_qkv[:, D:3 * D]], 2 * D,
                          lambda nc, w, ps: nc.scalar.activation(win(qkv, w), ps, ACT.Copy))
            store(nc, shared, [(q_dram.rearrange("(w p) f -> p w f", p=P), q[:]),
                              (kv_dram.rearrange("(w p) f -> p w f", p=P), qkv[:])])
        attention_edges(nc, a, iota, spans, keys, src, dst, q_dram, kv_dram, acc)
        with nc.Block() as block:

            @block.vector
            def _(dve):
                nc.vector.tensor_tensor(x[:], x[:], acc[:], ALU.add)
        layer_norm(nc, shared, x[:], acc[:], stat)
        whole = (NW - 1) * P
        store(nc, shared, [(out[0:whole, :].rearrange("(w p) f -> p w f", p=P), x[:, 0:NW - 1, :]),
                          (out[whole:N, :], x[0:N - whole, NW - 1, :])])
        acc_scope.close()


def conv_edges(nc, a, iota, spans, keys, src, y_dram, acc):
    with ExitStack() as st:
        sem = nc.alloc_semaphore

        def sb(name, shape, dt=f32):
            return st.enter_context(nc.sbuf_tensor(f"conv_{name}", shape, dt))

        c = Names()
        c.iota, c.keys, c.spans = iota, keys, spans[:, 1]
        c.hot = sb("hot", [P, T, P])
        span_semaphores(sem, c, "conv")
        rows = sb("rows", [P, S, T, D])
        stage = sb("stage", [P, S, T], i32)
        scalars = sb("scalars", [10, S, GE])
        harm = sb("harm", [P, NT, 4])
        w1 = sb("w1", [10, 100])
        w2 = sb("w2", [100, D])
        hid = sb("hid", [100, 2, GE])
        msg = sb("msg", [P, T, 2 * D])
        ysh = sb("ysh", [P, T, D])
        t01 = sb("t01", [P, T, MUL])
        t11 = sb("t11", [P, T, 3, MUL])
        part_ps = st.enter_context(nc.psum_tensor("conv_part", [P, 512], f32))
        hid_ps = st.enter_context(nc.psum_tensor("conv_hid_ps", [P, 2, GE], f32))
        w_ps = st.enter_context(nc.psum_tensor("conv_w_ps", [P, 2, T, D], f32))
        part = part_ps[:, 0:2 * D]
        loaded = sem("conv_loaded")
        scaled = sem("conv_scaled")
        own_done = sem("conv_own_done")
        staged = sem("conv_staged")
        turn = sem("conv_turn")
        rows_used = sem("conv_rows_used")
        hid_sum = sem("conv_hid_sum")
        hid_done = sem("conv_hid_done")
        w_done = sem("conv_w_done")
        msg_done = sem("conv_msg_done")
        gathered = [nc.alloc_semaphore(f"conv_gathered{s}") for s in range(S)]
        scalars_in = [sem(f"conv_scalars_in{s}") for s in range(S)]

        with nc.Block() as block:

            @block.sync
            def _(sp):
                for to, of in [(w1[:], a["L2_fc1"]), (w2[:], a["L2_fc2"]), (harm[:], a["harm"])]:
                    sp.dma_start(to, of).then_inc(loaded, 16)
                sp.wait_ge(loaded, 48)

            @block.vector
            def _(dve):
                own = Steps(dve, scaled)
                dve.wait_ge(loaded, 48)
                own.do(nc.vector.tensor_scalar(w2[:], w2[:], 0.1, None, ALU.mult))
                nc.vector.tensor_scalar(w2[:, MUL:2 * MUL], w2[:, MUL:2 * MUL], 3 ** -0.5, None, ALU.mult)

        with nc.Block() as block:

            @block.sync
            def _(sp):
                sp.dma_start(scalars[:, 0, :], a["scalars"][:, 0:GE]).then_inc(scalars_in[0], 16)
                with sp.Fori(0, NI) as i:
                    for s in range(S):
                        sp.wait_ge(hid_sum, S * i + (s == S - 1))
                        n = (s + 1) % S
                        sp.dma_start(scalars[:, n, :], a["scalars"][:, bass.ds((S * i + s + 1) * GE, GE)]).then_inc(scalars_in[n], 16)
                sp.wait_ge(scalars_in[0], 16 * (NI + 1))

            @block.scalar
            def _(act):
                def silu(g, n):
                    act.wait_ge(hid_sum, g + 1)
                    nc.scalar.activation(hid[:, n], hid_ps[0:100, n], ACT.Silu, scale=10 ** -0.5).then_inc(hid_done, 1)

                silu(0, 0)
                with act.Fori(0, NI) as i:
                    for s in range(S):
                        act.wait_ge(gathered[s], 16 * T * i)
                        nc.scalar.activation(stage[:, s], src[:, bass.ds((S * i + s) * T, T)], ACT.Copy).then_inc(staged, 1)
                        act.wait_ge(w_done, S * i + s)
                        silu(S * i + s + 1, (s + 1) % 2)

            @block.gpsimd
            def _(pool):
                with pool.Fori(0, NI) as i:
                    for s in range(S):
                        pool.wait_ge(staged, S * i + s + 1)
                        pool.wait_ge(rows_used, S * i + s + 1)
                        pool.sem_inc(turn, 1)
                        for t in range(T):
                            pool.indirect_dma_start(
                                rows[:, s, t, :], None, y_dram,
                                bass.IndirectOffsetOnAxis(ap=stage[:, s, t:t + 1], axis=0)).then_inc(gathered[s], 16)

            @block.tensor
            def _(pe):
                def first(n, slot, count):
                    pe.wait_ge(scalars_in[slot], count)
                    nc.tensor.matmul(hid_ps[0:100, n], w1[:], scalars[:, slot, :], start=True, stop=True).then_inc(hid_sum, 1)

                def second(g, n):
                    pe.wait_ge(hid_done, g + 1)
                    for t in range(T):
                        ins = nc.tensor.matmul(w_ps[:, n, t, :], hid[:, n, t * P:(t + 1) * P], w2[:], start=True, stop=True)
                    ins.then_inc(w_done, 1)

                first(0, 0, 16)
                second(0, 0)
                with pe.Fori(0, NI) as i:
                    for s in range(S):
                        g = S * i + s
                        n = (s + 1) % S
                        pe.wait_ge(hid_done, g)
                        first((s + 1) % 2, n, 16 * (i + 1 + (n == 0)))
                        pe.wait_ge(msg_done, g)
                        second(g + 1, (s + 1) % 2)
                        pe.wait_ge(msg_done, g + 1)
                        tensor_windows(nc, pe, c, g, part, msg)

            @block.vector
            def _(dve):
                dve.sem_inc(rows_used, S)
                with dve.Fori(0, NI) as i:
                    own = Steps(dve, own_done, i * (7 * S))
                    for s in range(S):
                        g = S * i + s
                        hs = harm[:, bass.ds(g * T, T), :]
                        w = w_ps[:, s % 2]
                        dve.wait_ge(gathered[s], 16 * T * (i + 1))
                        own.mark(nc.vector.tensor_tensor(ysh[:], rows[:, s], hs[:, :, 0:1].to_broadcast([P, T, D]), ALU.mult))
                        y0 = rows[:, s, :, 0:MUL]
                        y1 = rows[:, s, :, MUL:D].rearrange("p t (c u) -> p t c u", c=3)
                        sh1 = hs[:, :, 1:4].unsqueeze(3).to_broadcast([P, T, 3, MUL])
                        own.mark(nc.vector.tensor_tensor(t11[:], y1, sh1, ALU.mult))
                        dve.wait_ge(w_done, g + 1)
                        nc.vector.tensor_tensor(t01[:], w[:, :, 2 * MUL:3 * MUL], y0, ALU.mult).then_inc(rows_used, 1)
                        own.wait()
                        dve.wait_ge(rows_used, S + g + 1)
                        own.mark(nc.vector.tensor_tensor(msg[:, :, 0:MUL], w[:, :, 0:MUL], ysh[:, :, 0:MUL], ALU.mult))
                        m10 = msg[:, :, 2 * MUL + 3 * MUL:].rearrange("p t (c u) -> p t c u", c=3)
                        w10 = w[:, :, 3 * MUL:].unsqueeze(2).to_broadcast([P, T, 3, MUL])
                        own.mark(nc.vector.tensor_tensor(m10, w10, ysh[:, :, MUL:].rearrange("p t (c u) -> p t c u", c=3), ALU.mult))
                        m01 = msg[:, :, 2 * MUL:5 * MUL].rearrange("p t (c u) -> p t c u", c=3)
                        own.mark(nc.vector.tensor_tensor(m01, t01[:].unsqueeze(2).to_broadcast([P, T, 3, MUL]), sh1, ALU.mult))
                        own.do(nc.vector.tensor_tensor(t11[:, :, 0], t11[:, :, 0], t11[:, :, 1], ALU.add))
                        own.do(nc.vector.tensor_tensor(t11[:, :, 0], t11[:, :, 0], t11[:, :, 2], ALU.add))
                        nc.vector.tensor_tensor(msg[:, :, MUL:2 * MUL], w[:, :, MUL:2 * MUL], t11[:, :, 0], ALU.mult).then_inc(msg_done, 1)
                        vector_windows(nc, dve, c, g, acc, part)


def attention_edges(nc, a, iota, spans, keys, src, dst, q_dram, kv_dram, acc):
    NC = HID // P
    with ExitStack() as st:
        sem = nc.alloc_semaphore

        sem = nc.alloc_semaphore

        def sb(name, shape, dt=f32):
            return st.enter_context(nc.sbuf_tensor(f"att_{name}", shape, dt))

        c = Names()
        c.iota, c.keys, c.spans = iota, keys, spans[:, 1]
        c.hot = sb("hot", [P, T, P])
        span_semaphores(sem, c, "att")
        q_rows = sb("q_rows", [P, S, T, D])
        kv_rows = sb("kv_rows", [P, S, T, 2 * D])
        stage = sb("stage", [P, S, 2, T], i32)
        rad = sb("rad", [64, S, GE])
        sph = sb("sph", [32, S, GE])
        cut = sb("cut", [P, NT])
        rad_w0 = sb("rad_w0", [64, HID])
        sph_w0 = sb("sph_w0", [32, HID])
        w1 = sb("w1", [P, 2 * NC, D])
        b0 = sb("b0", [P, 2 * NC])
        b1 = sb("b1", [P, 2, D])
        hid = sb("hid", [P, 2 * NC, GE])
        qw = sb("qw", [P, T, D])
        alpha = sb("alpha", [P, T, HEADS])
        msg = sb("msg", [P, T, D])
        part_ps = st.enter_context(nc.psum_tensor("att_part", [P, 512], f32))
        hid_ps = st.enter_context(nc.psum_tensor("att_hid_ps", [P, 2 * NC, GE], f32))
        w_ps = st.enter_context(nc.psum_tensor("att_w_ps", [P, 2, T, D], f32))
        part = part_ps[:, 0:D]
        loaded = sem("att_loaded")
        scaled = sem("att_scaled")
        own_done = sem("att_own_done")
        staged = sem("att_staged")
        turn = sem("att_turn")
        rows_used = sem("att_rows_used")
        hid_sum = sem("att_hid_sum")
        hid_done = sem("att_hid_done")
        w_done = sem("att_w_done")
        msg_done = sem("att_msg_done")
        gathered = [nc.alloc_semaphore(f"att_gathered{s}") for s in range(S)]
        feats_in = [sem(f"att_feats_in{s}") for s in range(S)]

        with nc.Block() as block:

            @block.sync
            def _(sp):
                loads = [(rad_w0[:], a["rad_w0"]), (sph_w0[:], a["sph_w0"]), (cut[:], a["cut"]), (b0[:], a["b0"]),
                         (w1[:, 0:NC], a["rad_w1"].rearrange("(k p) f -> p k f", p=P)),
                         (w1[:, NC:], a["sph_w1"].rearrange("(k p) f -> p k f", p=P)),
                         (b1[:, 0, :], a["rad_b1"].partition_broadcast(P)), (b1[:, 1, :], a["sph_b1"].partition_broadcast(P))]
                for to, of in loads:
                    sp.dma_start(to, of).then_inc(loaded, 16)
                sp.wait_ge(loaded, 16 * 8)

            @block.vector
            def _(dve):
                own = Steps(dve, scaled)
                dve.wait_ge(loaded, 16 * 8)
                nc.vector.tensor_tensor(b1[:, 0], b1[:, 0], b1[:, 1], ALU.add)
                nc.vector.tensor_scalar(cut[:], cut[:], 1.0 / 64.0, None, ALU.mult)

        with nc.Block() as block:

            @block.sync
            def _(sp):
                def load(n, g):
                    sp.dma_start(rad[:, n, :], a["rad"][:, bass.ds(g * GE, GE)]).then_inc(feats_in[n], 16)
                    sp.dma_start(sph[:, n, :], a["sph"][:, bass.ds(g * GE, GE)]).then_inc(feats_in[n], 16)

                load(0, 0)
                with sp.Fori(0, NI) as i:
                    for s in range(S):
                        sp.wait_ge(hid_sum, 2 * NC * (S * i + (s == S - 1)))
                        load((s + 1) % S, S * i + s + 1)
                sp.wait_ge(feats_in[0], 32 * (NI + 1))

            @block.scalar
            def _(act):
                def silu(g):
                    for n in range(2 * NC):
                        act.wait_ge(hid_sum, 2 * NC * g + n + 1)
                        nc.scalar.activation(hid[:, n], hid_ps[:, n], ACT.Silu, bias=b0[:, n:n + 1]).then_inc(hid_done, 1)

                silu(0)
                with act.Fori(0, NI) as i:
                    for s in range(S):
                        act.wait_ge(gathered[s], 32 * T * i)
                        nc.scalar.activation(stage[:, s, 0], src[:, bass.ds((S * i + s) * T, T)], ACT.Copy)
                        nc.scalar.activation(stage[:, s, 1], dst[:, bass.ds((S * i + s) * T, T)], ACT.Copy).then_inc(staged, 1)
                        act.wait_ge(w_done, S * i + s + 1)
                        silu(S * i + s + 1)

            @block.gpsimd
            def _(pool):
                with pool.Fori(0, NI) as i:
                    for s in range(S):
                        pool.wait_ge(staged, S * i + s + 1)
                        pool.wait_ge(rows_used, S * i + s + 1)
                        pool.sem_inc(turn, 1)
                        for t in range(T):
                            pool.indirect_dma_start(
                                kv_rows[:, s, t, :], None, kv_dram,
                                bass.IndirectOffsetOnAxis(ap=stage[:, s, 0, t:t + 1], axis=0)).then_inc(gathered[s], 16)
                            pool.indirect_dma_start(
                                q_rows[:, s, t, :], None, q_dram,
                                bass.IndirectOffsetOnAxis(ap=stage[:, s, 1, t:t + 1], axis=0)).then_inc(gathered[s], 16)

            @block.tensor
            def _(pe):
                def first(g, slot, count):
                    pe.wait_ge(feats_in[slot], count)
                    for n in range(2 * NC):
                        pe.wait_ge(hid_done, 2 * NC * g + n + 1)
                        if n < NC:
                            ins = nc.tensor.matmul(hid_ps[:, n], rad_w0[:, n * P:(n + 1) * P], rad[:, slot, :], start=True, stop=True)
                        else:
                            ins = nc.tensor.matmul(hid_ps[:, n], sph_w0[:, (n - NC) * P:(n - NC + 1) * P], sph[:, slot, :], start=True, stop=True)
                        ins.then_inc(hid_sum, 1)

                def second(g, half):
                    pe.wait_ge(hid_done, 2 * NC * g)
                    for t in range(T):
                        for n in range(2 * NC):
                            ins = nc.tensor.matmul(w_ps[:, half, t, :], hid[:, n, t * P:(t + 1) * P], w1[:, n, :],
                                                   start=n == 0, stop=n == 2 * NC - 1)
                    ins.then_inc(w_done, 1)

                pe.sem_inc(hid_done, 2 * NC)
                first(0, 0, 32)
                second(2, 0)
                with pe.Fori(0, NI) as i:
                    for s in range(S):
                        g = S * i + s
                        n = (s + 1) % S
                        first(g + 1, n, 32 * (i + 1 + (n == 0)))
                        pe.wait_ge(msg_done, g)
                        second(g + 3, (s + 1) % 2)
                        pe.wait_ge(msg_done, g + 1)
                        tensor_windows(nc, pe, c, g, part, msg)

            @block.vector
            def _(dve):
                dve.sem_inc(rows_used, S)
                with dve.Fori(0, NI) as i:
                    own = Steps(dve, own_done, i * (5 * S))
                    for s in range(S):
                        g = S * i + s
                        shape = [P, T, D]
                        dve.wait_ge(w_done, g + 1)
                        own.do(nc.vector.tensor_tensor(qw[:], w_ps[:, s % 2], b1[:, 0].unsqueeze(1).to_broadcast(shape), ALU.add))
                        dve.wait_ge(gathered[s], 32 * T * (i + 1))
                        own.do(nc.vector.tensor_tensor(qw[:], qw[:], q_rows[:, s], ALU.mult))
                        own.do(nc.vector.tensor_tensor(qw[:], qw[:], kv_rows[:, s, :, 0:D], ALU.mult))
                        own.do(nc.vector.tensor_reduce(alpha[:], qw[:].rearrange("p t (h d) -> p t h d", h=HEADS), AX.X, ALU.add))
                        own.do(nc.vector.tensor_tensor(alpha[:], alpha[:], over(cut[:, bass.ds(g * T, T)], [P, T, HEADS], 2), ALU.mult))
                        v = kv_rows[:, s, :, D:].rearrange("p t (h d) -> p t h d", h=HEADS)
                        nc.vector.tensor_tensor(msg[:].rearrange("p t (h d) -> p t h d", h=HEADS), v,
                                                over(alpha[:], [P, T, HEADS, HD], 3), ALU.mult).then_inc(msg_done, 1)
                        vector_windows(nc, dve, c, g, acc, part)
                        dve.sem_inc(rows_used, 1)


def laid_out(inputs):
    z = {k: np.asarray(v) for k, v in inputs.items()}

    def edges(v):
        p = np.full((EP,), PAD, v.dtype)
        p[:E] = v
        return p

    def tiles(v):
        return np.ascontiguousarray(v.reshape(NT, P, -1).transpose(1, 0, 2))

    def zeros_after(v, n):
        p = np.zeros((n,) + v.shape[1:], v.dtype)
        p[:v.shape[0]] = v
        return p

    src, dst = edges(z["src"]), edges(z["dst"])
    x = zeros_after(z["x"], NP)
    o = {"x": x.reshape(NW, P, D).transpose(1, 0, 2), "xT": np.ascontiguousarray(x.T), "edges": np.stack([src, dst]),
         "src_tiles": tiles(src)[:, :, 0], "dst_tiles": tiles(dst)[:, :, 0]}
    o["L0_W"] = z["L0_gnn_W"]
    o["L0_WT"] = z["L0_gnn_W"].T
    o["L0_a"] = z["L0_gnn_a"].reshape(2, D).T
    o["L1_W"] = z["L1_gnn_W"]
    o["L1_aggWT"] = z["L1_gnn_agg_W"].T
    o["L1_agg_b"] = z["L1_gnn_agg_b"].reshape(D, 1)
    o["L1_b"] = z["L1_gnn_b"].reshape(1, D)
    o["L1_gamma"] = z["L1_gnn_gamma"]
    o["L1_beta"] = z["L1_gnn_beta"]
    o["node_vec"] = zeros_after(z["node_vec1"], NP).reshape(NW, P).T
    w_in = np.zeros((D, 2 * D), np.float32)
    w_in[:MUL, :MUL] = z["L2_gnn_W_l1_0"]
    w_in[:MUL, D:D + MUL] = z["L2_gnn_W_sc0"]
    w_out = np.zeros((2 * D, D + 1), np.float32)
    w_out[:2 * MUL, :MUL] = z["L2_gnn_W_l2_0"]
    w_out[:2 * MUL, D] = z["L2_gnn_W_alpha"][:, 0]
    for c in range(3):
        w_in[MUL + c:D:3, MUL + c * MUL:MUL + (c + 1) * MUL] = z["L2_gnn_W_l1_1"]
        w_in[MUL + c:D:3, D + MUL + c:2 * D:3] = z["L2_gnn_W_sc1"]
        at = 2 * MUL + c * MUL
        w_out[at:at + MUL, MUL + c:D:3] = z["L2_gnn_W_l2_1"][:MUL]
        w_out[at + 3 * MUL:at + 4 * MUL, MUL + c:D:3] = z["L2_gnn_W_l2_1"][MUL:]
    o["L2_in"], o["L2_out"] = w_in, w_out
    o["L2_fc1"], o["L2_fc2"] = z["L2_gnn_W_fc1"], z["L2_gnn_W_fc2"]
    o["harm"] = tiles(zeros_after(z["edge_attr_4"], EP))
    o["scalars"] = zeros_after(z["edge_attr_10"], EA).T
    o["L3_wqkv"] = np.concatenate([z["L3_gnn_wq"], z["L3_gnn_wk"], z["L3_gnn_wv"]], axis=1)
    o["rad"] = zeros_after(z["edge_attr_64"], EA).T
    o["sph"] = zeros_after(z["edge_attr_32"], EA).T
    o["cut"] = tiles(zeros_after(z["edge_weight"], EP))[:, :, 0]
    o["rad_w0"], o["sph_w0"] = z["L3_gnn_rad_w0"], z["L3_gnn_sph_w0"]
    o["rad_w1"], o["sph_w1"] = z["L3_gnn_rad_w1"], z["L3_gnn_sph_w1"]
    o["b0"] = np.concatenate([z["L3_gnn_rad_b0"].reshape(HID // P, P), z["L3_gnn_sph_b0"].reshape(HID // P, P)]).T
    o["rad_b1"], o["sph_b1"] = z["L3_gnn_rad_b1"], z["L3_gnn_sph_b1"]
    return {k: np.ascontiguousarray(v) for k, v in o.items()}


def kernel(**inputs):
    import concourse.bacc as bacc
    from concourse.bass_utils import run_bass_kernel_spmd

    nc = bacc.Bacc("TRN2", target_bir_lowering=False, num_devices=1)
    arrays = {f"in_{k}": v for k, v in laid_out(inputs).items()}
    aps = {k[3:]: nc.dram_tensor(k, v.shape, mybir.dt.from_np(v.dtype), kind="ExternalInput").ap() for k, v in arrays.items()}
    out = nc.dram_tensor("out_x", (N, D), f32, kind="ExternalOutput").ap()
    gnn_kernel(nc, aps, out)
    got = run_bass_kernel_spmd(nc, [arrays], core_ids=[0])
    return got.results[0]["out_x"]
```

```python
from contextlib import ExitStack

import concourse.bass as bass
import numpy as np
from concourse import mybir

f32 = mybir.dt.float32
bf16 = mybir.dt.bfloat16
i32 = mybir.dt.int32
i16 = mybir.dt.int16
ALU = mybir.AluOpType
ACT = mybir.ActivationFunctionType
AX = mybir.AxisListType

P = 128
N = 6250
E = 206250
D = 128
NW = -(-N // P)
NP = NW * P
PAD = NP - 1
T = 4
GE = T * P
S = 4
NI = -(-E // (S * GE))
NG = NI * S
NT = NG * T
EP = NT * P
EA = EP + S * GE
R = 7
NB = NW // R
MUL = 32
HEADS, HD = 8, 16
HID = 256
LN_EPS = 1e-5
SOFT_EPS = 1e-10


class Names:
    pass


class Steps:

    def __init__(self, eng, sem, base=0):
        self.eng, self.sem, self.base, self.n = eng, sem, base, 0

    def mark(self, ins):
        self.n += 1
        ins.then_inc(self.sem, 1)

    def wait(self):
        self.eng.wait_ge(self.sem, self.base + self.n)

    def do(self, ins):
        self.mark(ins)
        self.wait()


def over(ap, shape, axis):
    return ap.unsqueeze(axis).to_broadcast(shape)


def win(ap, w):
    return ap[:, bass.ds(w, 1), :].rearrange("p a f -> p (a f)")


def node_products(nc, c, name, ident, sources, weights, width, evacuate, bias=None):
    ns = len(sources)
    with ExitStack() as st:
        staged = st.enter_context(nc.sbuf_tensor(f"{name}_staged", [P, R, ns, P], f32))
        turned = st.enter_context(nc.sbuf_tensor(f"{name}_turned", [P, R, ns, P], f32))
        bank = st.enter_context(nc.psum_tensor(f"{name}_bank", [P, R, 4 * P], f32))
        stage_done, turn_done, copy_done, product_done, out_done = c.ring
        used = NW * c.ring_uses
        c.ring_uses += 1

        with nc.Block() as block:

            @block.vector
            def _(dve):
                with dve.Fori(0, NB) as i:
                    for j in range(R):
                        dve.wait_ge(turn_done, used + R * i + j + 1)
                        for n, source in enumerate(sources):
                            ins = nc.vector.tensor_copy(staged[:, j, n, :], source(R * i + j))
                        ins.then_inc(stage_done, 1)

            @block.tensor
            def _(pe):
                if used == 0:
                    pe.sem_inc(turn_done, R)
                if used == 0:
                    pe.sem_inc(product_done, R)
                with pe.Fori(0, NB) as i:
                    for j in range(R):
                        pe.wait_ge(stage_done, used + R * i + j + 1)
                        pe.wait_ge(out_done, used + R * i + j + 1)
                        for n in range(ns):
                            ins = nc.tensor.transpose(bank[:, j, n * P:(n + 1) * P], staged[:, j, n, :], ident)
                        ins.then_inc(turn_done, 1)
                    for j in range(R):
                        pe.wait_ge(copy_done, used + R + R * i + j + 1)
                        out = bank[:, j, 2 * P:2 * P + width]
                        for n in range(ns):
                            ins = nc.tensor.matmul(out, turned[:, j, n, :], weights[n], start=n == 0,
                                                   stop=bias is None and n == ns - 1)
                        if bias is not None:
                            ins = nc.tensor.matmul(out, bias[0], bias[1], start=False, stop=True)
                        ins.then_inc(product_done, 1)

            @block.scalar
            def _(act):
                if used == 0:
                    act.sem_inc(copy_done, R)
                if used == 0:
                    act.sem_inc(out_done, R)
                with act.Fori(0, NB) as i:
                    for j in range(R):
                        act.wait_ge(turn_done, used + R + R * i + j + 1)
                        act.wait_ge(product_done, used + R * i + j + 1)
                        nc.scalar.activation(turned[:, j].rearrange("p n f -> p (n f)"), bank[:, j, 0:ns * P], ACT.Copy).then_inc(copy_done, 1)
                    for j in range(R):
                        act.wait_ge(product_done, used + R + R * i + j + 1)
                        evacuate(nc, R * i + j, bank[:, j, 2 * P:2 * P + width]).then_inc(out_done, 1)


def layer_norm(nc, c, x, tmp, stat):
    shape = [P, NW, D]
    steps_done, var_ready, std_ready = c.norm
    used = c.norm_uses
    c.norm_uses += 1
    with nc.Block() as block:

        @block.vector
        def _(dve):
            own = Steps(dve, steps_done, 6 * used)
            own.do(nc.vector.tensor_reduce(stat[:, 0], x, AX.X, ALU.add))
            own.do(nc.vector.tensor_scalar(stat[:, 0], stat[:, 0], 1.0 / D, None, ALU.mult))
            own.do(nc.vector.tensor_tensor(x, x, over(stat[:, 0], shape, 2), ALU.subtract))
            own.do(nc.vector.tensor_tensor(tmp, x, x, ALU.mult))
            own.do(nc.vector.tensor_reduce(stat[:, 1], tmp, AX.X, ALU.add))
            nc.vector.tensor_scalar(stat[:, 1], stat[:, 1], 1.0 / D, LN_EPS, ALU.mult, ALU.add).then_inc(var_ready, 1)
            dve.wait_ge(std_ready, used + 1)
            own.do(nc.vector.reciprocal(stat[:, 1], stat[:, 0]))
            nc.vector.tensor_tensor(x, x, over(stat[:, 1], shape, 2), ALU.mult)

        @block.scalar
        def _(act):
            act.wait_ge(var_ready, used + 1)
            nc.scalar.activation(stat[:, 0], stat[:, 1], ACT.Sqrt).then_inc(std_ready, 1)


def store(nc, c, pairs):
    c.stores += len(pairs)
    with nc.Block() as block:

        @block.sync
        def _(sp):
            for dst, src in pairs:
                sp.dma_start(dst, src).then_inc(c.landed, 16)
            sp.wait_ge(c.landed, 16 * c.stores)


class Body:

    def __init__(self, eng, spans, i):
        self.word = eng.value_load(spans.bodies[:, bass.ds(i, 1)], min_val=0, max_val=2 ** 31 - 1)
        self.any_more = eng.snap(self.word >> (6 * (S + 1)))
        self.firsts, self.eng = {}, eng

    def first(self, s):
        if s not in self.firsts:
            self.firsts[s] = self.eng.snap((self.word >> (6 * (s + 1))) & 63)
        return self.firsts[s]


def load_more(eng, spans, g):
    v = eng.value_load(spans.groups[:, bass.ds(g, 1)], min_val=0, max_val=2 ** 31 - 1)
    return eng.snap(v & 63), eng.snap(v >> 6)


def window_of(nc, first, j):
    return nc.s_assert_within(first + j, 0, NW - 1, skip_runtime_bounds_check_because="spans hold windows of real nodes")


class Sums:

    def __init__(self, nc, st, name, iota, keys, spans, acc, width, weight=None):
        self.iota, self.keys, self.spans, self.acc, self.weight = iota, keys, spans, acc, weight
        sem = nc.alloc_semaphore
        self.hot = st.enter_context(nc.sbuf_tensor(f"{name}_hot", [P, 2, T, P], f32))
        self.hot_x = st.enter_context(nc.sbuf_tensor(f"{name}_hot_x", [P, T, P], f32))
        part = st.enter_context(nc.psum_tensor(f"{name}_part", [P, 3, 512], f32))
        self.part, self.part_x = part[:, 0:2, 0:width], part[:, 2, 0:width]
        self.equal_done = sem(f"{name}_equal_done")
        self.hot_done = sem(f"{name}_hot_done")
        self.sums_done = sem(f"{name}_sums_done")
        self.added = sem(f"{name}_added")
        self.equal_done_x = sem(f"{name}_equal_done_x")
        self.hot_done_x = sem(f"{name}_hot_done_x")
        self.sums_done_x = sem(f"{name}_sums_done_x")
        self.added_x = sem(f"{name}_added_x")


def one_hot(nc, dve, c, hot, g, w, equal_done, count, hot_done):
    key = over(c.keys[:, bass.ds(g * T, T)], [P, T, P], 2)
    nodes = c.iota[:, bass.ds(w * P, P)].unsqueeze(1).to_broadcast([P, T, P])
    if c.weight is None:
        nc.vector.tensor_tensor(hot, nodes, key, ALU.is_equal).then_inc(hot_done, 1)
    else:
        nc.vector.tensor_tensor(hot, nodes, key, ALU.is_equal).then_inc(equal_done, 1)
        dve.wait_ge(equal_done, count)
        weight = over(c.weight[:, bass.ds(g * T, T)], [P, T, P], 2)
        nc.vector.tensor_tensor(hot, hot, weight, ALU.mult).then_inc(hot_done, 1)


def vector_hot(nc, dve, c, body, s, g):
    w = window_of(nc, body.first(s), 0)
    dve.wait_ge(c.sums_done, g + 1)
    one_hot(nc, dve, c, c.hot[:, s % 2], g, w, c.equal_done, g + 1, c.hot_done)


def vector_add(nc, dve, c, body, s, g):
    w = window_of(nc, body.first(s), 0)
    dve.wait_ge(c.sums_done, 2 + g + 1)
    dve.wait_ge(c.added, 2 + g)
    nc.vector.tensor_tensor(win(c.acc, w), win(c.acc, w), c.part[:, s % 2], ALU.add).then_inc(c.added, 1)
    with dve.If(body.any_more > 0):
        more, before = load_more(dve, c.spans, g)
        with dve.If(more > 0):
            with dve.Fori(0, more) as j:
                w = window_of(nc, body.first(s), 1 + j)
                k = dve.snap(before + j)
                dve.wait_ge(c.sums_done_x, k + 1)
                one_hot(nc, dve, c, c.hot_x[:], g, w, c.equal_done_x, k + 1, c.hot_done_x)
                dve.wait_ge(c.sums_done_x, 1 + k + 1)
                dve.wait_ge(c.added, 2 + g + 1)
                nc.vector.tensor_tensor(win(c.acc, w), win(c.acc, w), c.part_x, ALU.add).then_inc(c.added_x, 1)
                dve.wait_ge(c.added_x, 1 + k + 1)


def tensor_sums(nc, pe, c, body, s, g, rows):
    pe.wait_ge(c.hot_done, g + 1)
    pe.wait_ge(c.added, g + 1)
    for t in range(T):
        ins = nc.tensor.matmul(c.part[:, s % 2], c.hot[:, s % 2, t, :], rows[:, t, :], start=t == 0, stop=t == T - 1)
    ins.then_inc(c.sums_done, 1)
    with pe.If(body.any_more > 0):
        more, before = load_more(pe, c.spans, g)
        with pe.If(more > 0):
            with pe.Fori(0, more) as j:
                k = pe.snap(before + j)
                pe.wait_ge(c.hot_done_x, k + 1)
                pe.wait_ge(c.added_x, k + 1)
                for t in range(T):
                    ins = nc.tensor.matmul(c.part_x, c.hot_x[:, t, :], rows[:, t, :], start=t == 0, stop=t == T - 1)
                ins.then_inc(c.sums_done_x, 1)


def vector_sums_start(dve, c):
    dve.sem_inc(c.added, 2)
    dve.sem_inc(c.added_x, 1)


def tensor_sums_start(pe, c):
    pe.sem_inc(c.sums_done, 2)
    pe.sem_inc(c.sums_done_x, 1)


class EdgeMlp:

    NC = HID // P

    def __init__(self, nc, st, a, w_dram):
        def sb(name, shape, dt=f32):
            return st.enter_context(nc.sbuf_tensor(f"mlp_{name}", shape, dt))

        sem = nc.alloc_semaphore
        self.a, self.w_dram, NC = a, w_dram, self.NC
        self.rad = sb("rad", [64, GE])
        self.sph = sb("sph", [32, GE])
        self.rad_w0 = sb("rad_w0", [64, HID])
        self.sph_w0 = sb("sph_w0", [32, HID])
        self.w1 = sb("w1", [P, 2 * NC, D])
        self.b0 = sb("b0", [P, 2 * NC])
        self.b1 = sb("b1", [P, 2, D])
        self.hid = sb("hid", [P, 2 * NC, GE])
        self.w = sb("w", [P, T, D])
        self.loaded = sem("mlp_loaded")
        self.feats_in = sem("mlp_feats_in")
        self.hid_sum = sem("mlp_hid_sum")
        self.hid_done = sem("mlp_hid_done")
        self.w_sum = sem("mlp_w_sum")
        self.w_taken = sem("mlp_w_taken")
        self.w_stored = sem("mlp_w_stored")
        self.w_free = sem("mlp_w_free")

        loads = [(self.rad_w0[:], a["rad_w0"]), (self.sph_w0[:], a["sph_w0"]), (self.b0[:], a["b0"]),
                 (self.w1[:, 0:NC], a["rad_w1"].rearrange("(k p) f -> p k f", p=P)),
                 (self.w1[:, NC:], a["sph_w1"].rearrange("(k p) f -> p k f", p=P)),
                 (self.b1[:, 0, :], a["rad_b1"].partition_broadcast(P)),
                 (self.b1[:, 1, :], a["sph_b1"].partition_broadcast(P))]
        with nc.Block() as block:

            @block.sync
            def _(sp):
                for to, of in loads:
                    sp.dma_start(to, of).then_inc(self.loaded, 16)
                self.load(sp, 0)
                sp.wait_ge(self.loaded, 16 * len(loads))
                sp.sem_inc(self.w_free, 1)

            @block.tensor
            def _(pe):
                pe.sem_inc(self.hid_sum, 1)
                pe.sem_inc(self.w_sum, 1)

            @block.scalar
            def _(act):
                act.sem_inc(self.hid_done, 2)

            @block.vector
            def _(dve):
                dve.wait_ge(self.loaded, 16 * len(loads))
                dve.sem_inc(self.w_taken, 1)
                nc.vector.tensor_tensor(self.b1[:, 0], self.b1[:, 0], self.b1[:, 1], ALU.add)

    def psum(self, nc, st, name):
        bank = st.enter_context(nc.psum_tensor(f"{name}_mlp", [P, 3, GE], f32))
        self.hid_ps, self.w_ps = bank[:, 0:2], bank[:, 2]

    def load(self, sp, u):
        sp.dma_start(self.rad[:], self.a["rad"][:, bass.ds(u * GE, GE)]).then_inc(self.feats_in, 16)
        sp.dma_start(self.sph[:], self.a["sph"][:, bass.ds(u * GE, GE)]).then_inc(self.feats_in, 16)

    def sync(self, sp, u):
        sp.wait_ge(self.hid_sum, 1 + 2 * self.NC * (u + 1))
        self.load(sp, u + 1)
        sp.wait_ge(self.w_taken, 1 + u + 1)
        sp.dma_start(self.w_dram[:, bass.ds(u * T * D, T * D)], self.w[:].rearrange("p t f -> p (t f)")).then_inc(self.w_stored, 16)
        sp.wait_ge(self.w_stored, 16 * (u + 1))
        sp.sem_inc(self.w_free, 1)

    def tensor_first(self, nc, pe, u, chunks):
        pe.wait_ge(self.feats_in, 32 * (u + 1))
        for n in chunks:
            pe.wait_ge(self.hid_done, 2 * self.NC * u + n + 1)
            w, of = (self.rad_w0, self.rad) if n < self.NC else (self.sph_w0, self.sph)
            m = n % self.NC
            nc.tensor.matmul(self.hid_ps[:, n % 2], w[:, m * P:(m + 1) * P], of[:], start=True, stop=True).then_inc(self.hid_sum, 1)

    def tensor_second(self, nc, pe, u, tiles):
        if 0 in tiles:
            pe.wait_ge(self.hid_done, 2 + 2 * self.NC * (u + 1))
            pe.wait_ge(self.w_taken, u + 1)
        for t in tiles:
            for n in range(2 * self.NC):
                ins = nc.tensor.matmul(self.w_ps[:, t * D:(t + 1) * D], self.hid[:, n, t * P:(t + 1) * P], self.w1[:, n, :],
                                       start=n == 0, stop=n == 2 * self.NC - 1)
        if T - 1 in tiles:
            ins.then_inc(self.w_sum, 1)

    def scalar(self, nc, act, u, chunks):
        if 0 in chunks:
            act.wait_ge(self.w_sum, u + 1)
        for n in chunks:
            act.wait_ge(self.hid_sum, 1 + 2 * self.NC * u + n + 1)
            nc.scalar.activation(self.hid[:, n], self.hid_ps[:, n % 2], ACT.Silu, bias=self.b0[:, n:n + 1]).then_inc(self.hid_done, 1)

    def vector(self, nc, dve, u):
        dve.wait_ge(self.w_sum, 1 + u + 1)
        dve.wait_ge(self.w_free, u + 1)
        nc.vector.tensor_tensor(self.w[:], self.w_ps.rearrange("p (t f) -> p t f", t=T),
                                self.b1[:, 0].unsqueeze(1).to_broadcast([P, T, D]), ALU.add).then_inc(self.w_taken, 1)


def sum_rows(nc, name, iota, keys, spans, table, indices, acc, mlp, unit, weight=None):
    with ExitStack() as st:
        def sb(n, shape, dt=f32):
            return st.enter_context(nc.sbuf_tensor(f"{name}_{n}", shape, dt))

        sem = nc.alloc_semaphore
        c = Sums(nc, st, name, iota, keys, spans, acc, D + 1, weight)
        mlp.psum(nc, st, name)
        rows = sb("rows", [P, S, T, D + 1])
        stage = sb("stage", [P, S, T], i32)
        ones_set = sem(f"{name}_ones_set")
        staged = sem(f"{name}_staged")
        rows_used = sem(f"{name}_rows_used")
        turn = sem(f"{name}_turn")
        gathered = [sem(f"{name}_gathered{s}") for s in range(S)]

        with nc.Block() as block:

            @block.sync
            def _(sp):
                with sp.Fori(0, NI) as i:
                    mlp.sync(sp, unit + i)

            @block.scalar
            def _(act):
                def body(i, last):
                    for s in range(S):
                        if s in (0, 1):
                            mlp.scalar(nc, act, unit + i, range(2 * s, 2 * s + 2))
                        if not last:
                            act.wait_ge(gathered[s], 16 * T * (i + 1))
                            nc.scalar.copy(stage[:, s], indices(S * (i + 1) + s)).then_inc(staged, 1)

                for s in range(S):
                    nc.scalar.copy(stage[:, s], indices(s)).then_inc(staged, 1)
                with act.Fori(0, NI - 1) as i:
                    body(i, False)
                body(NI - 1, True)

            @block.gpsimd
            def _(pool):
                with pool.Fori(0, NI) as i:
                    for s in range(S):
                        pool.wait_ge(staged, S * i + s + 1)
                        pool.wait_ge(rows_used, S * i + s + 1)
                        pool.sem_inc(turn, 1)
                        for t in range(T):
                            pool.indirect_dma_start(
                                rows[:, s, t, 0:D], None, table,
                                bass.IndirectOffsetOnAxis(ap=stage[:, s, t:t + 1], axis=0)).then_inc(gathered[s], 16)

            @block.vector
            def _(dve):
                nc.vector.memset(rows[:, :, :, D:D + 1], 1.0).then_inc(ones_set, 1)
                dve.sem_inc(rows_used, S)
                vector_sums_start(dve, c)

                def take(body, s, g):
                    vector_add(nc, dve, c, body, s, g)
                    dve.sem_inc(rows_used, 1)

                def one_body(i, first):
                    body = Body(dve, spans, i)
                    for s in range(S):
                        vector_hot(nc, dve, c, body, s, S * i + s)
                        if s > 0 or not first:
                            take(body, s - 1, S * i + s - 1)
                        if s == 0 and not first:
                            mlp.vector(nc, dve, unit + i - 1)
                    return body

                one_body(0, True)
                with dve.Fori(1, NI) as i:
                    one_body(i, False)
                take(Body(dve, spans, NI - 1), S - 1, NG - 1)
                mlp.vector(nc, dve, unit + NI - 1)

            @block.tensor
            def _(pe):
                pe.wait_ge(ones_set, 1)
                tensor_sums_start(pe, c)
                with pe.Fori(0, NI) as i:
                    body = Body(pe, spans, i)
                    for s in range(S):
                        pe.wait_ge(gathered[s], 16 * T * (i + 1))
                        tensor_sums(nc, pe, c, body, s, S * i + s, rows[:, s])
                        if s == 0:
                            mlp.tensor_first(nc, pe, unit + i, range(0, 2))
                        elif s == 1:
                            mlp.tensor_first(nc, pe, unit + i, range(2, 4))
                        elif s == 2:
                            mlp.tensor_second(nc, pe, unit + i, range(0, 2))
                        else:
                            mlp.tensor_second(nc, pe, unit + i, range(2, 4))


def gnn_kernel(nc, a, out):
    top = ExitStack()

    def dram(name, shape, dt=f32):
        return nc.dram_tensor(name, shape, dt).ap()

    def sb(st, name, shape, dt=f32):
        return st.enter_context(nc.sbuf_tensor(name, shape, dt))

    sem = nc.alloc_semaphore
    shared = Names()
    shared.ring = [sem(n) for n in ("stage_done", "turn_done", "copy_done", "product_done", "out_done")]
    shared.norm = [sem(n) for n in ("norm_steps_done", "var_ready", "std_ready")]
    shared.landed = sem("landed")
    shared.ring_uses = shared.norm_uses = shared.stores = 0
    lo_dram = dram("lo_dram", [2, EP], bf16)
    sorted_dram = dram("sorted_dram", [EP, 4], i32)
    wh_dram = dram("wh_dram", [NP, D])
    x_dram = dram("x_dram", [NP, D])
    y_dram = dram("y_dram", [NP, D])
    q_dram = dram("q_dram", [NP, D])
    kv_dram = dram("kv_dram", [NP, 2 * D])
    w_dram = dram("w_dram", [P, EP // P * D])

    with top:
        iota = sb(top, "iota", [P, NP])
        own_lane = sb(top, "own_lane", [P, 1])
        ident = sb(top, "ident", [P, P])
        x = sb(top, "x", [P, NW, D])
        src = sb(top, "src", [P, NT], i32)
        spans = []
        for n in range(2):
            spans.append(Names())
            spans[n].bodies = sb(top, f"bodies{n}", [1, NI], i32)[:]
            spans[n].groups = sb(top, f"groups{n}", [1, NG], i32)[:]
        stat = sb(top, "stat", [P, 2, NW])
        degree = sb(top, "degree", [P, NW])
        keys = sb(top, "keys", [P, NT])
        mlp_scope = ExitStack()
        mlp = EdgeMlp(nc, mlp_scope, a, w_dram)
        L0 = ExitStack()
        before = sb(L0, "before", [P, P])
        ones = sb(L0, "ones", [P, P])
        s_nodes = sb(L0, "s_nodes", [P, NW, 2])
        w_ext = sb(L0, "w_ext", [P, D + 2])
        w0 = sb(L0, "w0", [P, D])
        a0 = sb(L0, "a0", [P, 2])
        wh = sb(L0, "wh", [P, NW, D])
        xt = sb(L0, "xt", [P, R, P])
        dst = sb(L0, "dst", [P, NT], i32)

        loaded = sem("loaded")
        pool_steps = sem("pool_steps")
        const_done = sem("const_done")
        with nc.Block() as block:

            @block.sync
            def _(sp):
                loads = [(x[:], a["x"]), (src[:], a["src_tiles"]),
                         (dst[:], a["dst_tiles"]), (w0[:], a["L0_W"]), (a0[:], a["L0_a"]),
                         (w_ext[:, 0:D], a["L0_WT"])]
                for to, of in loads:
                    sp.dma_start(to, of).then_inc(loaded, 16)
                sp.wait_ge(loaded, 16 * len(loads))

            @block.gpsimd
            def _(pool):
                nc.gpsimd.iota(iota[:], pattern=[[1, NP]], base=0, channel_multiplier=0,
                               allow_small_or_imprecise_dtypes=True).then_inc(pool_steps, 1)
                nc.gpsimd.iota(own_lane[:], pattern=[[0, 1]], base=0, channel_multiplier=1,
                               allow_small_or_imprecise_dtypes=True).then_inc(pool_steps, 1)

            @block.vector
            def _(dve):
                dve.wait_ge(pool_steps, 2)
                nc.vector.tensor_scalar(ident[:], iota[:, 0:P], own_lane[:], None, ALU.is_equal)
                nc.vector.tensor_scalar(before[:], iota[:, 0:P], own_lane[:], None, ALU.is_gt)
                nc.vector.memset(ones[:], 1.0)

        with ExitStack() as st:
            ps = st.enter_context(nc.psum_tensor("wh_ps", [P, R + 1, 4 * P], f32))
            xt_loaded = [sem(f"xt_loaded{j}") for j in range(R)]
            ext_ready = sem("ext_ready")
            ext_done = sem("ext_done")
            wh_product = sem("wh_product")
            wh_taken = sem("wh_taken")
            with nc.Block() as block:

                @block.sync
                def _(sp):
                    with sp.Fori(0, NB) as i:
                        for j in range(R):
                            sp.wait_ge(wh_product, R * i + j + 1)
                            sp.dma_start(xt[:, j, :], a["xT"][:, bass.ds((R * i + j) * P, P)]).then_inc(xt_loaded[j], 16)

                @block.tensor
                def _(pe):
                    nc.tensor.matmul(ps[:, R, 0:2], w0[:], a0[:], start=True, stop=True).then_inc(ext_ready, 1)
                    pe.sem_inc(wh_product, R)
                    pe.wait_ge(ext_done, 1)
                    with pe.Fori(0, NB) as i:
                        for j in range(R):
                            pe.wait_ge(xt_loaded[j], 16 * (i + 1))
                            pe.wait_ge(wh_taken, R * i + j + 1)
                            nc.tensor.matmul(ps[:, j, 0:D + 2], xt[:, j, :], w_ext[:], start=True, stop=True).then_inc(wh_product, 1)

                @block.scalar
                def _(act):
                    act.sem_inc(wh_taken, R)
                    with act.Fori(0, NB) as i:
                        for j in range(R):
                            act.wait_ge(wh_product, R + R * i + j + 1)
                            nc.scalar.activation(win(s_nodes, R * i + j), ps[:, j, D:D + 2], ACT.Copy)
                            nc.scalar.activation(win(wh, R * i + j), ps[:, j, 0:D], ACT.Copy).then_inc(wh_taken, 1)

                @block.vector
                def _(dve):
                    dve.wait_ge(ext_ready, 1)
                    nc.vector.tensor_copy(w_ext[:, D:D + 2], ps[:, R, 0:2]).then_inc(ext_done, 1)

        rec = sb(L0, "rec", [P, NT, 3], i32)
        hi = sb(L0, "hi", [P, 2, NT])
        with ExitStack() as st:
            flat = sb(st, "flat", [P, 2, NT], i32)
            flat_lo = sb(st, "flat_lo", [P, 2, NT], bf16)
            mask = sb(st, "mask", [P, NT], i16)
            ones_row = sb(st, "ones_row", [P, NT], bf16)
            running = sb(st, "running", [P, NT])
            place = sb(st, "place", [P, NT])
            count = sb(st, "count", [P, NW])
            offset = sb(st, "offset", [P, NW])
            upto = sb(st, "upto", [P, NW])
            count_ps = st.enter_context(nc.psum_tensor("count_ps", [P, 2, 512], f32))
            flat_loaded = sem("flat_loaded")
            lo_ready = sem("lo_ready")
            lo_stored = sem("lo_stored")
            own_done = sem("rank_own_done")
            counted = sem("counted")
            totals_done = sem("totals_done")
            first_done = sem("first_done")
            second_done = sem("second_done")
            rank_turn = sem("rank_turn")
            flat_src = a["edges"].rearrange("k (p c) -> p k c", p=P)
            with nc.Block() as block:

                @block.sync
                def _(sp):
                    sp.dma_start(flat[:], flat_src).then_inc(flat_loaded, 16)
                    sp.dma_start(wh_dram.rearrange("(w p) f -> p w f", p=P), wh[:]).then_inc(flat_loaded, 16)
                    sp.wait_ge(lo_ready, 1)
                    sp.dma_start(lo_dram.rearrange("k (p c) -> p k c", p=P), flat_lo[:]).then_inc(lo_stored, 16)
                    sp.wait_ge(flat_loaded, 32)
                    sp.wait_ge(lo_stored, 16)

                @block.gpsimd
                def _(pool):
                    last = s_nodes[:, NW - 1, 1:2]
                    nc.gpsimd.affine_select(out=last, in_=last, compare_op=ALU.is_gt, fill=-1e30,
                                            base=N - (NW - 1) * P, pattern=[[0, 1]], channel_multiplier=-1)

                @block.tensor
                def _(pe):
                    pe.wait_ge(counted, 1)
                    nc.tensor.matmul(count_ps[:, 0, 0:NW], before[:], count[:], start=True, stop=True)
                    nc.tensor.matmul(count_ps[:, 1, 0:NW], ones[:], count[:], start=True, stop=True).then_inc(totals_done, 1)

                @block.vector
                def _(dve):
                    own = Steps(dve, own_done)
                    own.mark(nc.vector.memset(ones_row[:], 1.0))
                    for n, nodes in enumerate((src, dst)):
                        own.do(nc.vector.tensor_scalar(rec[:, :, 2], nodes[:], 7, None, ALU.logical_shift_right))
                        own.do(nc.vector.tensor_copy(hi[:, n, :], rec[:, :, 2]))
                        own.mark(nc.vector.tensor_copy(rec[:, :, n], nodes[:]))
                    own.mark(nc.vector.tensor_copy(keys[:], dst[:]))
                    dve.wait_ge(flat_loaded, 32)
                    own.do(nc.vector.tensor_scalar(flat[:], flat[:], P - 1, None, ALU.bitwise_and))
                    nc.vector.tensor_copy(flat_lo[:], flat[:]).then_inc(lo_ready, 1)
                    dve.sem_inc(first_done, 1)
                    with dve.Fori(0, NW) as w:
                        dve.wait_ge(first_done, 1 + 2 * w)
                        nc.vector.tensor_scalar(mask[:], hi[:, 0, :], iota[:, bass.ds(w, 1)], None, ALU.is_equal).then_inc(first_done, 1)
                        dve.wait_ge(first_done, 1 + 2 * w + 1)
                        nc.vector.tensor_reduce(count[:, bass.ds(w, 1)], mask[:], AX.X, ALU.add).then_inc(first_done, 1)
                    dve.wait_ge(first_done, 1 + 2 * NW)
                    dve.sem_inc(counted, 1)
                    dve.wait_ge(totals_done, 1)
                    own.do(nc.vector.tensor_copy(offset[:], count_ps[:, 1, 0:NW]))
                    own.do(nc.vector.tensor_tensor_scan(upto[:], ones_row[:, 0:NW], offset[:], 0.0, ALU.mult, ALU.add))
                    own.do(nc.vector.tensor_tensor(upto[:], upto[:], offset[:], ALU.subtract))
                    own.do(nc.vector.tensor_tensor(upto[:], upto[:], count_ps[:, 0, 0:NW], ALU.add))
                    own.do(nc.vector.tensor_scalar(offset[:], upto[:], -1.0, None, ALU.add))
                    own.do(nc.vector.memset(place[:], 0.0))
                    dve.sem_inc(second_done, 1)
                    with dve.Fori(0, NW) as w:
                        dve.wait_ge(second_done, 1 + 3 * w)
                        nc.vector.tensor_scalar(mask[:], hi[:, 0, :], iota[:, bass.ds(w, 1)], None, ALU.is_equal).then_inc(second_done, 1)
                        dve.wait_ge(second_done, 1 + 3 * w + 1)
                        nc.vector.tensor_tensor_scan(running[:], ones_row[:], mask[:], offset[:, bass.ds(w, 1)], ALU.mult, ALU.add).then_inc(second_done, 1)
                        dve.wait_ge(second_done, 1 + 3 * w + 2)
                        dve.sem_inc(rank_turn, 1)
                        nc.vector.copy_predicated(place[:], mask[:], running[:]).then_inc(second_done, 1)
                    dve.wait_ge(second_done, 1 + 3 * NW)
                    group4, tile = flat[:, 0, :], flat[:, 1, :]
                    spot = rec[:, :, 2]
                    own.do(nc.vector.tensor_copy(spot, place[:]))
                    own.mark(nc.vector.tensor_scalar(group4, spot, 9, 2, ALU.logical_shift_right, ALU.logical_shift_left))
                    own.do(nc.vector.tensor_scalar(tile, spot, T - 1, None, ALU.bitwise_and))
                    own.mark(nc.vector.tensor_tensor(group4, group4, tile, ALU.bitwise_or))
                    own.do(nc.vector.tensor_scalar(spot, spot, 2, P - 1, ALU.logical_shift_right, ALU.bitwise_and))
                    own.do(nc.vector.tensor_scalar(place[:], spot, float(NT), None, ALU.mult))
                    nc.vector.tensor_tensor(spot, place[:], group4, ALU.add)

        with ExitStack() as st:
            lanes = sb(st, "lanes", [P, S, 2, GE], bf16)
            hot_t = sb(st, "hot_t", [P, S, 2, GE])
            pick = sb(st, "pick", [P, 2, T, 2, NW])
            pick_prod = sb(st, "pick_prod", [P, T, 2, NW])
            stage = sb(st, "rec_stage", [P, S, T, 4], i32)
            score_ps = st.enter_context(nc.psum_tensor("score_ps", [P, S, 512], f32))
            mlp.psum(nc, st, "score")
            pool_sent = sem("pool_sent")
            lanes_in = [sem(f"lanes_in{s}") for s in range(S)]
            hot_ready = sem("hot_ready")
            picked_from = sem("picked_from")
            tables_done = sem("tables_done")
            scored = sem("scored")
            rec_staged = sem("rec_staged")
            pick_own = sem("pick_own")
            turn = sem("scatter_turn")
            sent = [sem(f"sent{s}") for s in range(S)]
            with nc.Block() as block:

                @block.sync
                def _(sp):
                    def load(s, g):
                        rows = lo_dram[:, bass.ds(g * GE, GE)].partition_broadcast(P)
                        sp.dma_start(lanes[:, s], rows).then_inc(lanes_in[s], 16)

                    for s in range(S):
                        load(s, s)
                    with sp.Fori(0, NI - 1) as i:
                        for s in range(S):
                            sp.wait_ge(hot_ready, S * i + s + 1)
                            load(s, S * (i + 1) + s)
                        mlp.sync(sp, 2 * i)
                        mlp.sync(sp, 2 * i + 1)
                    mlp.sync(sp, 2 * NI - 2)
                    mlp.sync(sp, 2 * NI - 1)

                @block.tensor
                def _(pe):
                    pe.sem_inc(tables_done, S)
                    with pe.Fori(0, NI) as i:
                        for s in range(S):
                            pe.wait_ge(hot_ready, S * i + s + 1)
                            pe.wait_ge(scored, S * i + s + 1)
                            table = score_ps[:, s, 0:T * 2 * NW].rearrange("p (t k w) -> p t k w", t=T, k=2)
                            for t in range(T):
                                for n in range(2):
                                    ins = nc.tensor.matmul(table[:, t, n, :], hot_t[:, s, n, t * P:(t + 1) * P],
                                                           s_nodes[:, :, n], start=True, stop=True)
                            ins.then_inc(tables_done, 1)
                            if s == 1:
                                mlp.tensor_first(nc, pe, 2 * i, range(4))
                        mlp.tensor_second(nc, pe, 2 * i, range(T))
                        mlp.tensor_first(nc, pe, 2 * i + 1, range(4))
                        mlp.tensor_second(nc, pe, 2 * i + 1, range(T))

                @block.vector
                def _(dve):
                    dve.sem_inc(scored, S)

                    def body(i, first):
                        for s in range(S):
                            dve.wait_ge(lanes_in[s], 16 * (i + 1))
                            dve.wait_ge(tables_done, S * i + s + 1)
                            nc.vector.tensor_scalar(hot_t[:, s], lanes[:, s], own_lane[:], None, ALU.is_equal).then_inc(hot_ready, 1)
                        own = Steps(dve, pick_own, i * (2 * S))
                        for s in range(S):
                            g = S * i + s
                            windows = hi[:, :, bass.ds(g * T, T)].rearrange("p k t -> p t k").unsqueeze(3).to_broadcast([P, T, 2, NW])
                            cols = iota[:, 0:NW].unsqueeze(1).unsqueeze(1).to_broadcast([P, T, 2, NW])
                            own.do(nc.vector.tensor_tensor(pick[:, 0], cols, windows, ALU.is_equal))
                            dve.wait_ge(tables_done, S + g + 1)
                            table = score_ps[:, s, 0:T * 2 * NW].rearrange("p (t k w) -> p t k w", t=T, k=2)
                            own.do(nc.vector.tensor_tensor(pick_prod[:], pick[:, 0], table, ALU.mult))
                            dve.wait_ge(pool_sent, g + 1)
                            score = stage[:, s, :, 3].bitcast(f32)
                            nc.vector.tensor_reduce(score, pick_prod[:], AX.XY, ALU.add).then_inc(scored, 1)
                            if s == 0 and not first:
                                mlp.vector(nc, dve, 2 * i - 1)
                        mlp.vector(nc, dve, 2 * i)

                    body(0, True)
                    with dve.Fori(1, NI) as i:
                        body(i, False)
                    mlp.vector(nc, dve, 2 * NI - 1)

                @block.scalar
                def _(act):
                    with act.Fori(0, NI) as i:
                        for s in range(S):
                            act.wait_ge(pool_sent, S * i + s + 1)
                            nc.scalar.copy(stage[:, s, :, 0:3], rec[:, bass.ds((S * i + s) * T, T), :]).then_inc(rec_staged, 1)
                            if s % 2 == 1:
                                mlp.scalar(nc, act, 2 * i + s // 2, range(4))

                @block.gpsimd
                def _(pool):
                    pool.sem_inc(pool_sent, S - 2)

                    def send(s, g, i, landed):
                        pool.wait_ge(rec_staged, g + 1)
                        pool.wait_ge(scored, S + g + 1)
                        pool.sem_inc(turn, 1)
                        for t in range(T):
                            pool.indirect_dma_start(
                                sorted_dram, bass.IndirectOffsetOnAxis(ap=stage[:, s, t, 2:3], axis=0),
                                stage[:, s, t, :], None).then_inc(sent[s], 16)
                        if landed is not None:
                            pool.wait_ge(sent[(s - 2) % S], 16 * T * landed)
                        pool.sem_inc(pool_sent, 1)

                    for s in range(S):
                        send(s, s, 0, None if s < 2 else 1)
                    with pool.Fori(1, NI) as i:
                        for s in range(S):
                            send(s, S * i + s, i, i + (s >= 2))
                    for s in range(S):
                        pool.wait_ge(sent[s], 16 * T * NI)
                    pool.sem_inc(turn, 1)
        L0.close()

        L0 = ExitStack()
        srec = sb(L0, "srec", [P, NG, T, 4], i32)
        weight = sb(L0, "weight", [P, NT])
        keys_src = sb(L0, "keys_src", [P, NT])
        with ExitStack() as st:
            wide = sb(st, "wide", [P, 2, NT])
            wide_i = sb(st, "wide_i", [P, NT], i32)
            ends = sb(st, "ends", [P, 2, 2, NG])
            ends_all = sb(st, "ends_all", [P, 2, 2, NG])
            row = sb(st, "row", [1, 2, 3, NG])
            row_i = sb(st, "row_i", [1, 2, 3, NG], i32)
            one_row = sb(st, "one_row", [1, NG])
            some = sb(st, "some", [1, 3, NI])
            some_i = sb(st, "some_i", [1, 3, NI], i32)
            top_score = sb(st, "top_score", [P, 3])
            recs_in = sem("recs_in")
            own_done = sem("span_own_done")
            ends_ready = sem("ends_ready")
            ends_reduced = sem("ends_reduced")
            weights_in = sem("weights_in")
            with nc.Block() as block:

                @block.sync
                def _(sp):
                    sp.dma_start(srec[:].rearrange("p g t c -> p (g t c)"),
                                 sorted_dram.rearrange("(p e) c -> p (e c)", p=P)).then_inc(recs_in, 16)

                @block.vector
                def _(dve):
                    own = Steps(dve, own_done)
                    own.mark(nc.vector.memset(one_row[:], 1.0))
                    dve.wait_ge(recs_in, 16)
                    flat_rec = srec[:].rearrange("p g t c -> p (g t) c")
                    own.do(nc.vector.tensor_copy(keys_src[:], flat_rec[:, :, 0]))
                    for n, nodes in enumerate((keys_src, keys)):
                        own.do(nc.vector.tensor_copy(wide_i[:], nodes[:]))
                        own.do(nc.vector.tensor_scalar(wide_i[:], wide_i[:], 7, None, ALU.logical_shift_right))
                        own.do(nc.vector.tensor_copy(wide[:, n], wide_i[:]))
                        by_group = wide[:, n].rearrange("p (g t) -> p g t", t=T)
                        own.mark(nc.vector.tensor_reduce(ends[:, n, 1], by_group, AX.X, ALU.max))
                        own.do(nc.vector.tensor_reduce(ends[:, n, 0], by_group, AX.X, ALU.min, negate=True))
                    score = flat_rec[:, :, 3].bitcast(f32)
                    own.do(nc.vector.tensor_reduce(top_score[:, 0:1], score, AX.X, ALU.max))
                    dve.sem_inc(ends_ready, 1)
                    own.do(nc.vector.tensor_scalar(weight[:], score, 0.2, None, ALU.mult))
                    own.do(nc.vector.tensor_tensor(weight[:], weight[:], score, ALU.max))
                    dve.wait_ge(ends_reduced, 2)
                    own.do(nc.vector.tensor_scalar(top_score[:, 2:3], top_score[:, 1:2], 0.2, None, ALU.mult))
                    own.do(nc.vector.tensor_tensor(top_score[:, 2:3], top_score[:, 2:3], top_score[:, 1:2], ALU.max))
                    nc.vector.tensor_scalar(weight[:], weight[:], top_score[:, 2:3], None, ALU.subtract).then_inc(weights_in, 1)
                    for n in range(2):
                        lows, highs = ends_all[0:1, n, 0], ends_all[0:1, n, 1]
                        own.mark(nc.vector.tensor_scalar(row[:, n, 0], lows, -1.0, None, ALU.mult))
                        own.do(nc.vector.tensor_tensor(row[:, n, 1], highs, lows, ALU.add))
                        own.do(nc.vector.tensor_tensor_scan(row[:, n, 2], one_row[:], row[:, n, 1], 0.0, ALU.mult, ALU.add))
                        own.do(nc.vector.tensor_tensor(row[:, n, 2], row[:, n, 2], row[:, n, 1], ALU.subtract))
                        firsts = row[:, n, 0].rearrange("a (i s) -> a i s", s=S)
                        own.do(nc.vector.tensor_copy(some[:, 0], firsts[:, :, 0]))
                        for m in range(1, S):
                            own.do(nc.vector.tensor_scalar(some[:, 1], firsts[:, :, m], float(64 ** m), None, ALU.mult))
                            own.do(nc.vector.tensor_tensor(some[:, 0], some[:, 0], some[:, 1], ALU.add))
                        mores = row[:, n, 1].rearrange("a (i s) -> a i s", s=S)
                        own.do(nc.vector.tensor_reduce(some[:, 1], mores, AX.X, ALU.max))
                        own.do(nc.vector.tensor_tensor(some[:, 1, 1:], some[:, 1, 1:], mores[:, 0:NI - 1, S - 1], ALU.max))
                        own.do(nc.vector.tensor_scalar(some[:, 1], some[:, 1], 1.0, None, ALU.min))
                        own.mark(nc.vector.memset(some[:, 2, 0:1], 0.0))
                        own.do(nc.vector.tensor_copy(some[:, 2, 1:], firsts[:, 0:NI - 1, S - 1]))
                        own.do(nc.vector.tensor_copy(some_i[:], some[:]))
                        own.mark(nc.vector.tensor_scalar(some_i[:, 1], some_i[:, 1], 6 * (S + 1), None, ALU.logical_shift_left))
                        own.do(nc.vector.tensor_scalar(some_i[:, 0], some_i[:, 0], 6, None, ALU.logical_shift_left))
                        own.do(nc.vector.tensor_tensor(some_i[:, 0], some_i[:, 0], some_i[:, 1], ALU.bitwise_or))
                        own.mark(nc.vector.tensor_tensor(spans[n].bodies, some_i[:, 0], some_i[:, 2], ALU.bitwise_or))
                        own.do(nc.vector.tensor_copy(row_i[:, n], row[:, n]))
                        own.do(nc.vector.tensor_scalar(row_i[:, n, 2], row_i[:, n, 2], 6, None, ALU.logical_shift_left))
                        own.do(nc.vector.tensor_tensor(spans[n].groups, row_i[:, n, 1], row_i[:, n, 2], ALU.bitwise_or))

                @block.gpsimd
                def _(pool):
                    pool.wait_ge(ends_ready, 1)
                    from_all = bass.bass_isa.ReduceOp.max
                    nc.gpsimd.partition_all_reduce(top_score[:, 1:2], top_score[:, 0:1], P, from_all).then_inc(ends_reduced, 1)
                    nc.gpsimd.partition_all_reduce(ends_all[:].rearrange("p a b g -> p (a b g)"),
                                                   ends[:].rearrange("p a b g -> p (a b g)"), P, from_all).then_inc(ends_reduced, 1)

                @block.scalar
                def _(act):
                    act.wait_ge(weights_in, 1)
                    nc.scalar.activation(weight[:], weight[:], ACT.Exp)

        acc_scope = ExitStack()
        acc = sb(acc_scope, "acc0", [P, NW, D + 1])
        tmp = sb(acc_scope, "tmp0", [P, NW, D])
        with nc.Block() as block:

            @block.vector
            def _(dve):
                nc.vector.memset(acc[:], 0.0)

        flat_rec = srec[:].rearrange("p g t c -> p (g t) c")
        sum_rows(nc, "soft", iota, keys_src, spans[0], wh_dram, lambda g: flat_rec[:, bass.ds(g * T, T), 1],
                 acc, mlp, 2 * NI, weight)

        def soft_end():
            own_done = sem("elu_own_done")
            low_ready = sem("low_ready")
            exp_done = sem("exp_done")
            shape = [P, NW, D]
            with nc.Block() as block:

                @block.vector
                def _(dve):
                    own = Steps(dve, own_done)
                    h = acc[:, :, 0:D]
                    own.do(nc.vector.tensor_scalar(stat[:, 0], acc[:, :, D], SOFT_EPS, None, ALU.add))
                    own.do(nc.vector.reciprocal(stat[:, 1], stat[:, 0]))
                    own.do(nc.vector.tensor_tensor(h, h, over(stat[:, 1], shape, 2), ALU.mult))
                    nc.vector.tensor_scalar(tmp[:], h, 0.0, None, ALU.min).then_inc(low_ready, 1)
                    own.do(nc.vector.tensor_scalar(h, h, 0.0, None, ALU.max))
                    own.do(nc.vector.tensor_tensor(x[:], x[:], h, ALU.add))
                    dve.wait_ge(exp_done, 1)
                    own.do(nc.vector.tensor_scalar(tmp[:], tmp[:], -1.0, None, ALU.add))
                    own.do(nc.vector.tensor_tensor(x[:], x[:], tmp[:], ALU.add))
                    nc.vector.memset(acc[:], 0.0)

                @block.scalar
                def _(act):
                    act.wait_ge(low_ready, 1)
                    nc.scalar.activation(tmp[:], tmp[:], ACT.Exp).then_inc(exp_done, 1)

        soft_end()
        layer_norm(nc, shared, x[:], tmp[:], stat)
        store(nc, shared, [(x_dram.rearrange("(w p) f -> p w f", p=P), x[:])])

        sum_rows(nc, "mean", iota, keys, spans[1], x_dram, lambda g: src[:, bass.ds(g * T, T)], acc, mlp, 3 * NI)
        with ExitStack() as st:
            w_top = sb(st, "w_top", [P, D])
            w_bot = sb(st, "w_bot", [P, D])
            w_agg = sb(st, "w_agg", [P, D])
            w_both = sb(st, "w_both", [P, D])
            b_agg = sb(st, "b_agg", [P, 1])
            b_row = sb(st, "b_row", [1, D])
            one_row = sb(st, "one_lane", [1, P])
            gamma = sb(st, "gamma", [P, 2, D])
            loaded1 = sem("loaded1")
            both_done = sem("both_done")
            own_done = sem("mean_own_done")
            with nc.psum_tensor("w_ps", [P, 2, 512], f32) as w_ps, nc.Block() as block:

                @block.sync
                def _(sp):
                    loads = [(w_top[:], a["L1_W"][0:D, :]), (w_bot[:], a["L1_W"][D:2 * D, :]), (w_agg[:], a["L1_aggWT"]),
                             (b_agg[:], a["L1_agg_b"]), (b_row[:], a["L1_b"]),
                             (gamma[:, 0, :], a["L1_gamma"].partition_broadcast(P)), (gamma[:, 1, :], a["L1_beta"].partition_broadcast(P))]
                    for to, of in loads:
                        sp.dma_start(to, of).then_inc(loaded1, 16)
                    sp.wait_ge(loaded1, 16 * 7)

                @block.tensor
                def _(pe):
                    pe.wait_ge(loaded1, 16 * 7)
                    nc.tensor.matmul(w_ps[:, 0, 0:D], w_agg[:], w_bot[:], start=True, stop=True)
                    nc.tensor.matmul(w_ps[0:1, 1, 0:D], b_agg[:], w_bot[:], start=True, stop=True).then_inc(both_done, 1)

                @block.vector
                def _(dve):
                    own = Steps(dve, own_done)
                    own.mark(nc.vector.memset(one_row[:], 1.0))
                    own.do(nc.vector.tensor_scalar(stat[:, 0], acc[:, :, D], 1.0, None, ALU.max))
                    own.do(nc.vector.reciprocal(degree[:], stat[:, 0]))
                    own.do(nc.vector.tensor_tensor(acc[:, :, 0:D], acc[:, :, 0:D], over(degree[:], [P, NW, D], 2), ALU.mult))
                    dve.wait_ge(both_done, 1)
                    nc.vector.tensor_copy(w_both[:], w_ps[:, 0, 0:D])
                    nc.vector.tensor_tensor(b_row[:], b_row[:], w_ps[0:1, 1, 0:D], ALU.add)

            node_products(nc, shared, "agg", ident[:], [lambda w: win(x, w), lambda w: acc[:, bass.ds(w, 1), 0:D].rearrange("p a f -> p (a f)")],
                          [w_top[:], w_both[:]], D,
                          lambda nc, w, ps: nc.scalar.activation(win(tmp, w), ps, ACT.Relu), bias=(one_row[:], b_row[:]))
            layer_norm(nc, shared, tmp[:], acc[:, :, 0:D], stat)
            own_done = sem("mean_end_own")
            with nc.Block() as block:

                @block.vector
                def _(dve):
                    own = Steps(dve, own_done)
                    shape = [P, NW, D]
                    own.do(nc.vector.tensor_tensor(tmp[:], tmp[:], gamma[:, 0, :].unsqueeze(1).to_broadcast(shape), ALU.mult))
                    own.do(nc.vector.tensor_tensor(tmp[:], tmp[:], gamma[:, 1, :].unsqueeze(1).to_broadcast(shape), ALU.add))
                    nc.vector.tensor_tensor(x[:], x[:], tmp[:], ALU.add)
            layer_norm(nc, shared, x[:], tmp[:], stat)
        acc_scope.close()
        L0.close()
        mlp_scope.close()

        acc_scope = ExitStack()
        acc = sb(acc_scope, "acc2", [P, NW, 2 * D])
        direct = sb(acc_scope, "direct", [P, NW, D])
        node_scale = sb(acc_scope, "node_scale", [P, 2, NW])
        with ExitStack() as st:
            w_y = sb(st, "w_y", [P, 2 * D])
            y = sb(st, "y", [P, NW, D])
            loaded2 = sem("loaded2")
            with nc.Block() as block:

                @block.sync
                def _(sp):
                    sp.dma_start(w_y[:], a["L2_in"]).then_inc(loaded2, 16)
                    sp.dma_start(node_scale[:, 0], a["node_vec"]).then_inc(loaded2, 16)
                    sp.wait_ge(loaded2, 32)

                @block.vector
                def _(dve):
                    own = Steps(dve, sem("scale_own"))
                    dve.wait_ge(loaded2, 32)
                    own.do(nc.vector.tensor_scalar(node_scale[:, 1], node_scale[:, 0], (2 * MUL) ** -0.5, None, ALU.mult))
                    nc.vector.tensor_scalar(node_scale[:, 0], node_scale[:, 0], MUL ** -0.5, None, ALU.mult)
                    nc.vector.memset(acc[:], 0.0)

            def taken(to):
                return lambda nc, w, ps: nc.scalar.activation(win(to, w), ps, ACT.Copy, scale=node_scale[:, 0, bass.ds(w, 1)])

            node_products(nc, shared, "y", ident[:], [lambda w: win(x, w)], [w_y[:, 0:D]], D, taken(y))
            node_products(nc, shared, "direct", ident[:], [lambda w: win(x, w)], [w_y[:, D:2 * D]], D, taken(direct))
            store(nc, shared, [(y_dram.rearrange("(w p) f -> p w f", p=P), y[:])])
        conv_edges(nc, a, iota, spans[1], keys, src, y_dram, acc)
        with ExitStack() as st:
            w_z = sb(st, "w_z", [P, 2, D + 1])
            conv = sb(st, "conv", [P, NW, D + 1])
            loaded3 = sem("loaded3")
            with nc.Block() as block:

                @block.sync
                def _(sp):
                    sp.dma_start(w_z[:], a["L2_out"].rearrange("(k p) f -> p k f", p=P)).then_inc(loaded3, 16)
                    sp.wait_ge(loaded3, 16)

                @block.vector
                def _(dve):
                    nc.vector.tensor_tensor(acc[:], acc[:], over(degree[:], [P, NW, 2 * D], 2), ALU.mult)

            def half(n):
                return lambda w: acc[:, bass.ds(w, 1), n * D:(n + 1) * D].rearrange("p a f -> p (a f)")

            node_products(nc, shared, "conv", ident[:], [half(0), half(1)], [w_z[:, 0, :], w_z[:, 1, :]], D + 1,
                          lambda nc, w, ps: nc.scalar.activation(win(conv, w), ps, ACT.Copy, scale=node_scale[:, 1, bass.ds(w, 1)]))
            own_done = sem("conv_end_own")
            with nc.Block() as block:

                @block.vector
                def _(dve):
                    own = Steps(dve, own_done)
                    shape = [P, NW, D]
                    own.do(nc.vector.tensor_tensor(x[:], x[:], direct[:], ALU.add))
                    own.do(nc.vector.tensor_tensor(direct[:], conv[:, :, 0:D], conv[:, :, D:D + 1].to_broadcast(shape), ALU.mult))
                    nc.vector.tensor_tensor(x[:], x[:], direct[:], ALU.add)
            layer_norm(nc, shared, x[:], direct[:], stat)
        acc_scope.close()

        acc_scope = ExitStack()
        acc = sb(acc_scope, "acc3", [P, NW, D])
        with ExitStack() as st:
            w_qkv = sb(st, "w_qkv", [P, 3 * D])
            qkv = sb(st, "qkv", [P, NW, 2 * D])
            q = sb(st, "q", [P, NW, D])
            loaded4 = sem("loaded4")
            with nc.Block() as block:

                @block.sync
                def _(sp):
                    sp.dma_start(w_qkv[:], a["L3_wqkv"]).then_inc(loaded4, 16)
                    sp.wait_ge(loaded4, 16)

                @block.vector
                def _(dve):
                    nc.vector.memset(acc[:], 0.0)

            node_products(nc, shared, "q", ident[:], [lambda w: win(x, w)], [w_qkv[:, 0:D]], D,
                          lambda nc, w, ps: nc.scalar.activation(win(q, w), ps, ACT.Copy))
            node_products(nc, shared, "kv", ident[:], [lambda w: win(x, w)], [w_qkv[:, D:3 * D]], 2 * D,
                          lambda nc, w, ps: nc.scalar.activation(win(qkv, w), ps, ACT.Copy))
            store(nc, shared, [(q_dram.rearrange("(w p) f -> p w f", p=P), q[:]),
                              (kv_dram.rearrange("(w p) f -> p w f", p=P), qkv[:])])
        attention_edges(nc, a, iota, spans[1], keys, src, w_dram, q_dram, kv_dram, acc)
        with nc.Block() as block:

            @block.vector
            def _(dve):
                nc.vector.tensor_tensor(x[:], x[:], acc[:], ALU.add)
        layer_norm(nc, shared, x[:], acc[:], stat)
        whole = (NW - 1) * P
        store(nc, shared, [(out[0:whole, :].rearrange("(w p) f -> p w f", p=P), x[:, 0:NW - 1, :]),
                          (out[whole:N, :], x[0:N - whole, NW - 1, :])])
        acc_scope.close()


def conv_edges(nc, a, iota, spans, keys, src, y_dram, acc):
    with ExitStack() as st:
        sem = nc.alloc_semaphore

        def sb(name, shape, dt=f32):
            return st.enter_context(nc.sbuf_tensor(f"conv_{name}", shape, dt))

        c = Sums(nc, st, "conv", iota, keys, spans, acc, 2 * D)
        rows = sb("rows", [P, S, T, D])
        stage = sb("stage", [P, S, T], i32)
        scalars = sb("scalars", [10, S, GE])
        harm = sb("harm", [P, NT, 4])
        w1 = sb("w1", [10, 100])
        w2 = sb("w2", [100, D])
        hid = sb("hid", [100, 2, GE])
        msgs = sb("msgs", [P, 2, T, 2 * D])
        ysh = sb("ysh", [P, T, D])
        t01 = sb("t01", [P, T, MUL])
        t11 = sb("t11", [P, T, 3, MUL])
        hid_ps = st.enter_context(nc.psum_tensor("conv_hid_ps", [P, 2, GE], f32))
        w_ps = st.enter_context(nc.psum_tensor("conv_w_ps", [P, 2, T, D], f32))
        loaded = sem("conv_loaded")
        scaled = sem("conv_scaled")
        own_done = sem("conv_own_done")
        staged = sem("conv_staged")
        turn = sem("conv_turn")
        rows_used = sem("conv_rows_used")
        hid_sum = sem("conv_hid_sum")
        hid_done = sem("conv_hid_done")
        w_done = sem("conv_w_done")
        msg_done = sem("conv_msg_done")
        gathered = [nc.alloc_semaphore(f"conv_gathered{s}") for s in range(S)]
        scalars_in = [sem(f"conv_scalars_in{s}") for s in range(S)]

        with nc.Block() as block:

            @block.sync
            def _(sp):
                for to, of in [(w1[:], a["L2_fc1"]), (w2[:], a["L2_fc2"]), (harm[:], a["harm"])]:
                    sp.dma_start(to, of).then_inc(loaded, 16)
                sp.wait_ge(loaded, 48)

            @block.vector
            def _(dve):
                own = Steps(dve, scaled)
                dve.wait_ge(loaded, 48)
                own.do(nc.vector.tensor_scalar(w2[:], w2[:], 0.1, None, ALU.mult))
                nc.vector.tensor_scalar(w2[:, MUL:2 * MUL], w2[:, MUL:2 * MUL], 3 ** -0.5, None, ALU.mult)

        with nc.Block() as block:

            @block.sync
            def _(sp):
                for s in range(S):
                    sp.dma_start(scalars[:, s, :], a["scalars"][:, s * GE:(s + 1) * GE]).then_inc(scalars_in[s], 16)
                with sp.Fori(0, NI) as i:
                    for s in range(S):
                        sp.wait_ge(hid_sum, S * i + s + 1)
                        sp.dma_start(scalars[:, s, :], a["scalars"][:, bass.ds((S * (i + 1) + s) * GE, GE)]).then_inc(scalars_in[s], 16)
                for s in range(S):
                    sp.wait_ge(scalars_in[s], 16 * (NI + 1))

            @block.scalar
            def _(act):
                def silu(g, n):
                    act.wait_ge(hid_sum, g + 1)
                    nc.scalar.activation(hid[:, n], hid_ps[0:100, n], ACT.Silu, scale=10 ** -0.5).then_inc(hid_done, 1)

                def indices(s, g):
                    nc.scalar.copy(stage[:, s], src[:, bass.ds(g * T, T)]).then_inc(staged, 1)

                def body(i, last):
                    for s in range(S):
                        act.wait_ge(w_done, S * i + s + 1)
                        silu(S * i + s + 2, s % 2)
                        if not last:
                            act.wait_ge(gathered[s], 16 * T * (i + 1))
                            indices(s, S * (i + 1) + s)

                for s in range(S):
                    indices(s, s)
                silu(0, 0)
                silu(1, 1)
                with act.Fori(0, NI - 1) as i:
                    body(i, False)
                body(NI - 1, True)

            @block.gpsimd
            def _(pool):
                with pool.Fori(0, NI) as i:
                    for s in range(S):
                        pool.wait_ge(staged, S * i + s + 1)
                        pool.wait_ge(rows_used, S * i + s + 1)
                        pool.sem_inc(turn, 1)
                        for t in range(T):
                            pool.indirect_dma_start(
                                rows[:, s, t, :], None, y_dram,
                                bass.IndirectOffsetOnAxis(ap=stage[:, s, t:t + 1], axis=0)).then_inc(gathered[s], 16)

            @block.tensor
            def _(pe):
                def first(n, slot, count):
                    pe.wait_ge(scalars_in[slot], count)
                    nc.tensor.matmul(hid_ps[0:100, n], w1[:], scalars[:, slot, :], start=True, stop=True).then_inc(hid_sum, 1)

                def second(g, n):
                    pe.wait_ge(hid_done, g + 1)
                    for t in range(T):
                        ins = nc.tensor.matmul(w_ps[:, n, t, :], hid[:, n, t * P:(t + 1) * P], w2[:], start=True, stop=True)
                    ins.then_inc(w_done, 1)

                tensor_sums_start(pe, c)
                first(0, 0, 16)
                first(1, 1, 16)
                second(0, 0)
                with pe.Fori(0, NI) as i:
                    body = Body(pe, spans, i)
                    for s in range(S):
                        g = S * i + s
                        pe.wait_ge(hid_done, g + 1)
                        first(s % 2, (s + 2) % S, 16 * (i + 1 + (s >= S - 2)))
                        pe.wait_ge(msg_done, 1 + g)
                        second(g + 1, (s + 1) % 2)
                        pe.wait_ge(msg_done, 1 + g + 1)
                        tensor_sums(nc, pe, c, body, s, g, msgs[:, s % 2])

            @block.vector
            def _(dve):
                dve.sem_inc(rows_used, S)
                dve.sem_inc(msg_done, 1)
                vector_sums_start(dve, c)

                def one_body(i, first):
                    own = Steps(dve, own_done, i * (7 * S))
                    body = Body(dve, spans, i)
                    for s in range(S):
                        g = S * i + s
                        msg = msgs[:, s % 2]
                        hs = harm[:, bass.ds(g * T, T), :]
                        w = w_ps[:, s % 2]
                        dve.wait_ge(msg_done, 1 + g)
                        dve.wait_ge(gathered[s], 16 * T * (i + 1))
                        own.mark(nc.vector.tensor_tensor(ysh[:], rows[:, s], hs[:, :, 0:1].to_broadcast([P, T, D]), ALU.mult))
                        y0 = rows[:, s, :, 0:MUL]
                        y1 = rows[:, s, :, MUL:D].rearrange("p t (c u) -> p t c u", c=3)
                        sh1 = hs[:, :, 1:4].unsqueeze(3).to_broadcast([P, T, 3, MUL])
                        own.mark(nc.vector.tensor_tensor(t11[:], y1, sh1, ALU.mult))
                        dve.wait_ge(w_done, g + 1)
                        nc.vector.tensor_tensor(t01[:], w[:, :, 2 * MUL:3 * MUL], y0, ALU.mult).then_inc(rows_used, 1)
                        own.wait()
                        dve.wait_ge(rows_used, S + g + 1)
                        own.mark(nc.vector.tensor_tensor(msg[:, :, 0:MUL], w[:, :, 0:MUL], ysh[:, :, 0:MUL], ALU.mult))
                        m10 = msg[:, :, 2 * MUL + 3 * MUL:].rearrange("p t (c u) -> p t c u", c=3)
                        w10 = w[:, :, 3 * MUL:].unsqueeze(2).to_broadcast([P, T, 3, MUL])
                        own.mark(nc.vector.tensor_tensor(m10, w10, ysh[:, :, MUL:].rearrange("p t (c u) -> p t c u", c=3), ALU.mult))
                        m01 = msg[:, :, 2 * MUL:5 * MUL].rearrange("p t (c u) -> p t c u", c=3)
                        own.mark(nc.vector.tensor_tensor(m01, t01[:].unsqueeze(2).to_broadcast([P, T, 3, MUL]), sh1, ALU.mult))
                        own.do(nc.vector.tensor_tensor(t11[:, :, 0], t11[:, :, 0], t11[:, :, 1], ALU.add))
                        own.do(nc.vector.tensor_tensor(t11[:, :, 0], t11[:, :, 0], t11[:, :, 2], ALU.add))
                        nc.vector.tensor_tensor(msg[:, :, MUL:2 * MUL], w[:, :, MUL:2 * MUL], t11[:, :, 0], ALU.mult).then_inc(msg_done, 1)
                        vector_hot(nc, dve, c, body, s, g)
                        if s > 0 or not first:
                            vector_add(nc, dve, c, body, s - 1, g - 1)

                one_body(0, True)
                with dve.Fori(1, NI) as i:
                    one_body(i, False)
                vector_add(nc, dve, c, Body(dve, spans, NI - 1), S - 1, NG - 1)


def attention_edges(nc, a, iota, spans, keys, src, w_dram, q_dram, kv_dram, acc):
    with ExitStack() as st:
        sem = nc.alloc_semaphore

        def sb(name, shape, dt=f32):
            return st.enter_context(nc.sbuf_tensor(f"att_{name}", shape, dt))

        c = Sums(nc, st, "att", iota, keys, spans, acc, D)
        q_rows = sb("q_rows", [P, S, T, D])
        kv_rows = sb("kv_rows", [P, S, T, 2 * D])
        w_rows = sb("w_rows", [P, S, T, D])
        stage = sb("stage", [P, S, 2, T], i32)
        cut = sb("cut", [P, NT])
        qk = sb("qk", [P, T, D])
        alpha = sb("alpha", [P, T, HEADS])
        msgs = sb("msgs", [P, 2, T, D])
        loaded = sem("att_loaded")
        own_done = sem("att_own_done")
        staged = sem("att_staged")
        turn = sem("att_turn")
        rows_used = sem("att_rows_used")
        msg_done = sem("att_msg_done")
        gathered = [sem(f"att_gathered{s}") for s in range(S)]
        w_in = [sem(f"att_w_in{s}") for s in range(S)]

        with nc.Block() as block:

            @block.sync
            def _(sp):
                sp.dma_start(cut[:], a["cut"]).then_inc(loaded, 16)

            @block.vector
            def _(dve):
                dve.wait_ge(loaded, 16)
                nc.vector.tensor_scalar(cut[:], cut[:], 1.0 / 64.0, None, ALU.mult)

        with nc.Block() as block:

            @block.sync
            def _(sp):
                with sp.Fori(0, NI) as i:
                    for s in range(S):
                        sp.wait_ge(rows_used, S * i + s + 1)
                        sp.dma_start(w_rows[:, s].rearrange("p t f -> p (t f)"),
                                     w_dram[:, bass.ds((S * i + s) * T * D, T * D)]).then_inc(w_in[s], 16)

            @block.scalar
            def _(act):
                with act.Fori(0, NI) as i:
                    for s in range(S):
                        act.wait_ge(rows_used, S * i + s + 1)
                        nc.scalar.copy(stage[:, s, 0], src[:, bass.ds((S * i + s) * T, T)])
                        nc.scalar.copy(stage[:, s, 1], keys[:, bass.ds((S * i + s) * T, T)]).then_inc(staged, 1)

            @block.gpsimd
            def _(pool):
                with pool.Fori(0, NI) as i:
                    for s in range(S):
                        pool.wait_ge(staged, S * i + s + 1)
                        pool.sem_inc(turn, 1)
                        for t in range(T):
                            pool.indirect_dma_start(
                                kv_rows[:, s, t, :], None, kv_dram,
                                bass.IndirectOffsetOnAxis(ap=stage[:, s, 0, t:t + 1], axis=0)).then_inc(gathered[s], 16)
                            pool.indirect_dma_start(
                                q_rows[:, s, t, :], None, q_dram,
                                bass.IndirectOffsetOnAxis(ap=stage[:, s, 1, t:t + 1], axis=0)).then_inc(gathered[s], 16)

            @block.tensor
            def _(pe):
                tensor_sums_start(pe, c)
                with pe.Fori(0, NI) as i:
                    body = Body(pe, spans, i)
                    for s in range(S):
                        g = S * i + s
                        pe.wait_ge(msg_done, g + 1)
                        tensor_sums(nc, pe, c, body, s, g, msgs[:, s % 2])

            @block.vector
            def _(dve):
                dve.sem_inc(rows_used, S)
                vector_sums_start(dve, c)

                def one_body(i, first):
                    own = Steps(dve, own_done, i * (4 * S))
                    body = Body(dve, spans, i)
                    for s in range(S):
                        g = S * i + s
                        dve.wait_ge(gathered[s], 32 * T * (i + 1))
                        own.do(nc.vector.tensor_tensor(qk[:], q_rows[:, s], kv_rows[:, s, :, 0:D], ALU.mult))
                        dve.wait_ge(w_in[s], 16 * (i + 1))
                        own.do(nc.vector.tensor_tensor(qk[:], qk[:], w_rows[:, s], ALU.mult))
                        own.do(nc.vector.tensor_reduce(alpha[:], qk[:].rearrange("p t (h d) -> p t h d", h=HEADS), AX.X, ALU.add))
                        own.do(nc.vector.tensor_tensor(alpha[:], alpha[:], over(cut[:, bass.ds(g * T, T)], [P, T, HEADS], 2), ALU.mult))
                        v = kv_rows[:, s, :, D:].rearrange("p t (h d) -> p t h d", h=HEADS)
                        nc.vector.tensor_tensor(msgs[:, s % 2].rearrange("p t (h d) -> p t h d", h=HEADS), v,
                                                over(alpha[:], [P, T, HEADS, HD], 3), ALU.mult).then_inc(msg_done, 1)
                        vector_hot(nc, dve, c, body, s, g)
                        dve.wait_ge(msg_done, g + 1)
                        dve.sem_inc(rows_used, 1)
                        if s > 0 or not first:
                            vector_add(nc, dve, c, body, s - 1, g - 1)

                one_body(0, True)
                with dve.Fori(1, NI) as i:
                    one_body(i, False)
                vector_add(nc, dve, c, Body(dve, spans, NI - 1), S - 1, NG - 1)


def laid_out(inputs):
    z = {k: np.asarray(v) for k, v in inputs.items()}

    def edges(v):
        p = np.full((EP,), PAD, v.dtype)
        p[:E] = v
        return p

    def tiles(v):
        return np.ascontiguousarray(v.reshape(NT, P, -1).transpose(1, 0, 2))

    def zeros_after(v, n):
        p = np.zeros((n,) + v.shape[1:], v.dtype)
        p[:v.shape[0]] = v
        return p

    src, dst = edges(z["src"]), edges(z["dst"])
    x = zeros_after(z["x"], NP)
    o = {"x": x.reshape(NW, P, D).transpose(1, 0, 2), "xT": np.ascontiguousarray(x.T), "edges": np.stack([src, dst]),
         "src_tiles": tiles(src)[:, :, 0], "dst_tiles": tiles(dst)[:, :, 0]}
    o["L0_W"] = z["L0_gnn_W"]
    o["L0_WT"] = z["L0_gnn_W"].T
    o["L0_a"] = z["L0_gnn_a"].reshape(2, D).T
    o["L1_W"] = z["L1_gnn_W"]
    o["L1_aggWT"] = z["L1_gnn_agg_W"].T
    o["L1_agg_b"] = z["L1_gnn_agg_b"].reshape(D, 1)
    o["L1_b"] = z["L1_gnn_b"].reshape(1, D)
    o["L1_gamma"] = z["L1_gnn_gamma"]
    o["L1_beta"] = z["L1_gnn_beta"]
    o["node_vec"] = zeros_after(z["node_vec1"], NP).reshape(NW, P).T
    w_in = np.zeros((D, 2 * D), np.float32)
    w_in[:MUL, :MUL] = z["L2_gnn_W_l1_0"]
    w_in[:MUL, D:D + MUL] = z["L2_gnn_W_sc0"]
    w_out = np.zeros((2 * D, D + 1), np.float32)
    w_out[:2 * MUL, :MUL] = z["L2_gnn_W_l2_0"]
    w_out[:2 * MUL, D] = z["L2_gnn_W_alpha"][:, 0]
    for c in range(3):
        w_in[MUL + c:D:3, MUL + c * MUL:MUL + (c + 1) * MUL] = z["L2_gnn_W_l1_1"]
        w_in[MUL + c:D:3, D + MUL + c:2 * D:3] = z["L2_gnn_W_sc1"]
        at = 2 * MUL + c * MUL
        w_out[at:at + MUL, MUL + c:D:3] = z["L2_gnn_W_l2_1"][:MUL]
        w_out[at + 3 * MUL:at + 4 * MUL, MUL + c:D:3] = z["L2_gnn_W_l2_1"][MUL:]
    o["L2_in"], o["L2_out"] = w_in, w_out
    o["L2_fc1"], o["L2_fc2"] = z["L2_gnn_W_fc1"], z["L2_gnn_W_fc2"]
    o["harm"] = tiles(zeros_after(z["edge_attr_4"], EP))
    o["scalars"] = zeros_after(z["edge_attr_10"], EA).T
    o["L3_wqkv"] = np.concatenate([z["L3_gnn_wq"], z["L3_gnn_wk"], z["L3_gnn_wv"]], axis=1)
    o["rad"] = zeros_after(z["edge_attr_64"], EA).T
    o["sph"] = zeros_after(z["edge_attr_32"], EA).T
    o["cut"] = tiles(zeros_after(z["edge_weight"], EP))[:, :, 0]
    o["rad_w0"], o["sph_w0"] = z["L3_gnn_rad_w0"], z["L3_gnn_sph_w0"]
    o["rad_w1"], o["sph_w1"] = z["L3_gnn_rad_w1"], z["L3_gnn_sph_w1"]
    o["b0"] = np.concatenate([z["L3_gnn_rad_b0"].reshape(HID // P, P), z["L3_gnn_sph_b0"].reshape(HID // P, P)]).T
    o["rad_b1"], o["sph_b1"] = z["L3_gnn_rad_b1"], z["L3_gnn_sph_b1"]
    return {k: np.ascontiguousarray(v) for k, v in o.items()}


def kernel(**inputs):
    import concourse.bacc as bacc
    from concourse.bass_utils import run_bass_kernel_spmd

    nc = bacc.Bacc("TRN2", target_bir_lowering=False, num_devices=1)
    arrays = {f"in_{k}": v for k, v in laid_out(inputs).items()}
    aps = {k[3:]: nc.dram_tensor(k, v.shape, mybir.dt.from_np(v.dtype), kind="ExternalInput").ap() for k, v in arrays.items()}
    out = nc.dram_tensor("out_x", (N, D), f32, kind="ExternalOutput").ap()
    gnn_kernel(nc, aps, out)
    got = run_bass_kernel_spmd(nc, [arrays], core_ids=[0])
    return got.results[0]["out_x"]
```

```python
from contextlib import ExitStack

import concourse.bass as bass
import numpy as np
from concourse import mybir

f32 = mybir.dt.float32
bf16 = mybir.dt.bfloat16
i32 = mybir.dt.int32
i16 = mybir.dt.int16
ALU = mybir.AluOpType
ACT = mybir.ActivationFunctionType
AX = mybir.AxisListType

P = 128
N = 6250
E = 206250
D = 128
NW = -(-N // P)
NP = NW * P
PAD = NP - 1
T = 4
GE = T * P
S = 4
NI = -(-E // (S * GE))
NG = NI * S
NT = NG * T
EP = NT * P
EA = EP + S * GE
R = 7
NB = NW // R
MUL = 32
HEADS, HD = 8, 16
HID = 256
LN_EPS = 1e-5
SOFT_EPS = 1e-10


class Names:
    pass


class Steps:

    def __init__(self, eng, sem, base=0):
        self.eng, self.sem, self.base, self.n = eng, sem, base, 0

    def mark(self, ins):
        self.n += 1
        ins.then_inc(self.sem, 1)

    def wait(self):
        self.eng.wait_ge(self.sem, self.base + self.n)

    def do(self, ins):
        self.mark(ins)
        self.wait()


def over(ap, shape, axis):
    return ap.unsqueeze(axis).to_broadcast(shape)


def win(ap, w):
    return ap[:, bass.ds(w, 1), :].rearrange("p a f -> p (a f)")


def node_products(nc, c, name, ident, sources, weights, width, evacuate, bias=None):
    ns = len(sources)
    with ExitStack() as st:
        staged = st.enter_context(nc.sbuf_tensor(f"{name}_staged", [P, R, ns, P], f32))
        turned = st.enter_context(nc.sbuf_tensor(f"{name}_turned", [P, R, ns, P], f32))
        bank = st.enter_context(nc.psum_tensor(f"{name}_bank", [P, R, 4 * P], f32))
        stage_done, turn_done, copy_done, product_done, out_done = c.ring
        used = NW * c.ring_uses
        c.ring_uses += 1

        with nc.Block() as block:

            @block.vector
            def _(dve):
                with dve.Fori(0, NB) as i:
                    for j in range(R):
                        dve.wait_ge(turn_done, used + R * i + j + 1)
                        for n, source in enumerate(sources):
                            ins = nc.vector.tensor_copy(staged[:, j, n, :], source(R * i + j))
                        ins.then_inc(stage_done, 1)

            @block.tensor
            def _(pe):
                if used == 0:
                    pe.sem_inc(turn_done, R)
                if used == 0:
                    pe.sem_inc(product_done, R)
                with pe.Fori(0, NB) as i:
                    for j in range(R):
                        pe.wait_ge(stage_done, used + R * i + j + 1)
                        pe.wait_ge(out_done, used + R * i + j + 1)
                        for n in range(ns):
                            ins = nc.tensor.transpose(bank[:, j, n * P:(n + 1) * P], staged[:, j, n, :], ident)
                        ins.then_inc(turn_done, 1)
                    for j in range(R):
                        pe.wait_ge(copy_done, used + R + R * i + j + 1)
                        out = bank[:, j, 2 * P:2 * P + width]
                        for n in range(ns):
                            ins = nc.tensor.matmul(out, turned[:, j, n, :], weights[n], start=n == 0,
                                                   stop=bias is None and n == ns - 1)
                        if bias is not None:
                            ins = nc.tensor.matmul(out, bias[0], bias[1], start=False, stop=True)
                        ins.then_inc(product_done, 1)

            @block.scalar
            def _(act):
                if used == 0:
                    act.sem_inc(copy_done, R)
                if used == 0:
                    act.sem_inc(out_done, R)
                with act.Fori(0, NB) as i:
                    for j in range(R):
                        act.wait_ge(turn_done, used + R + R * i + j + 1)
                        act.wait_ge(product_done, used + R * i + j + 1)
                        nc.scalar.activation(turned[:, j].rearrange("p n f -> p (n f)"), bank[:, j, 0:ns * P], ACT.Copy).then_inc(copy_done, 1)
                    for j in range(R):
                        act.wait_ge(product_done, used + R + R * i + j + 1)
                        evacuate(nc, R * i + j, bank[:, j, 2 * P:2 * P + width]).then_inc(out_done, 1)


def layer_norm(nc, c, x, tmp, stat):
    shape = [P, NW, D]
    var_ready, std_ready = c.norm
    used = c.norm_uses
    c.norm_uses += 1
    with nc.Block() as block:

        @block.vector
        def _(dve):
            own = c.own
            own.do(nc.vector.tensor_reduce(stat[:, 0], x, AX.X, ALU.add))
            own.do(nc.vector.tensor_scalar(stat[:, 0], stat[:, 0], 1.0 / D, None, ALU.mult))
            own.do(nc.vector.tensor_tensor(x, x, over(stat[:, 0], shape, 2), ALU.subtract))
            own.do(nc.vector.tensor_tensor(tmp, x, x, ALU.mult))
            own.do(nc.vector.tensor_reduce(stat[:, 1], tmp, AX.X, ALU.add))
            nc.vector.tensor_scalar(stat[:, 1], stat[:, 1], 1.0 / D, LN_EPS, ALU.mult, ALU.add).then_inc(var_ready, 1)
            dve.wait_ge(std_ready, used + 1)
            own.do(nc.vector.reciprocal(stat[:, 1], stat[:, 0]))
            nc.vector.tensor_tensor(x, x, over(stat[:, 1], shape, 2), ALU.mult)

        @block.scalar
        def _(act):
            act.wait_ge(var_ready, used + 1)
            nc.scalar.activation(stat[:, 0], stat[:, 1], ACT.Sqrt).then_inc(std_ready, 1)


def store(nc, c, pairs):
    c.stores += len(pairs)
    with nc.Block() as block:

        @block.sync
        def _(sp):
            for dst, src in pairs:
                sp.dma_start(dst, src).then_inc(c.landed, 16)
            sp.wait_ge(c.landed, 16 * c.stores)


class Body:

    def __init__(self, eng, spans, i):
        self.word = eng.value_load(spans.bodies[:, bass.ds(i, 1)], min_val=0, max_val=2 ** 31 - 1)
        self.mores = eng.value_load(spans.mores[:, bass.ds(i, 1)], min_val=0, max_val=2 ** (S + 1) - 1)
        self.firsts, self.eng = {}, eng

    def first(self, s):
        if s not in self.firsts:
            self.firsts[s] = self.eng.snap((self.word >> (6 * (s + 1))) & 63)
        return self.firsts[s]

    def more(self, s):
        return self.eng.snap((self.mores >> (s + 1)) & 1)


def load_more(eng, spans, g):
    v = eng.value_load(spans.groups[:, bass.ds(g, 1)], min_val=0, max_val=2 ** 31 - 1)
    return eng.snap(v & 63), eng.snap(v >> 6)


def window_of(nc, first, j):
    return nc.s_assert_within(first + j, 0, NW - 1, skip_runtime_bounds_check_because="spans hold windows of real nodes")


class Sums:

    def __init__(self, nc, st, name, iota, keys, spans, acc, width, weight=None):
        self.iota, self.keys, self.spans, self.acc, self.weight = iota, keys, spans, acc, weight
        sem = nc.alloc_semaphore
        self.hot = st.enter_context(nc.sbuf_tensor(f"{name}_hot", [P, 2, T, P], f32))
        self.hot_x = st.enter_context(nc.sbuf_tensor(f"{name}_hot_x", [P, T, P], f32))
        part = st.enter_context(nc.psum_tensor(f"{name}_part", [P, 3, 512], f32))
        self.part, self.part_x = part[:, 0:2, 0:width], part[:, 2, 0:width]
        self.equal_done = sem(f"{name}_equal_done")
        self.hot_done = sem(f"{name}_hot_done")
        self.sums_done = sem(f"{name}_sums_done")
        self.added = sem(f"{name}_added")
        self.equal_done_x = sem(f"{name}_equal_done_x")
        self.hot_done_x = sem(f"{name}_hot_done_x")
        self.sums_done_x = sem(f"{name}_sums_done_x")
        self.added_x = sem(f"{name}_added_x")


def one_hot(nc, dve, c, hot, g, w, equal_done, count, hot_done):
    key = over(c.keys[:, bass.ds(g * T, T)], [P, T, P], 2)
    nodes = c.iota[:, bass.ds(w * P, P)].unsqueeze(1).to_broadcast([P, T, P])
    if c.weight is None:
        nc.vector.tensor_tensor(hot, nodes, key, ALU.is_equal).then_inc(hot_done, 1)
    else:
        nc.vector.tensor_tensor(hot, nodes, key, ALU.is_equal).then_inc(equal_done, 1)
        dve.wait_ge(equal_done, count)
        weight = over(c.weight[:, bass.ds(g * T, T)], [P, T, P], 2)
        nc.vector.tensor_tensor(hot, hot, weight, ALU.mult).then_inc(hot_done, 1)


def vector_hot(nc, dve, c, body, s, g):
    w = window_of(nc, body.first(s), 0)
    dve.wait_ge(c.sums_done, g + 1)
    one_hot(nc, dve, c, c.hot[:, s % 2], g, w, c.equal_done, g + 1, c.hot_done)


def scalar_hot(nc, act, c, body, s, g):
    nodes = c.iota[:, bass.ds(window_of(nc, body.first(s), 0) * P, P)]
    hot = c.hot[:, s % 2]
    act.wait_ge(c.sums_done, g + 1)
    for t in range(T):
        ins = nc.scalar.activation(hot[:, t, :], nodes, ACT.Square, scale=-1.0, bias=c.keys[:, bass.ds(g * T + t, 1)])
    ins.then_inc(c.equal_done, 1)
    act.wait_ge(c.equal_done, g + 1)
    nc.scalar.activation(hot, hot, ACT.Relu, scale=-1.0, bias=1.0).then_inc(c.hot_done, 1)


def vector_add(nc, dve, c, body, s, g):
    with dve.If(body.more(s) > 0):
        more, before = load_more(dve, c.spans, g)
        with dve.Fori(0, more) as j:
            w = window_of(nc, body.first(s), 1 + j)
            k = dve.snap(before + j)
            dve.wait_ge(c.sums_done_x, k + 1)
            one_hot(nc, dve, c, c.hot_x[:], g, w, c.equal_done_x, k + 1, c.hot_done_x)
            dve.wait_ge(c.sums_done_x, 1 + k + 1)
            dve.wait_ge(c.added, 2 + g)
            nc.vector.tensor_tensor(win(c.acc, w), win(c.acc, w), c.part_x, ALU.add).then_inc(c.added_x, 1)
            dve.wait_ge(c.added_x, 1 + k + 1)
    w = window_of(nc, body.first(s), 0)
    dve.wait_ge(c.sums_done, 2 + g + 1)
    dve.wait_ge(c.added, 2 + g)
    nc.vector.tensor_tensor(win(c.acc, w), win(c.acc, w), c.part[:, s % 2], ALU.add).then_inc(c.added, 1)


def tensor_sums(nc, pe, c, body, s, g, rows):
    pe.wait_ge(c.hot_done, g + 1)
    pe.wait_ge(c.added, g + 1)
    for t in range(T):
        ins = nc.tensor.matmul(c.part[:, s % 2], c.hot[:, s % 2, t, :], rows[:, t, :], start=t == 0, stop=t == T - 1)
    ins.then_inc(c.sums_done, 1)
    with pe.If(body.more(s) > 0):
        more, before = load_more(pe, c.spans, g)
        with pe.Fori(0, more) as j:
            k = pe.snap(before + j)
            pe.wait_ge(c.hot_done_x, k + 1)
            pe.wait_ge(c.added_x, k + 1)
            for t in range(T):
                ins = nc.tensor.matmul(c.part_x, c.hot_x[:, t, :], rows[:, t, :], start=t == 0, stop=t == T - 1)
            ins.then_inc(c.sums_done_x, 1)


def vector_sums_start(dve, c):
    dve.sem_inc(c.added, 2)
    dve.sem_inc(c.added_x, 1)


def tensor_sums_start(pe, c):
    pe.sem_inc(c.sums_done, 2)
    pe.sem_inc(c.sums_done_x, 1)


class EdgeMlp:

    NC = HID // P

    def __init__(self, nc, st, a, w_dram):
        def sb(name, shape, dt=f32):
            return st.enter_context(nc.sbuf_tensor(f"mlp_{name}", shape, dt))

        sem = nc.alloc_semaphore
        self.a, self.w_dram, NC = a, w_dram, self.NC
        self.rad = sb("rad", [64, GE])
        self.sph = sb("sph", [32, GE])
        self.rad_w0 = sb("rad_w0", [64, HID])
        self.sph_w0 = sb("sph_w0", [32, HID])
        self.w1 = sb("w1", [P, 2 * NC, D])
        self.b0 = sb("b0", [P, 2 * NC])
        self.b1 = sb("b1", [P, 2, D])
        self.hid = sb("hid", [P, 2 * NC, GE])
        self.w = sb("w", [P, T, D])
        self.cut = sb("cut", [P, NT])
        self.loaded = sem("mlp_loaded")
        self.feats_in = sem("mlp_feats_in")
        self.hid_sum = sem("mlp_hid_sum")
        self.hid_done = sem("mlp_hid_done")
        self.w_sum = sem("mlp_w_sum")
        self.w_moved = sem("mlp_w_moved")
        self.w_taken = sem("mlp_w_taken")
        self.w_stored = sem("mlp_w_stored")

        loads = [(self.cut[:], a["cut"]), (self.rad_w0[:], a["rad_w0"]), (self.sph_w0[:], a["sph_w0"]), (self.b0[:], a["b0"]),
                 (self.w1[:, 0:NC], a["rad_w1"].rearrange("(k p) f -> p k f", p=P)),
                 (self.w1[:, NC:], a["sph_w1"].rearrange("(k p) f -> p k f", p=P)),
                 (self.b1[:, 0, :], a["rad_b1"].partition_broadcast(P)),
                 (self.b1[:, 1, :], a["sph_b1"].partition_broadcast(P))]
        with nc.Block() as block:

            @block.sync
            def _(sp):
                for to, of in loads:
                    sp.dma_start(to, of).then_inc(self.loaded, 16)
                self.load(sp, 0)
                sp.wait_ge(self.loaded, 16 * len(loads))
                sp.sem_inc(self.w_stored, 16)

            @block.tensor
            def _(pe):
                pe.sem_inc(self.hid_sum, 1)
                pe.sem_inc(self.w_sum, 1)

            @block.scalar
            def _(act):
                act.sem_inc(self.hid_done, 2)

            @block.vector
            def _(dve):
                dve.wait_ge(self.loaded, 16 * len(loads))
                dve.sem_inc(self.w_taken, 1)
                nc.vector.tensor_tensor(self.b1[:, 0], self.b1[:, 0], self.b1[:, 1], ALU.add)
                nc.vector.tensor_scalar(self.cut[:], self.cut[:], 1.0 / 64.0, None, ALU.mult)

    def psum(self, nc, st, name):
        bank = st.enter_context(nc.psum_tensor(f"{name}_mlp", [P, 3, GE], f32))
        self.hid_ps, self.w_ps = bank[:, 0:2], bank[:, 2]

    def load(self, sp, u):
        sp.dma_start(self.rad[:], self.a["rad"][:, bass.ds(u * GE, GE)]).then_inc(self.feats_in, 16)
        sp.dma_start(self.sph[:], self.a["sph"][:, bass.ds(u * GE, GE)]).then_inc(self.feats_in, 16)

    def load_next(self, sp, u):
        sp.wait_ge(self.hid_sum, 1 + 2 * self.NC * (u + 1))
        self.load(sp, u + 1)

    def store(self, sp, u):
        sp.wait_ge(self.w_taken, 1 + u + 1)
        sp.dma_start(self.w_dram[:, bass.ds(u * T * D, T * D)], self.w[:].rearrange("p t f -> p (t f)")).then_inc(self.w_stored, 16)

    def stored(self, sp, u):
        sp.wait_ge(self.w_stored, 16 * (u + 2))

    def tensor_first(self, nc, pe, u, chunks):
        pe.wait_ge(self.feats_in, 32 * (u + 1))
        for n in chunks:
            pe.wait_ge(self.hid_done, 2 * self.NC * u + n + 1)
            w, of = (self.rad_w0, self.rad) if n < self.NC else (self.sph_w0, self.sph)
            m = n % self.NC
            nc.tensor.matmul(self.hid_ps[:, n % 2], w[:, m * P:(m + 1) * P], of[:], start=True, stop=True).then_inc(self.hid_sum, 1)

    def tensor_second(self, nc, pe, u, tiles):
        if 0 in tiles:
            pe.wait_ge(self.hid_done, 2 + 2 * self.NC * (u + 1))
            pe.wait_ge(self.w_taken, u + 1)
        for t in tiles:
            for n in range(2 * self.NC):
                ins = nc.tensor.matmul(self.w_ps[:, t * D:(t + 1) * D], self.hid[:, n, t * P:(t + 1) * P], self.w1[:, n, :],
                                       start=n == 0, stop=n == 2 * self.NC - 1)
        if T - 1 in tiles:
            ins.then_inc(self.w_sum, 1)

    def scalar(self, nc, act, u, chunks):
        if 0 in chunks:
            act.wait_ge(self.w_sum, u + 1)
        for n in chunks:
            act.wait_ge(self.hid_sum, 1 + 2 * self.NC * u + n + 1)
            nc.scalar.activation(self.hid[:, n], self.hid_ps[:, n % 2], ACT.Silu, bias=self.b0[:, n:n + 1]).then_inc(self.hid_done, 1)

    def vector(self, nc, dve, u):
        dve.wait_ge(self.w_sum, 1 + u + 1)
        dve.wait_ge(self.w_stored, 16 * (u + 1))
        nc.vector.tensor_tensor(self.w[:], self.w_ps.rearrange("p (t f) -> p t f", t=T),
                                self.b1[:, 0].unsqueeze(1).to_broadcast([P, T, D]), ALU.add).then_inc(self.w_moved, 1)
        dve.wait_ge(self.w_moved, u + 1)
        nc.vector.tensor_tensor(self.w[:], self.w[:], over(self.cut[:, bass.ds(u * T, T)], [P, T, D], 2), ALU.mult).then_inc(self.w_taken, 1)


def sum_rows(nc, name, iota, keys, spans, table, indices, acc, mlp, unit, weight=None):
    with ExitStack() as st:
        def sb(n, shape, dt=f32):
            return st.enter_context(nc.sbuf_tensor(f"{name}_{n}", shape, dt))

        sem = nc.alloc_semaphore
        c = Sums(nc, st, name, iota, keys, spans, acc, D + 1, weight)
        mlp.psum(nc, st, name)
        rows = sb("rows", [P, S, T, D + 1])
        stage = sb("stage", [P, S, T], i32)
        ones_set = sem(f"{name}_ones_set")
        staged = sem(f"{name}_staged")
        rows_used = sem(f"{name}_rows_used")
        turn = sem(f"{name}_turn")
        gathered = [sem(f"{name}_gathered{s}") for s in range(S)]

        with nc.Block() as block:

            @block.sync
            def _(sp):
                with sp.Fori(0, NI) as i:
                    mlp.load_next(sp, unit + i)
                    mlp.store(sp, unit + i)
                mlp.stored(sp, unit + NI - 1)

            @block.scalar
            def _(act):
                def body(i, last):
                    for s in range(S):
                        if s in (0, 1):
                            mlp.scalar(nc, act, unit + i, range(2 * s, 2 * s + 2))
                        if not last:
                            act.wait_ge(gathered[s], 16 * T * (i + 1))
                            nc.scalar.copy(stage[:, s], indices(S * (i + 1) + s)).then_inc(staged, 1)

                for s in range(S):
                    nc.scalar.copy(stage[:, s], indices(s)).then_inc(staged, 1)
                with act.Fori(0, NI - 1) as i:
                    body(i, False)
                body(NI - 1, True)

            @block.gpsimd
            def _(pool):
                with pool.Fori(0, NI) as i:
                    for s in range(S):
                        pool.wait_ge(staged, S * i + s + 1)
                        pool.wait_ge(rows_used, S * i + s + 1)
                        pool.sem_inc(turn, 1)
                        for t in range(T):
                            pool.indirect_dma_start(
                                rows[:, s, t, 0:D], None, table,
                                bass.IndirectOffsetOnAxis(ap=stage[:, s, t:t + 1], axis=0)).then_inc(gathered[s], 16)

            @block.vector
            def _(dve):
                nc.vector.memset(rows[:, :, :, D:D + 1], 1.0).then_inc(ones_set, 1)
                dve.sem_inc(rows_used, S)
                vector_sums_start(dve, c)

                def take(body, s, g):
                    vector_add(nc, dve, c, body, s, g)
                    dve.sem_inc(rows_used, 1)

                def one_body(i, first):
                    body = Body(dve, spans, i)
                    for s in range(S):
                        vector_hot(nc, dve, c, body, s, S * i + s)
                        if s > 0 or not first:
                            take(body, s - 1, S * i + s - 1)
                        if s == 0 and not first:
                            mlp.vector(nc, dve, unit + i - 1)
                    return body

                one_body(0, True)
                with dve.Fori(1, NI) as i:
                    one_body(i, False)
                take(Body(dve, spans, NI - 1), S - 1, NG - 1)
                mlp.vector(nc, dve, unit + NI - 1)

            @block.tensor
            def _(pe):
                pe.wait_ge(ones_set, 1)
                tensor_sums_start(pe, c)
                with pe.Fori(0, NI) as i:
                    body = Body(pe, spans, i)
                    for s in range(S):
                        pe.wait_ge(gathered[s], 16 * T * (i + 1))
                        tensor_sums(nc, pe, c, body, s, S * i + s, rows[:, s])
                        if s == 0:
                            mlp.tensor_first(nc, pe, unit + i, range(0, 2))
                        elif s == 1:
                            mlp.tensor_first(nc, pe, unit + i, range(2, 4))
                        elif s == 2:
                            mlp.tensor_second(nc, pe, unit + i, range(0, 2))
                        else:
                            mlp.tensor_second(nc, pe, unit + i, range(2, 4))


def gnn_kernel(nc, a, out):
    top = ExitStack()

    def dram(name, shape, dt=f32):
        return nc.dram_tensor(name, shape, dt).ap()

    def sb(st, name, shape, dt=f32):
        return st.enter_context(nc.sbuf_tensor(name, shape, dt))

    sem = nc.alloc_semaphore
    shared = Names()
    shared.ring = [sem(n) for n in ("stage_done", "turn_done", "copy_done", "product_done", "out_done")]
    shared.norm = [sem(n) for n in ("var_ready", "std_ready")]
    shared.landed = sem("landed")
    shared.own = Steps(nc.vector, sem("vector_steps_done"))
    shared.ring_uses = shared.norm_uses = shared.stores = 0
    lo_dram = dram("lo_dram", [2, EP], bf16)
    sorted_dram = dram("sorted_dram", [EP, 4], i32)
    wh_dram = dram("wh_dram", [NP, D])
    x_dram = dram("x_dram", [NP, D])
    y_dram = dram("y_dram", [NP, D])
    kv_dram = dram("kv_dram", [NP, 2 * D])
    w_dram = dram("w_dram", [P, EP // P * D])

    with top:
        iota = sb(top, "iota", [P, NP])
        own_lane = sb(top, "own_lane", [P, 1])
        ident = sb(top, "ident", [P, P])
        x = sb(top, "x", [P, NW, D])
        src = sb(top, "src", [P, NT], i32)
        spans = []
        for n in range(2):
            spans.append(Names())
            spans[n].bodies = sb(top, f"bodies{n}", [1, NI], i32)[:]
            spans[n].mores = sb(top, f"mores{n}", [1, NI], i32)[:]
            spans[n].groups = sb(top, f"groups{n}", [1, NG], i32)[:]
        stat = sb(top, "stat", [P, 2, NW])
        degree = sb(top, "degree", [P, NW])
        keys = sb(top, "keys", [P, NT])
        mlp_scope = ExitStack()
        mlp = EdgeMlp(nc, mlp_scope, a, w_dram)
        L0 = ExitStack()
        before = sb(L0, "before", [P, P])
        ones = sb(L0, "ones", [P, P])
        s_nodes = sb(L0, "s_nodes", [P, NW, 2])
        w_ext = sb(L0, "w_ext", [P, D + 2])
        w0 = sb(L0, "w0", [P, D])
        a0 = sb(L0, "a0", [P, 2])
        wh = sb(L0, "wh", [P, NW, D])
        xt = sb(L0, "xt", [P, R, P])
        dst = sb(L0, "dst", [P, NT], i32)

        loaded = sem("loaded")
        pool_steps = sem("pool_steps")
        const_done = sem("const_done")
        with nc.Block() as block:

            @block.sync
            def _(sp):
                loads = [(x[:], a["x"]), (src[:], a["src_tiles"]),
                         (dst[:], a["dst_tiles"]), (w0[:], a["L0_W"]), (a0[:], a["L0_a"]),
                         (w_ext[:, 0:D], a["L0_WT"])]
                for to, of in loads:
                    sp.dma_start(to, of).then_inc(loaded, 16)
                sp.wait_ge(loaded, 16 * len(loads))

            @block.gpsimd
            def _(pool):
                nc.gpsimd.iota(iota[:], pattern=[[1, NP]], base=0, channel_multiplier=0,
                               allow_small_or_imprecise_dtypes=True).then_inc(pool_steps, 1)
                nc.gpsimd.iota(own_lane[:], pattern=[[0, 1]], base=0, channel_multiplier=1,
                               allow_small_or_imprecise_dtypes=True).then_inc(pool_steps, 1)

            @block.vector
            def _(dve):
                dve.wait_ge(pool_steps, 2)
                nc.vector.tensor_scalar(ident[:], iota[:, 0:P], own_lane[:], None, ALU.is_equal)
                nc.vector.tensor_scalar(before[:], iota[:, 0:P], own_lane[:], None, ALU.is_gt)
                nc.vector.memset(ones[:], 1.0)

        with ExitStack() as st:
            ps = st.enter_context(nc.psum_tensor("wh_ps", [P, R + 1, 4 * P], f32))
            xt_loaded = [sem(f"xt_loaded{j}") for j in range(R)]
            ext_ready = sem("ext_ready")
            ext_done = sem("ext_done")
            wh_product = sem("wh_product")
            wh_taken = sem("wh_taken")
            with nc.Block() as block:

                @block.sync
                def _(sp):
                    with sp.Fori(0, NB) as i:
                        for j in range(R):
                            sp.wait_ge(wh_product, R * i + j + 1)
                            sp.dma_start(xt[:, j, :], a["xT"][:, bass.ds((R * i + j) * P, P)]).then_inc(xt_loaded[j], 16)

                @block.tensor
                def _(pe):
                    nc.tensor.matmul(ps[:, R, 0:2], w0[:], a0[:], start=True, stop=True).then_inc(ext_ready, 1)
                    pe.sem_inc(wh_product, R)
                    pe.wait_ge(ext_done, 1)
                    with pe.Fori(0, NB) as i:
                        for j in range(R):
                            pe.wait_ge(xt_loaded[j], 16 * (i + 1))
                            pe.wait_ge(wh_taken, R * i + j + 1)
                            nc.tensor.matmul(ps[:, j, 0:D + 2], xt[:, j, :], w_ext[:], start=True, stop=True).then_inc(wh_product, 1)

                @block.scalar
                def _(act):
                    act.sem_inc(wh_taken, R)
                    with act.Fori(0, NB) as i:
                        for j in range(R):
                            act.wait_ge(wh_product, R + R * i + j + 1)
                            nc.scalar.activation(win(s_nodes, R * i + j), ps[:, j, D:D + 2], ACT.Copy)
                            nc.scalar.activation(win(wh, R * i + j), ps[:, j, 0:D], ACT.Copy).then_inc(wh_taken, 1)

                @block.vector
                def _(dve):
                    dve.wait_ge(ext_ready, 1)
                    nc.vector.tensor_copy(w_ext[:, D:D + 2], ps[:, R, 0:2]).then_inc(ext_done, 1)

        rec = sb(L0, "rec", [P, NT, 3], i32)
        hi = sb(L0, "hi", [P, 2, NT])
        with ExitStack() as st:
            flat = sb(st, "flat", [P, 2, NT], i32)
            flat_lo = sb(st, "flat_lo", [P, 2, NT], bf16)
            mask = sb(st, "mask", [P, NT], i16)
            ones_row = sb(st, "ones_row", [P, NT], bf16)
            running = sb(st, "running", [P, NT])
            place = sb(st, "place", [P, NT])
            count = sb(st, "count", [P, NW])
            offset = sb(st, "offset", [P, NW])
            upto = sb(st, "upto", [P, NW])
            count_ps = st.enter_context(nc.psum_tensor("count_ps", [P, 2, 512], f32))
            flat_loaded = sem("flat_loaded")
            lo_ready = sem("lo_ready")
            lo_stored = sem("lo_stored")
            counted = sem("counted")
            totals_done = sem("totals_done")
            first_done = sem("first_done")
            second_done = sem("second_done")
            rank_turn = sem("rank_turn")
            flat_src = a["edges"].rearrange("k (p c) -> p k c", p=P)
            with nc.Block() as block:

                @block.sync
                def _(sp):
                    sp.dma_start(flat[:], flat_src).then_inc(flat_loaded, 16)
                    sp.dma_start(wh_dram.rearrange("(w p) f -> p w f", p=P), wh[:]).then_inc(flat_loaded, 16)
                    sp.wait_ge(lo_ready, 1)
                    sp.dma_start(lo_dram.rearrange("k (p c) -> p k c", p=P), flat_lo[:]).then_inc(lo_stored, 16)
                    sp.wait_ge(flat_loaded, 32)
                    sp.wait_ge(lo_stored, 16)

                @block.gpsimd
                def _(pool):
                    last = s_nodes[:, NW - 1, 1:2]
                    nc.gpsimd.affine_select(out=last, in_=last, compare_op=ALU.is_gt, fill=-1e30,
                                            base=N - (NW - 1) * P, pattern=[[0, 1]], channel_multiplier=-1)

                @block.tensor
                def _(pe):
                    pe.wait_ge(counted, 1)
                    nc.tensor.matmul(count_ps[:, 0, 0:NW], before[:], count[:], start=True, stop=True)
                    nc.tensor.matmul(count_ps[:, 1, 0:NW], ones[:], count[:], start=True, stop=True).then_inc(totals_done, 1)

                @block.vector
                def _(dve):
                    own = shared.own
                    own.mark(nc.vector.memset(ones_row[:], 1.0))
                    for n, nodes in enumerate((src, dst)):
                        own.do(nc.vector.tensor_scalar(rec[:, :, 2], nodes[:], 7, None, ALU.logical_shift_right))
                        own.do(nc.vector.tensor_copy(hi[:, n, :], rec[:, :, 2]))
                        own.mark(nc.vector.tensor_copy(rec[:, :, n], nodes[:]))
                    own.mark(nc.vector.tensor_copy(keys[:], dst[:]))
                    dve.wait_ge(flat_loaded, 32)
                    own.do(nc.vector.tensor_scalar(flat[:], flat[:], P - 1, None, ALU.bitwise_and))
                    nc.vector.tensor_copy(flat_lo[:], flat[:]).then_inc(lo_ready, 1)
                    dve.sem_inc(first_done, 1)
                    with dve.Fori(0, NW) as w:
                        dve.wait_ge(first_done, 1 + 2 * w)
                        nc.vector.tensor_scalar(mask[:], hi[:, 0, :], iota[:, bass.ds(w, 1)], None, ALU.is_equal).then_inc(first_done, 1)
                        dve.wait_ge(first_done, 1 + 2 * w + 1)
                        nc.vector.tensor_reduce(count[:, bass.ds(w, 1)], mask[:], AX.X, ALU.add).then_inc(first_done, 1)
                    dve.wait_ge(first_done, 1 + 2 * NW)
                    dve.sem_inc(counted, 1)
                    dve.wait_ge(totals_done, 1)
                    own.do(nc.vector.tensor_copy(offset[:], count_ps[:, 1, 0:NW]))
                    own.do(nc.vector.tensor_tensor_scan(upto[:], ones_row[:, 0:NW], offset[:], 0.0, ALU.mult, ALU.add))
                    own.do(nc.vector.tensor_tensor(upto[:], upto[:], offset[:], ALU.subtract))
                    own.do(nc.vector.tensor_tensor(upto[:], upto[:], count_ps[:, 0, 0:NW], ALU.add))
                    own.do(nc.vector.tensor_scalar(offset[:], upto[:], -1.0, None, ALU.add))
                    own.do(nc.vector.memset(place[:], 0.0))
                    dve.sem_inc(second_done, 1)
                    with dve.Fori(0, NW) as w:
                        dve.wait_ge(second_done, 1 + 3 * w)
                        nc.vector.tensor_scalar(mask[:], hi[:, 0, :], iota[:, bass.ds(w, 1)], None, ALU.is_equal).then_inc(second_done, 1)
                        dve.wait_ge(second_done, 1 + 3 * w + 1)
                        nc.vector.tensor_tensor_scan(running[:], ones_row[:], mask[:], offset[:, bass.ds(w, 1)], ALU.mult, ALU.add).then_inc(second_done, 1)
                        dve.wait_ge(second_done, 1 + 3 * w + 2)
                        dve.sem_inc(rank_turn, 1)
                        nc.vector.copy_predicated(place[:], mask[:], running[:]).then_inc(second_done, 1)
                    dve.wait_ge(second_done, 1 + 3 * NW)
                    group4, tile = flat[:, 0, :], flat[:, 1, :]
                    spot = rec[:, :, 2]
                    own.do(nc.vector.tensor_copy(spot, place[:]))
                    own.mark(nc.vector.tensor_scalar(group4, spot, 9, 2, ALU.logical_shift_right, ALU.logical_shift_left))
                    own.do(nc.vector.tensor_scalar(tile, spot, T - 1, None, ALU.bitwise_and))
                    own.mark(nc.vector.tensor_tensor(group4, group4, tile, ALU.bitwise_or))
                    own.do(nc.vector.tensor_scalar(spot, spot, 2, P - 1, ALU.logical_shift_right, ALU.bitwise_and))
                    own.do(nc.vector.tensor_scalar(place[:], spot, float(NT), None, ALU.mult))
                    nc.vector.tensor_tensor(spot, place[:], group4, ALU.add)

        with ExitStack() as st:
            lanes = sb(st, "lanes", [P, S, 2, GE], bf16)
            hot_t = sb(st, "hot_t", [P, S, 2, GE], bf16)
            s_parts = sb(st, "s_parts", [P, 3, 2, NW], bf16)
            pick = sb(st, "pick", [P, T, 2, NW])
            pick_prod = sb(st, "pick_prod", [P, T, 2, NW])
            stage = sb(st, "rec_stage", [P, S, T, 4], i32)
            score_ps = st.enter_context(nc.psum_tensor("score_ps", [P, S, 512], f32))
            mlp.psum(nc, st, "score")
            pool_sent = sem("pool_sent")
            lanes_in = [sem(f"lanes_in{s}") for s in range(S)]
            hot_ready = sem("hot_ready")
            tables_done = sem("tables_done")
            scored = sem("scored")
            rec_staged = sem("rec_staged")
            pick_own = sem("pick_own")
            turn = sem("scatter_turn")
            sent = [sem(f"sent{s}") for s in range(S)]
            with nc.Block() as block:

                @block.vector
                def _(dve):
                    own = shared.own
                    scores = s_nodes[:].rearrange("p w k -> p k w")
                    for n in range(3):
                        own.do(nc.vector.tensor_copy(s_parts[:, n], scores))
                        if n < 2:
                            own.do(nc.vector.tensor_tensor(scores, scores, s_parts[:, n], ALU.subtract))

            with nc.Block() as block:

                @block.sync
                def _(sp):
                    def load(s, g):
                        rows = lo_dram[:, bass.ds(g * GE, GE)].partition_broadcast(P)
                        sp.dma_start(lanes[:, s], rows).then_inc(lanes_in[s], 16)

                    for s in range(S):
                        load(s, s)

                    def body(i, first, last):
                        for s in range(S):
                            if not last:
                                sp.wait_ge(hot_ready, S * i + s + 1)
                                load(s, S * (i + 1) + s)
                        if not first:
                            mlp.store(sp, 2 * i - 1)
                        mlp.load_next(sp, 2 * i)
                        mlp.store(sp, 2 * i)
                        mlp.load_next(sp, 2 * i + 1)

                    body(0, True, False)
                    with sp.Fori(1, NI - 1) as i:
                        body(i, False, False)
                    body(NI - 1, False, True)
                    mlp.store(sp, 2 * NI - 1)
                    mlp.stored(sp, 2 * NI - 1)

                @block.tensor
                def _(pe):
                    pe.sem_inc(tables_done, S)
                    with pe.Fori(0, NI) as i:
                        for s in range(S):
                            pe.wait_ge(hot_ready, S * i + s + 1)
                            pe.wait_ge(scored, S * i + s + 1)
                            table = score_ps[:, s, 0:T * 2 * NW].rearrange("p (t k w) -> p t k w", t=T, k=2)
                            for t in range(T):
                                for n in range(2):
                                    for m in range(3):
                                        ins = nc.tensor.matmul(table[:, t, n, :], hot_t[:, s, n, t * P:(t + 1) * P],
                                                               s_parts[:, m, n, :], start=m == 0, stop=m == 2)
                            ins.then_inc(tables_done, 1)
                            if s % 2 == 0:
                                mlp.tensor_first(nc, pe, 2 * i + s // 2, range(2 * mlp.NC))
                            else:
                                mlp.tensor_second(nc, pe, 2 * i + s // 2, range(T))

                @block.vector
                def _(dve):
                    dve.sem_inc(scored, S)

                    def columns(s, g, count):
                        dve.wait_ge(lanes_in[s], count)
                        dve.wait_ge(tables_done, g + 1)
                        nc.vector.tensor_scalar(hot_t[:, s], lanes[:, s], own_lane[:], None, ALU.is_equal).then_inc(hot_ready, 1)

                    def body(i, first, last):
                        own = Steps(dve, pick_own, i * (2 * S))
                        for s in range(S):
                            g = S * i + s
                            windows = hi[:, :, bass.ds(g * T, T)].rearrange("p k t -> p t k").unsqueeze(3).to_broadcast([P, T, 2, NW])
                            cols = iota[:, 0:NW].unsqueeze(1).unsqueeze(1).to_broadcast([P, T, 2, NW])
                            own.do(nc.vector.tensor_tensor(pick[:], cols, windows, ALU.is_equal))
                            dve.wait_ge(tables_done, S + g + 1)
                            table = score_ps[:, s, 0:T * 2 * NW].rearrange("p (t k w) -> p t k w", t=T, k=2)
                            own.do(nc.vector.tensor_tensor(pick_prod[:], pick[:], table, ALU.mult))
                            dve.wait_ge(pool_sent, g + 1)
                            score = stage[:, s, :, 3].bitcast(f32)
                            nc.vector.tensor_reduce(score, pick_prod[:], AX.XY, ALU.add).then_inc(scored, 1)
                            if not last:
                                columns(s, S * (i + 1) + s, 16 * (i + 2))
                            if s == 2:
                                mlp.vector(nc, dve, 2 * i)
                            elif s == 0 and not first:
                                mlp.vector(nc, dve, 2 * i - 1)

                    for s in range(S):
                        columns(s, s, 16)
                    body(0, True, False)
                    with dve.Fori(1, NI - 1) as i:
                        body(i, False, False)
                    body(NI - 1, False, True)
                    mlp.vector(nc, dve, 2 * NI - 1)

                @block.scalar
                def _(act):
                    with act.Fori(0, NI) as i:
                        for s in range(S):
                            act.wait_ge(pool_sent, S * i + s + 1)
                            nc.scalar.copy(stage[:, s, :, 0:3], rec[:, bass.ds((S * i + s) * T, T), :]).then_inc(rec_staged, 1)
                            if s % 2 == 0:
                                mlp.scalar(nc, act, 2 * i + s // 2, range(2 * mlp.NC))

                @block.gpsimd
                def _(pool):
                    pool.sem_inc(pool_sent, S - 2)

                    def send(s, g, i, landed):
                        pool.wait_ge(rec_staged, g + 1)
                        pool.wait_ge(scored, S + g + 1)
                        pool.sem_inc(turn, 1)
                        for t in range(T):
                            pool.indirect_dma_start(
                                sorted_dram, bass.IndirectOffsetOnAxis(ap=stage[:, s, t, 2:3], axis=0),
                                stage[:, s, t, :], None).then_inc(sent[s], 16)
                        if landed is not None:
                            pool.wait_ge(sent[(s - 2) % S], 16 * T * landed)
                        pool.sem_inc(pool_sent, 1)

                    for s in range(S):
                        send(s, s, 0, None if s < 2 else 1)
                    with pool.Fori(1, NI) as i:
                        for s in range(S):
                            send(s, S * i + s, i, i + (s >= 2))
                    for s in range(S):
                        pool.wait_ge(sent[s], 16 * T * NI)
                    pool.sem_inc(turn, 1)
        L0.close()

        L0 = ExitStack()
        srec = sb(L0, "srec", [P, NG, T, 4], i32)
        weight = sb(L0, "weight", [P, NT])
        keys_src = sb(L0, "keys_src", [P, NT])
        with ExitStack() as st:
            wide = sb(st, "wide", [P, 2, NT])
            wide_i = sb(st, "wide_i", [P, NT], i32)
            ends = sb(st, "ends", [P, 2, 2, NG])
            ends_all = sb(st, "ends_all", [P, 2, 2, NG])
            row = sb(st, "row", [1, 2, 3, NG])
            row_i = sb(st, "row_i", [1, 2, 3, NG], i32)
            one_row = sb(st, "one_row", [1, NG])
            any_more = sb(st, "any_more", [1, NG])
            some = sb(st, "some", [1, 3, NI])
            some_i = sb(st, "some_i", [1, 3, NI], i32)
            top_score = sb(st, "top_score", [P, 3])
            recs_in = sem("recs_in")
            ends_ready = sem("ends_ready")
            ends_reduced = sem("ends_reduced")
            weights_in = sem("weights_in")
            with nc.Block() as block:

                @block.sync
                def _(sp):
                    sp.dma_start(srec[:].rearrange("p g t c -> p (g t c)"),
                                 sorted_dram.rearrange("(p e) c -> p (e c)", p=P)).then_inc(recs_in, 16)

                @block.vector
                def _(dve):
                    own = shared.own
                    own.mark(nc.vector.memset(one_row[:], 1.0))
                    dve.wait_ge(recs_in, 16)
                    flat_rec = srec[:].rearrange("p g t c -> p (g t) c")
                    own.do(nc.vector.tensor_copy(keys_src[:], flat_rec[:, :, 0]))
                    for n, nodes in enumerate((keys_src, keys)):
                        own.do(nc.vector.tensor_copy(wide_i[:], nodes[:]))
                        own.do(nc.vector.tensor_scalar(wide_i[:], wide_i[:], 7, None, ALU.logical_shift_right))
                        own.do(nc.vector.tensor_copy(wide[:, n], wide_i[:]))
                        by_group = wide[:, n].rearrange("p (g t) -> p g t", t=T)
                        own.mark(nc.vector.tensor_reduce(ends[:, n, 1], by_group, AX.X, ALU.max))
                        own.do(nc.vector.tensor_reduce(ends[:, n, 0], by_group, AX.X, ALU.min, negate=True))
                    score = flat_rec[:, :, 3].bitcast(f32)
                    own.do(nc.vector.tensor_reduce(top_score[:, 0:1], score, AX.X, ALU.max))
                    dve.sem_inc(ends_ready, 1)
                    own.do(nc.vector.tensor_scalar(weight[:], score, 0.2, None, ALU.mult))
                    own.do(nc.vector.tensor_tensor(weight[:], weight[:], score, ALU.max))
                    dve.wait_ge(ends_reduced, 2)
                    own.do(nc.vector.tensor_scalar(top_score[:, 2:3], top_score[:, 1:2], 0.2, None, ALU.mult))
                    own.do(nc.vector.tensor_tensor(top_score[:, 2:3], top_score[:, 2:3], top_score[:, 1:2], ALU.max))
                    nc.vector.tensor_scalar(weight[:], weight[:], top_score[:, 2:3], None, ALU.subtract).then_inc(weights_in, 1)
                    for n in range(2):
                        lows, highs = ends_all[0:1, n, 0], ends_all[0:1, n, 1]
                        own.mark(nc.vector.tensor_scalar(row[:, n, 0], lows, -1.0, None, ALU.mult))
                        own.do(nc.vector.tensor_tensor(row[:, n, 1], highs, lows, ALU.add))
                        own.do(nc.vector.tensor_tensor_scan(row[:, n, 2], one_row[:], row[:, n, 1], 0.0, ALU.mult, ALU.add))
                        own.do(nc.vector.tensor_tensor(row[:, n, 2], row[:, n, 2], row[:, n, 1], ALU.subtract))
                        firsts = row[:, n, 0].rearrange("a (i s) -> a i s", s=S)
                        own.do(nc.vector.tensor_copy(some[:, 0], firsts[:, :, 0]))
                        for m in range(1, S):
                            own.do(nc.vector.tensor_scalar(some[:, 1], firsts[:, :, m], float(64 ** m), None, ALU.mult))
                            own.do(nc.vector.tensor_tensor(some[:, 0], some[:, 0], some[:, 1], ALU.add))
                        own.mark(nc.vector.memset(some[:, 1:3, 0:1], 0.0))
                        own.do(nc.vector.tensor_copy(some[:, 1, 1:], firsts[:, 0:NI - 1, S - 1]))
                        own.do(nc.vector.tensor_copy(some_i[:, 0:2], some[:, 0:2]))
                        own.do(nc.vector.tensor_scalar(some_i[:, 0], some_i[:, 0], 6, None, ALU.logical_shift_left))
                        own.do(nc.vector.tensor_tensor(spans[n].bodies, some_i[:, 0], some_i[:, 1], ALU.bitwise_or))
                        own.do(nc.vector.tensor_scalar(any_more[:], row[:, n, 1], 1.0, None, ALU.min))
                        mores = any_more[:].rearrange("a (i s) -> a i s", s=S)
                        own.do(nc.vector.tensor_copy(some[:, 2, 1:], mores[:, 0:NI - 1, S - 1]))
                        for m in range(S):
                            own.do(nc.vector.tensor_scalar(some[:, 1], mores[:, :, m], float(2 ** (m + 1)), None, ALU.mult))
                            own.do(nc.vector.tensor_tensor(some[:, 2], some[:, 2], some[:, 1], ALU.add))
                        own.mark(nc.vector.tensor_copy(spans[n].mores, some[:, 2]))
                        own.do(nc.vector.tensor_copy(row_i[:, n], row[:, n]))
                        own.do(nc.vector.tensor_scalar(row_i[:, n, 2], row_i[:, n, 2], 6, None, ALU.logical_shift_left))
                        own.do(nc.vector.tensor_tensor(spans[n].groups, row_i[:, n, 1], row_i[:, n, 2], ALU.bitwise_or))

                @block.gpsimd
                def _(pool):
                    pool.wait_ge(ends_ready, 1)
                    from_all = bass.bass_isa.ReduceOp.max
                    nc.gpsimd.partition_all_reduce(top_score[:, 1:2], top_score[:, 0:1], P, from_all).then_inc(ends_reduced, 1)
                    nc.gpsimd.partition_all_reduce(ends_all[:].rearrange("p a b g -> p (a b g)"),
                                                   ends[:].rearrange("p a b g -> p (a b g)"), P, from_all).then_inc(ends_reduced, 1)

                @block.scalar
                def _(act):
                    act.wait_ge(weights_in, 1)
                    nc.scalar.activation(weight[:], weight[:], ACT.Exp)

        acc_scope = ExitStack()
        acc = sb(acc_scope, "acc0", [P, NW, D + 1])
        tmp = sb(acc_scope, "tmp0", [P, NW, D])
        with nc.Block() as block:

            @block.vector
            def _(dve):
                nc.vector.memset(acc[:], 0.0)

        flat_rec = srec[:].rearrange("p g t c -> p (g t) c")
        sum_rows(nc, "soft", iota, keys_src, spans[0], wh_dram, lambda g: flat_rec[:, bass.ds(g * T, T), 1],
                 acc, mlp, 2 * NI, weight)

        def soft_end():
            low_ready = sem("low_ready")
            exp_done = sem("exp_done")
            shape = [P, NW, D]
            with nc.Block() as block:

                @block.vector
                def _(dve):
                    own = shared.own
                    h = acc[:, :, 0:D]
                    own.do(nc.vector.tensor_scalar(stat[:, 0], acc[:, :, D], SOFT_EPS, None, ALU.add))
                    own.do(nc.vector.reciprocal(stat[:, 1], stat[:, 0]))
                    own.do(nc.vector.tensor_tensor(h, h, over(stat[:, 1], shape, 2), ALU.mult))
                    nc.vector.tensor_scalar(tmp[:], h, 0.0, None, ALU.min).then_inc(low_ready, 1)
                    own.do(nc.vector.tensor_scalar(h, h, 0.0, None, ALU.max))
                    own.do(nc.vector.tensor_tensor(x[:], x[:], h, ALU.add))
                    dve.wait_ge(exp_done, 1)
                    own.do(nc.vector.tensor_scalar(tmp[:], tmp[:], -1.0, None, ALU.add))
                    own.do(nc.vector.tensor_tensor(x[:], x[:], tmp[:], ALU.add))
                    nc.vector.memset(acc[:], 0.0)

                @block.scalar
                def _(act):
                    act.wait_ge(low_ready, 1)
                    nc.scalar.activation(tmp[:], tmp[:], ACT.Exp).then_inc(exp_done, 1)

        soft_end()
        layer_norm(nc, shared, x[:], tmp[:], stat)
        store(nc, shared, [(x_dram.rearrange("(w p) f -> p w f", p=P), x[:])])

        sum_rows(nc, "mean", iota, keys, spans[1], x_dram, lambda g: src[:, bass.ds(g * T, T)], acc, mlp, 3 * NI)
        with ExitStack() as st:
            w_top = sb(st, "w_top", [P, D])
            w_bot = sb(st, "w_bot", [P, D])
            w_agg = sb(st, "w_agg", [P, D])
            w_both = sb(st, "w_both", [P, D])
            b_agg = sb(st, "b_agg", [P, 1])
            b_row = sb(st, "b_row", [1, D])
            one_row = sb(st, "one_lane", [1, P])
            gamma = sb(st, "gamma", [P, 2, D])
            loaded1 = sem("loaded1")
            both_done = sem("both_done")
            with nc.psum_tensor("w_ps", [P, 2, 512], f32) as w_ps, nc.Block() as block:

                @block.sync
                def _(sp):
                    loads = [(w_top[:], a["L1_W"][0:D, :]), (w_bot[:], a["L1_W"][D:2 * D, :]), (w_agg[:], a["L1_aggWT"]),
                             (b_agg[:], a["L1_agg_b"]), (b_row[:], a["L1_b"]),
                             (gamma[:, 0, :], a["L1_gamma"].partition_broadcast(P)), (gamma[:, 1, :], a["L1_beta"].partition_broadcast(P))]
                    for to, of in loads:
                        sp.dma_start(to, of).then_inc(loaded1, 16)
                    sp.wait_ge(loaded1, 16 * 7)

                @block.tensor
                def _(pe):
                    pe.wait_ge(loaded1, 16 * 7)
                    nc.tensor.matmul(w_ps[:, 0, 0:D], w_agg[:], w_bot[:], start=True, stop=True)
                    nc.tensor.matmul(w_ps[0:1, 1, 0:D], b_agg[:], w_bot[:], start=True, stop=True).then_inc(both_done, 1)

                @block.vector
                def _(dve):
                    own = shared.own
                    own.mark(nc.vector.memset(one_row[:], 1.0))
                    own.do(nc.vector.tensor_scalar(stat[:, 0], acc[:, :, D], 1.0, None, ALU.max))
                    own.do(nc.vector.reciprocal(degree[:], stat[:, 0]))
                    own.do(nc.vector.tensor_tensor(acc[:, :, 0:D], acc[:, :, 0:D], over(degree[:], [P, NW, D], 2), ALU.mult))
                    dve.wait_ge(both_done, 1)
                    nc.vector.tensor_copy(w_both[:], w_ps[:, 0, 0:D])
                    nc.vector.tensor_tensor(b_row[:], b_row[:], w_ps[0:1, 1, 0:D], ALU.add)

            node_products(nc, shared, "agg", ident[:], [lambda w: win(x, w), lambda w: acc[:, bass.ds(w, 1), 0:D].rearrange("p a f -> p (a f)")],
                          [w_top[:], w_both[:]], D,
                          lambda nc, w, ps: nc.scalar.activation(win(tmp, w), ps, ACT.Relu), bias=(one_row[:], b_row[:]))
            layer_norm(nc, shared, tmp[:], acc[:, :, 0:D], stat)
            with nc.Block() as block:

                @block.vector
                def _(dve):
                    own = shared.own
                    shape = [P, NW, D]
                    own.do(nc.vector.tensor_tensor(tmp[:], tmp[:], gamma[:, 0, :].unsqueeze(1).to_broadcast(shape), ALU.mult))
                    own.do(nc.vector.tensor_tensor(tmp[:], tmp[:], gamma[:, 1, :].unsqueeze(1).to_broadcast(shape), ALU.add))
                    nc.vector.tensor_tensor(x[:], x[:], tmp[:], ALU.add)
            layer_norm(nc, shared, x[:], tmp[:], stat)
        acc_scope.close()
        L0.close()
        mlp_scope.close()

        acc_scope = ExitStack()
        acc = sb(acc_scope, "acc2", [P, NW, 2 * D])
        direct = sb(acc_scope, "direct", [P, NW, D])
        node_scale = sb(acc_scope, "node_scale", [P, 2, NW])
        with ExitStack() as st:
            w_y = sb(st, "w_y", [P, 2 * D])
            y = sb(st, "y", [P, NW, D])
            loaded2 = sem("loaded2")
            with nc.Block() as block:

                @block.sync
                def _(sp):
                    sp.dma_start(w_y[:], a["L2_in"]).then_inc(loaded2, 16)
                    sp.dma_start(node_scale[:, 0], a["node_vec"]).then_inc(loaded2, 16)
                    sp.wait_ge(loaded2, 32)

                @block.vector
                def _(dve):
                    own = shared.own
                    dve.wait_ge(loaded2, 32)
                    own.do(nc.vector.tensor_scalar(node_scale[:, 1], node_scale[:, 0], (2 * MUL) ** -0.5, None, ALU.mult))
                    nc.vector.tensor_scalar(node_scale[:, 0], node_scale[:, 0], MUL ** -0.5, None, ALU.mult)
                    nc.vector.memset(acc[:], 0.0)

            def taken(to):
                return lambda nc, w, ps: nc.scalar.activation(win(to, w), ps, ACT.Copy, scale=node_scale[:, 0, bass.ds(w, 1)])

            node_products(nc, shared, "y", ident[:], [lambda w: win(x, w)], [w_y[:, 0:D]], D, taken(y))
            node_products(nc, shared, "direct", ident[:], [lambda w: win(x, w)], [w_y[:, D:2 * D]], D, taken(direct))
            store(nc, shared, [(y_dram.rearrange("(w p) f -> p w f", p=P), y[:])])
        conv_edges(nc, shared, a, iota, spans[1], keys, src, y_dram, acc)
        with ExitStack() as st:
            w_z = sb(st, "w_z", [P, 2, D + 1])
            conv = sb(st, "conv", [P, NW, D + 1])
            loaded3 = sem("loaded3")
            with nc.Block() as block:

                @block.sync
                def _(sp):
                    sp.dma_start(w_z[:], a["L2_out"].rearrange("(k p) f -> p k f", p=P)).then_inc(loaded3, 16)
                    sp.wait_ge(loaded3, 16)

                @block.vector
                def _(dve):
                    nc.vector.tensor_tensor(acc[:], acc[:], over(degree[:], [P, NW, 2 * D], 2), ALU.mult)

            def half(n):
                return lambda w: acc[:, bass.ds(w, 1), n * D:(n + 1) * D].rearrange("p a f -> p (a f)")

            node_products(nc, shared, "conv", ident[:], [half(0), half(1)], [w_z[:, 0, :], w_z[:, 1, :]], D + 1,
                          lambda nc, w, ps: nc.scalar.activation(win(conv, w), ps, ACT.Copy, scale=node_scale[:, 1, bass.ds(w, 1)]))
            with nc.Block() as block:

                @block.vector
                def _(dve):
                    own = shared.own
                    shape = [P, NW, D]
                    own.do(nc.vector.tensor_tensor(x[:], x[:], direct[:], ALU.add))
                    own.do(nc.vector.tensor_tensor(direct[:], conv[:, :, 0:D], conv[:, :, D:D + 1].to_broadcast(shape), ALU.mult))
                    nc.vector.tensor_tensor(x[:], x[:], direct[:], ALU.add)
            layer_norm(nc, shared, x[:], direct[:], stat)
        acc_scope.close()

        acc_scope = ExitStack()
        acc = sb(acc_scope, "acc3", [P, NW, D])
        with ExitStack() as st:
            w_qkv = sb(st, "w_qkv", [P, 3 * D])
            kv = sb(st, "kv", [P, NW, 2 * D])
            loaded4 = sem("loaded4")
            with nc.Block() as block:

                @block.sync
                def _(sp):
                    sp.dma_start(w_qkv[:], a["L3_wqkv"]).then_inc(loaded4, 16)
                    sp.wait_ge(loaded4, 16)

            node_products(nc, shared, "kv", ident[:], [lambda w: win(x, w)], [w_qkv[:, D:3 * D]], 2 * D,
                          lambda nc, w, ps: nc.scalar.activation(win(kv, w), ps, ACT.Copy))
            node_products(nc, shared, "q", ident[:], [lambda w: win(x, w)], [w_qkv[:, 0:D]], D,
                          lambda nc, w, ps: nc.scalar.activation(win(acc, w), ps, ACT.Copy))
            store(nc, shared, [(kv_dram.rearrange("(w p) f -> p w f", p=P), kv[:])])
        q_parts = sb(acc_scope, "q_parts", [P, NW, 3, D], bf16)
        with nc.Block() as block:

            @block.vector
            def _(dve):
                own = shared.own
                for n in range(3):
                    own.do(nc.vector.tensor_copy(q_parts[:, :, n, :], acc[:]))
                    if n < 2:
                        own.do(nc.vector.tensor_tensor(acc[:], acc[:], q_parts[:, :, n, :], ALU.subtract))
                nc.vector.memset(acc[:], 0.0)

        attention_edges(nc, shared, a, iota, own_lane, spans[1], keys, src, lo_dram, w_dram, q_parts, kv_dram, acc)
        with nc.Block() as block:

            @block.vector
            def _(dve):
                nc.vector.tensor_tensor(x[:], x[:], acc[:], ALU.add)
        layer_norm(nc, shared, x[:], acc[:], stat)
        whole = (NW - 1) * P
        store(nc, shared, [(out[0:whole, :].rearrange("(w p) f -> p w f", p=P), x[:, 0:NW - 1, :]),
                          (out[whole:N, :], x[0:N - whole, NW - 1, :])])
        acc_scope.close()


def conv_edges(nc, shared, a, iota, spans, keys, src, y_dram, acc):
    with ExitStack() as st:
        sem = nc.alloc_semaphore

        def sb(name, shape, dt=f32):
            return st.enter_context(nc.sbuf_tensor(f"conv_{name}", shape, dt))

        c = Sums(nc, st, "conv", iota, keys, spans, acc, 2 * D)
        rows = sb("rows", [P, S, T, D])
        stage = sb("stage", [P, S, T], i32)
        scalars = sb("scalars", [10, S, GE])
        harm = sb("harm", [P, NT, 4])
        w1 = sb("w1", [10, 100])
        w2 = sb("w2", [100, D])
        hid = sb("hid", [100, 2, GE])
        msgs = sb("msgs", [P, 2, T, 2 * D])
        ysh = sb("ysh", [P, T, D])
        t01 = sb("t01", [P, T, MUL])
        t11 = sb("t11", [P, T, 3, MUL])
        hid_ps = st.enter_context(nc.psum_tensor("conv_hid_ps", [P, 2, GE], f32))
        w_ps = st.enter_context(nc.psum_tensor("conv_w_ps", [P, 2, T, D], f32))
        loaded = sem("conv_loaded")
        own_done = sem("conv_own_done")
        staged = sem("conv_staged")
        turn = sem("conv_turn")
        rows_used = sem("conv_rows_used")
        hid_sum = sem("conv_hid_sum")
        hid_done = sem("conv_hid_done")
        w_done = sem("conv_w_done")
        msg_done = sem("conv_msg_done")
        gathered = [nc.alloc_semaphore(f"conv_gathered{s}") for s in range(S)]
        scalars_in = [sem(f"conv_scalars_in{s}") for s in range(S)]

        with nc.Block() as block:

            @block.sync
            def _(sp):
                for to, of in [(w1[:], a["L2_fc1"]), (w2[:], a["L2_fc2"]), (harm[:], a["harm"])]:
                    sp.dma_start(to, of).then_inc(loaded, 16)
                sp.wait_ge(loaded, 48)

            @block.vector
            def _(dve):
                own = shared.own
                dve.wait_ge(loaded, 48)
                own.do(nc.vector.tensor_scalar(w2[:], w2[:], 0.1, None, ALU.mult))
                nc.vector.tensor_scalar(w2[:, MUL:2 * MUL], w2[:, MUL:2 * MUL], 3 ** -0.5, None, ALU.mult)

        with nc.Block() as block:

            @block.sync
            def _(sp):
                for s in range(S):
                    sp.dma_start(scalars[:, s, :], a["scalars"][:, s * GE:(s + 1) * GE]).then_inc(scalars_in[s], 16)
                with sp.Fori(0, NI) as i:
                    for s in range(S):
                        sp.wait_ge(hid_sum, S * i + s + 1)
                        sp.dma_start(scalars[:, s, :], a["scalars"][:, bass.ds((S * (i + 1) + s) * GE, GE)]).then_inc(scalars_in[s], 16)
                for s in range(S):
                    sp.wait_ge(scalars_in[s], 16 * (NI + 1))

            @block.scalar
            def _(act):
                def silu(g, n):
                    act.wait_ge(hid_sum, g + 1)
                    nc.scalar.activation(hid[:, n], hid_ps[0:100, n], ACT.Silu, scale=10 ** -0.5).then_inc(hid_done, 1)

                def indices(s, g):
                    nc.scalar.copy(stage[:, s], src[:, bass.ds(g * T, T)]).then_inc(staged, 1)

                def body(i, last):
                    windows = Body(act, spans, i)
                    for s in range(S):
                        scalar_hot(nc, act, c, windows, s, S * i + s)
                        act.wait_ge(w_done, S * i + s + 1)
                        silu(S * i + s + 2, s % 2)
                        if not last:
                            act.wait_ge(gathered[s], 16 * T * (i + 1))
                            indices(s, S * (i + 1) + s)

                for s in range(S):
                    indices(s, s)
                silu(0, 0)
                silu(1, 1)
                with act.Fori(0, NI - 1) as i:
                    body(i, False)
                body(NI - 1, True)

            @block.gpsimd
            def _(pool):
                with pool.Fori(0, NI) as i:
                    for s in range(S):
                        pool.wait_ge(staged, S * i + s + 1)
                        pool.wait_ge(rows_used, S * i + s + 1)
                        pool.sem_inc(turn, 1)
                        for t in range(T):
                            pool.indirect_dma_start(
                                rows[:, s, t, :], None, y_dram,
                                bass.IndirectOffsetOnAxis(ap=stage[:, s, t:t + 1], axis=0)).then_inc(gathered[s], 16)

            @block.tensor
            def _(pe):
                def first(n, slot, count):
                    pe.wait_ge(scalars_in[slot], count)
                    nc.tensor.matmul(hid_ps[0:100, n], w1[:], scalars[:, slot, :], start=True, stop=True).then_inc(hid_sum, 1)

                def second(g, n):
                    pe.wait_ge(hid_done, g + 1)
                    for t in range(T):
                        ins = nc.tensor.matmul(w_ps[:, n, t, :], hid[:, n, t * P:(t + 1) * P], w2[:], start=True, stop=True)
                    ins.then_inc(w_done, 1)

                tensor_sums_start(pe, c)
                first(0, 0, 16)
                first(1, 1, 16)
                second(0, 0)
                with pe.Fori(0, NI) as i:
                    body = Body(pe, spans, i)
                    for s in range(S):
                        g = S * i + s
                        pe.wait_ge(hid_done, g + 1)
                        first(s % 2, (s + 2) % S, 16 * (i + 1 + (s >= S - 2)))
                        pe.wait_ge(msg_done, 1 + g)
                        second(g + 1, (s + 1) % 2)
                        pe.wait_ge(msg_done, 1 + g + 1)
                        tensor_sums(nc, pe, c, body, s, g, msgs[:, s % 2])

            @block.vector
            def _(dve):
                dve.sem_inc(rows_used, S)
                dve.sem_inc(msg_done, 1)
                vector_sums_start(dve, c)

                def one_body(i, first):
                    own = Steps(dve, own_done, i * (7 * S))
                    for s in range(S):
                        g = S * i + s
                        msg = msgs[:, s % 2]
                        hs = harm[:, bass.ds(g * T, T), :]
                        w = w_ps[:, s % 2]
                        dve.wait_ge(msg_done, 1 + g)
                        dve.wait_ge(gathered[s], 16 * T * (i + 1))
                        own.mark(nc.vector.tensor_tensor(ysh[:], rows[:, s], hs[:, :, 0:1].to_broadcast([P, T, D]), ALU.mult))
                        y0 = rows[:, s, :, 0:MUL]
                        y1 = rows[:, s, :, MUL:D].rearrange("p t (c u) -> p t c u", c=3)
                        sh1 = hs[:, :, 1:4].unsqueeze(3).to_broadcast([P, T, 3, MUL])
                        own.mark(nc.vector.tensor_tensor(t11[:], y1, sh1, ALU.mult))
                        if s == 0:
                            body = Body(dve, spans, i)
                        dve.wait_ge(w_done, g + 1)
                        nc.vector.tensor_tensor(t01[:], w[:, :, 2 * MUL:3 * MUL], y0, ALU.mult).then_inc(rows_used, 1)
                        own.wait()
                        dve.wait_ge(rows_used, S + g + 1)
                        own.mark(nc.vector.tensor_tensor(msg[:, :, 0:MUL], w[:, :, 0:MUL], ysh[:, :, 0:MUL], ALU.mult))
                        m10 = msg[:, :, 2 * MUL + 3 * MUL:].rearrange("p t (c u) -> p t c u", c=3)
                        w10 = w[:, :, 3 * MUL:].unsqueeze(2).to_broadcast([P, T, 3, MUL])
                        own.mark(nc.vector.tensor_tensor(m10, w10, ysh[:, :, MUL:].rearrange("p t (c u) -> p t c u", c=3), ALU.mult))
                        m01 = msg[:, :, 2 * MUL:5 * MUL].rearrange("p t (c u) -> p t c u", c=3)
                        own.mark(nc.vector.tensor_tensor(m01, t01[:].unsqueeze(2).to_broadcast([P, T, 3, MUL]), sh1, ALU.mult))
                        own.do(nc.vector.tensor_tensor(t11[:, :, 0], t11[:, :, 0], t11[:, :, 1], ALU.add))
                        own.do(nc.vector.tensor_tensor(t11[:, :, 0], t11[:, :, 0], t11[:, :, 2], ALU.add))
                        nc.vector.tensor_tensor(msg[:, :, MUL:2 * MUL], w[:, :, MUL:2 * MUL], t11[:, :, 0], ALU.mult).then_inc(msg_done, 1)
                        if s > 0 or not first:
                            vector_add(nc, dve, c, body, s - 1, g - 1)

                one_body(0, True)
                with dve.Fori(1, NI) as i:
                    one_body(i, False)
                vector_add(nc, dve, c, Body(dve, spans, NI - 1), S - 1, NG - 1)


def attention_edges(nc, shared, a, iota, own_lane, spans, keys, src, lo_dram, w_dram, q_parts, kv_dram, acc):
    with ExitStack() as st:
        sem = nc.alloc_semaphore

        def sb(name, shape, dt=f32):
            return st.enter_context(nc.sbuf_tensor(f"att_{name}", shape, dt))

        c = Sums(nc, st, "att", iota, keys, spans, acc, D)
        kv_rows = sb("kv_rows", [P, S, T, 2 * D])
        w_rows = sb("w_rows", [P, S, T, D])
        stage = sb("stage", [P, S, T], i32)
        lanes = sb("lanes", [P, S, GE], bf16)
        hot_t = sb("hot_t", [P, 2, GE], bf16)
        window = sb("window", [P, NT])
        window_i = sb("window_i", [P, NT], i32)
        in_window = sb("in_window", [P, 2, T])
        qk = sb("qk", [P, T, D])
        alpha = sb("alpha", [P, T, HEADS])
        msgs = sb("msgs", [P, 2, T, D])
        q_ps = st.enter_context(nc.psum_tensor("att_q_ps", [P, 3, T, D], f32))
        own_done = sem("att_own_done")
        staged = sem("att_staged")
        turn = sem("att_turn")
        msg_done = sem("att_msg_done")
        hot_t_done = sem("att_hot_t_done")
        q_done = sem("att_q_done")
        q_done_x = sem("att_q_done_x")
        q_taken_x = sem("att_q_taken_x")
        masked = sem("att_masked")
        gathered = [sem(f"att_gathered{s}") for s in range(S)]
        w_in = [sem(f"att_w_in{s}") for s in range(S)]
        lanes_in = [sem(f"att_lanes_in{s}") for s in range(S)]

        with nc.Block() as block:

            @block.vector
            def _(dve):
                own = shared.own
                own.do(nc.vector.tensor_copy(window_i[:], keys[:]))
                own.do(nc.vector.tensor_scalar(window_i[:], window_i[:], 7, None, ALU.logical_shift_right))
                nc.vector.tensor_copy(window[:], window_i[:])

        with nc.Block() as block:

            @block.sync
            def _(sp):
                def load_lanes(s, g):
                    sp.dma_start(lanes[:, s], lo_dram[1, bass.ds(g * GE, GE)].partition_broadcast(P)).then_inc(lanes_in[s], 16)

                def load_w(s, g):
                    sp.wait_ge(msg_done, g + 1)
                    sp.dma_start(w_rows[:, s].rearrange("p t f -> p (t f)"),
                                 w_dram[:, bass.ds(g * T * D, T * D)]).then_inc(w_in[s], 16)

                for s in range(S):
                    load_lanes(s, s)
                with sp.Fori(0, NI - 1) as i:
                    for s in range(S):
                        load_w(s, S * i + s)
                        sp.wait_ge(hot_t_done, S * i + s + 1)
                        load_lanes(s, S * (i + 1) + s)
                for s in range(S):
                    load_w(s, S * (NI - 1) + s)

            @block.scalar
            def _(act):
                def indices(s, g):
                    nc.scalar.copy(stage[:, s], src[:, bass.ds(g * T, T)]).then_inc(staged, 1)

                def body(i, last):
                    windows = Body(act, spans, i)
                    for s in range(S):
                        scalar_hot(nc, act, c, windows, s, S * i + s)
                        if not last:
                            act.wait_ge(gathered[s], 16 * T * (i + 1))
                            indices(s, S * (i + 1) + s)

                for s in range(S):
                    indices(s, s)
                with act.Fori(0, NI - 1) as i:
                    body(i, False)
                body(NI - 1, True)

            @block.gpsimd
            def _(pool):
                with pool.Fori(0, NI) as i:
                    for s in range(S):
                        pool.wait_ge(staged, S * i + s + 1)
                        pool.wait_ge(msg_done, S * i + s + 1)
                        pool.sem_inc(turn, 1)
                        for t in range(T):
                            pool.indirect_dma_start(
                                kv_rows[:, s, t, :], None, kv_dram,
                                bass.IndirectOffsetOnAxis(ap=stage[:, s, t:t + 1], axis=0)).then_inc(gathered[s], 16)

            @block.tensor
            def _(pe):
                def pick_q(s, slot, w):
                    for t in range(T):
                        for n in range(3):
                            ins = nc.tensor.matmul(q_ps[:, slot, t, :], hot_t[:, s % 2, t * P:(t + 1) * P],
                                                   q_parts[:, bass.ds(w, 1), n, :].rearrange("p a f -> p (a f)"),
                                                   start=n == 0, stop=n == 2)
                    return ins

                def sums(body, s, g):
                    pe.wait_ge(msg_done, S + g + 1)
                    tensor_sums(nc, pe, c, body, s, g, msgs[:, s % 2])

                def one_body(i, first):
                    body = Body(pe, spans, i)
                    for s in range(S):
                        g = S * i + s
                        pe.wait_ge(hot_t_done, g + 1)
                        pe.wait_ge(msg_done, S - 2 + g + 1)
                        pick_q(s, s % 2, window_of(nc, body.first(s), 0)).then_inc(q_done, 1)
                        with pe.If(body.more(s) > 0):
                            more, before = load_more(pe, spans, g)
                            with pe.Fori(0, more) as j:
                                pe.wait_ge(q_taken_x, before + j + 1)
                                pick_q(s, 2, window_of(nc, body.first(s), 1 + j)).then_inc(q_done_x, 1)
                        if s > 0 or not first:
                            sums(body, s - 1, g - 1)

                pe.sem_inc(q_done, 1)
                tensor_sums_start(pe, c)
                one_body(0, True)
                with pe.Fori(1, NI) as i:
                    one_body(i, False)
                sums(Body(pe, spans, NI - 1), S - 1, NG - 1)

            @block.vector
            def _(dve):
                def columns(slot, s, count, g):
                    dve.wait_ge(lanes_in[slot], count)
                    dve.wait_ge(q_done, g)
                    nc.vector.tensor_scalar(hot_t[:, s], lanes[:, slot], own_lane[:], None, ALU.is_equal).then_inc(hot_t_done, 1)

                def q_of_window(s, g, w, k):
                    own = Steps(dve, masked, 5 * k)
                    q = q_ps[:, s % 2]
                    for n, test in enumerate((ALU.is_equal, ALU.not_equal)):
                        own.mark(nc.vector.tensor_scalar(in_window[:, n], window[:, bass.ds(g * T, T)], iota[:, bass.ds(w, 1)], None, test))
                    dve.wait_ge(q_done, 1 + g + 1)
                    dve.wait_ge(q_done_x, k + 1)
                    own.wait()
                    own.mark(nc.vector.tensor_tensor(q, q, over(in_window[:, 1], [P, T, D], 2), ALU.mult))
                    here = msgs[:, s % 2]
                    own.do(nc.vector.tensor_tensor(here, q_ps[:, 2], over(in_window[:, 0], [P, T, D], 2), ALU.mult))
                    dve.sem_inc(q_taken_x, 1)
                    own.do(nc.vector.tensor_tensor(q, q, here, ALU.add))

                def one_body(i, first, last):
                    own = Steps(dve, own_done, i * (3 * S))
                    for s in range(S):
                        g = S * i + s
                        if s < S - 1 or not last:
                            columns((s + 1) % S, (s + 1) % 2, 16 * (i + 1 + (s == S - 1)), g + 1)
                        dve.wait_ge(gathered[s], 16 * T * (i + 1))
                        dve.wait_ge(w_in[s], 16 * (i + 1))
                        own.mark(nc.vector.tensor_tensor(qk[:], w_rows[:, s], kv_rows[:, s, :, 0:D], ALU.mult))
                        if s == 0:
                            body = Body(dve, spans, i)
                        with dve.If(body.more(s) > 0):
                            more, before = load_more(dve, spans, g)
                            with dve.Fori(0, more) as j:
                                q_of_window(s, g, window_of(nc, body.first(s), 1 + j), dve.snap(before + j))
                        dve.wait_ge(q_done, 1 + g + 1)
                        own.wait()
                        own.do(nc.vector.tensor_tensor(qk[:], q_ps[:, s % 2], qk[:], ALU.mult))
                        own.do(nc.vector.tensor_reduce(alpha[:], qk[:].rearrange("p t (h d) -> p t h d", h=HEADS), AX.X, ALU.add))
                        v = kv_rows[:, s, :, D:].rearrange("p t (h d) -> p t h d", h=HEADS)
                        nc.vector.tensor_tensor(msgs[:, s % 2].rearrange("p t (h d) -> p t h d", h=HEADS), v,
                                                over(alpha[:], [P, T, HEADS, HD], 3), ALU.mult).then_inc(msg_done, 1)
                        if s > 0 or not first:
                            vector_add(nc, dve, c, body, s - 1, g - 1)

                dve.sem_inc(msg_done, S)
                dve.sem_inc(q_taken_x, 1)
                vector_sums_start(dve, c)
                dve.wait_ge(lanes_in[0], 16)
                nc.vector.tensor_scalar(hot_t[:, 0], lanes[:, 0], own_lane[:], None, ALU.is_equal).then_inc(hot_t_done, 1)
                one_body(0, True, False)
                with dve.Fori(1, NI - 1) as i:
                    one_body(i, False, False)
                one_body(NI - 1, False, True)
                vector_add(nc, dve, c, Body(dve, spans, NI - 1), S - 1, NG - 1)


def laid_out(inputs):
    z = {k: np.asarray(v) for k, v in inputs.items()}

    def edges(v):
        p = np.full((EP,), PAD, v.dtype)
        p[:E] = v
        return p

    def tiles(v):
        return np.ascontiguousarray(v.reshape(NT, P, -1).transpose(1, 0, 2))

    def zeros_after(v, n):
        p = np.zeros((n,) + v.shape[1:], v.dtype)
        p[:v.shape[0]] = v
        return p

    src, dst = edges(z["src"]), edges(z["dst"])
    x = zeros_after(z["x"], NP)
    o = {"x": x.reshape(NW, P, D).transpose(1, 0, 2), "xT": np.ascontiguousarray(x.T), "edges": np.stack([src, dst]),
         "src_tiles": tiles(src)[:, :, 0], "dst_tiles": tiles(dst)[:, :, 0]}
    o["L0_W"] = z["L0_gnn_W"]
    o["L0_WT"] = z["L0_gnn_W"].T
    o["L0_a"] = z["L0_gnn_a"].reshape(2, D).T
    o["L1_W"] = z["L1_gnn_W"]
    o["L1_aggWT"] = z["L1_gnn_agg_W"].T
    o["L1_agg_b"] = z["L1_gnn_agg_b"].reshape(D, 1)
    o["L1_b"] = z["L1_gnn_b"].reshape(1, D)
    o["L1_gamma"] = z["L1_gnn_gamma"]
    o["L1_beta"] = z["L1_gnn_beta"]
    o["node_vec"] = zeros_after(z["node_vec1"], NP).reshape(NW, P).T
    w_in = np.zeros((D, 2 * D), np.float32)
    w_in[:MUL, :MUL] = z["L2_gnn_W_l1_0"]
    w_in[:MUL, D:D + MUL] = z["L2_gnn_W_sc0"]
    w_out = np.zeros((2 * D, D + 1), np.float32)
    w_out[:2 * MUL, :MUL] = z["L2_gnn_W_l2_0"]
    w_out[:2 * MUL, D] = z["L2_gnn_W_alpha"][:, 0]
    for c in range(3):
        w_in[MUL + c:D:3, MUL + c * MUL:MUL + (c + 1) * MUL] = z["L2_gnn_W_l1_1"]
        w_in[MUL + c:D:3, D + MUL + c:2 * D:3] = z["L2_gnn_W_sc1"]
        at = 2 * MUL + c * MUL
        w_out[at:at + MUL, MUL + c:D:3] = z["L2_gnn_W_l2_1"][:MUL]
        w_out[at + 3 * MUL:at + 4 * MUL, MUL + c:D:3] = z["L2_gnn_W_l2_1"][MUL:]
    o["L2_in"], o["L2_out"] = w_in, w_out
    o["L2_fc1"], o["L2_fc2"] = z["L2_gnn_W_fc1"], z["L2_gnn_W_fc2"]
    o["harm"] = tiles(zeros_after(z["edge_attr_4"], EP))
    o["scalars"] = zeros_after(z["edge_attr_10"], EA).T
    o["L3_wqkv"] = np.concatenate([z["L3_gnn_wq"], z["L3_gnn_wk"], z["L3_gnn_wv"]], axis=1)
    o["rad"] = zeros_after(z["edge_attr_64"], EA).T
    o["sph"] = zeros_after(z["edge_attr_32"], EA).T
    o["cut"] = tiles(zeros_after(z["edge_weight"], EP))[:, :, 0]
    o["rad_w0"], o["sph_w0"] = z["L3_gnn_rad_w0"], z["L3_gnn_sph_w0"]
    o["rad_w1"], o["sph_w1"] = z["L3_gnn_rad_w1"], z["L3_gnn_sph_w1"]
    o["b0"] = np.concatenate([z["L3_gnn_rad_b0"].reshape(HID // P, P), z["L3_gnn_sph_b0"].reshape(HID // P, P)]).T
    o["rad_b1"], o["sph_b1"] = z["L3_gnn_rad_b1"], z["L3_gnn_sph_b1"]
    return {k: np.ascontiguousarray(v) for k, v in o.items()}


def kernel(**inputs):
    import concourse.bacc as bacc
    from concourse.bass_utils import run_bass_kernel_spmd

    nc = bacc.Bacc("TRN2", target_bir_lowering=False, num_devices=1)
    arrays = {f"in_{k}": v for k, v in laid_out(inputs).items()}
    aps = {k[3:]: nc.dram_tensor(k, v.shape, mybir.dt.from_np(v.dtype), kind="ExternalInput").ap() for k, v in arrays.items()}
    out = nc.dram_tensor("out_x", (N, D), f32, kind="ExternalOutput").ap()
    gnn_kernel(nc, aps, out)
    got = run_bass_kernel_spmd(nc, [arrays], core_ids=[0])
    return got.results[0]["out_x"]
```
